# Optimizing a Trainium2 kernel written in Bass

```python
import numpy as np
import jax
import jax.numpy as jnp

def _softmax(x, axis=-1):
    return jax.nn.softmax(x, axis=axis)

def _gelu(x):
    return jax.nn.gelu(x, approximate=True)

def _silu(x):
    return jax.nn.silu(x)

def _sigmoid(x):
    return jax.nn.sigmoid(x)

def _layernorm(x, axis=-1, eps=1e-05):
    m = jnp.mean(x, axis=axis, keepdims=True)
    v = jnp.var(x, axis=axis, keepdims=True)
    return (x - m) / jnp.sqrt(v + eps)

def _scatter_add(tgt, idx, src, axis=0):
    return tgt.at[idx].add(src)

def _segment_sum(src, seg, n):
    return jax.ops.segment_sum(src, seg, n)
kernel_name = 'mk_gnn_ffn_d4_gnn_r32_96481f'

def setup_inputs(seed: int=0):
    np.random.seed(seed)
    _w = jnp.asarray

    def _rec_inputs():
        import jax
        import jax.numpy as jnp
        _gk = jax.random.key(seed)
        x = -6.415e-05 + 1 * jax.random.normal(jax.random.fold_in(_gk, 1), (625, 512), jnp.float32)
        src = jax.random.randint(jax.random.fold_in(_gk, 2), (10000,), 0, 625, jnp.int32)
        dst = jax.random.randint(jax.random.fold_in(_gk, 3), (10000,), 0, 625, jnp.int32)
        _o = jnp.argsort(dst, stable=True)
        src = src[_o]
        dst = dst[_o]
        edge_attr_64 = 0.000268479 + 0.999861 * jax.random.normal(jax.random.fold_in(_gk, 11), (10000, 64), jnp.float32)
        edge_weight = -0.00121341 + 0.998923 * jax.random.normal(jax.random.fold_in(_gk, 14), (10000,), jnp.float32)
        node_vec1 = jax.random.uniform(jax.random.fold_in(_gk, 15), (625, 1), jnp.float32, 0.0, 0.999957)
        return (x, src, dst, edge_attr_64, edge_weight, node_vec1)
    x, src, dst, edge_attr_64, edge_weight, node_vec1 = _rec_inputs()

    def _L0_gnn_setup():
        import jax, jax.numpy as jnp
        import numpy as np
        N = 625
        E = 10000
        F_IN = 512
        HEADS = 8
        D = 64
        ALPHA = 0.2
        EPS = 1e-16

        def _gat_forward(x, edge_index, W_e, W_r, a):
            src = edge_index[0]
            dst = edge_index[1]
            h_e = jnp.einsum('nf,hfd->hnd', x, W_e)
            h_r = jnp.einsum('nf,hfd->hnd', x, W_r)
            a_src, a_dst, a_dif, a_abs, a_prd = jnp.split(a, 5, axis=1)
            s_src = jnp.einsum('hnd,hd->hn', h_e, a_src)[:, src]
            s_dst = jnp.einsum('hnd,hd->hn', h_e, a_dst)[:, dst]
            hr_src = h_r[:, src]
            hr_dst = h_r[:, dst]
            diff = hr_dst - hr_src
            score = s_src + s_dst + jnp.einsum('hed,hd->he', diff, a_dif) + jnp.einsum('hed,hd->he', jnp.abs(diff), a_abs) + jnp.einsum('hed,hd->he', hr_src * hr_dst, a_prd)
            alpha = jax.nn.leaky_relu(score, negative_slope=ALPHA)
            alpha_t = alpha.T
            m = jax.ops.segment_max(alpha_t, src, num_segments=N)
            ex = jnp.exp(alpha_t - m[src])
            denom = jax.ops.segment_sum(ex, src, num_segments=N)[src]
            att = ex / (denom + EPS)
            msg = att[:, :, None] * jnp.transpose(h_e[:, dst], (1, 0, 2))
            out = jax.ops.segment_sum(msg, src, num_segments=N)
            return out.reshape(N, HEADS * D)
        key = jax.random.key(seed)
        k1, k2, k3, k4, k5 = jax.random.split(key, 5)
        x = jax.random.normal(k1, (N, F_IN), dtype=jnp.float32)
        edge_index = jax.random.randint(k2, (2, E), 0, N, dtype=jnp.int64)
        s_w = np.sqrt(2.0 / (F_IN + D))
        W_e = jax.random.normal(k3, (HEADS, F_IN, D), dtype=jnp.float32) * s_w
        W_r = jax.random.normal(k4, (HEADS, F_IN, D), dtype=jnp.float32) * s_w
        s_a = np.sqrt(2.0 / (1 + 5 * D))
        a = jax.random.normal(k5, (HEADS, 5 * D), dtype=jnp.float32) * s_a
        return {'x': x, 'edge_index': edge_index, 'W_e': W_e, 'W_r': W_r, 'a': a}
    _L0_gnn_all = _L0_gnn_setup()
    _L0_gnn_in = {k: v for k, v in _L0_gnn_all.items() if k in ('W_e', 'W_r', 'a')}
    del _L0_gnn_all

    def _L0_ffn_setup():
        import jax, jax.numpy as jnp
        import numpy as np
        DIM = 512
        FFN_DIM = 1408
        GROUP = 128
        EPS = 1e-05

        def _quantize_weight(w, group_size):
            o, i = w.shape
            wg = w.reshape(o, i // group_size, group_size)
            scale = jnp.mean(jnp.abs(wg), axis=-1, keepdims=True) + EPS
            wq = jnp.clip(jnp.round(wg / scale), -1.0, 1.0) * scale
            return wq.reshape(o, i)

        def _bitlinear(x, w, group_size=GROUP):
            wq = w + jax.lax.stop_gradient(_quantize_weight(w, group_size) - w)
            return jnp.einsum('bsd,fd->bsf', x, wq)
        key = jax.random.key(seed)
        k_x, k_g, k_u, k_d = jax.random.split(key, 4)
        x = jax.random.normal(k_x, (8, 128, DIM), dtype=jnp.float32)
        sd_in = 1.0 / np.sqrt(DIM)
        sd_ffn = 1.0 / np.sqrt(FFN_DIM)
        w_gate = jax.random.normal(k_g, (FFN_DIM, DIM), dtype=jnp.float32) * sd_in
        w_up = jax.random.normal(k_u, (FFN_DIM, DIM), dtype=jnp.float32) * sd_in
        w_down = jax.random.normal(k_d, (DIM, FFN_DIM), dtype=jnp.float32) * sd_ffn
        return {'x': x, 'w_gate': w_gate, 'w_up': w_up, 'w_down': w_down}
    _L0_ffn_all = _L0_ffn_setup()
    _L0_ffn_in = {k: v for k, v in _L0_ffn_all.items() if k in ('w_gate', 'w_up', 'w_down')}
    del _L0_ffn_all

    def _L1_gnn_setup():
        import jax, jax.numpy as jnp
        import numpy as np
        N = 625
        E = 6250
        D = 512
        H = 512

        def _layernorm(x, gamma, beta, eps=1e-05):
            mu = jnp.mean(x, axis=-1, keepdims=True)
            var = jnp.mean((x - mu) ** 2, axis=-1, keepdims=True)
            return (x - mu) * jax.lax.rsqrt(var + eps) * gamma + beta
        key = jax.random.key(seed)
        ks = jax.random.split(key, 12)
        s = 0.02
        return {'source_features': jax.random.normal(ks[0], (N, D), jnp.float32), 'weighting_gate': jax.random.normal(ks[1], (E,), jnp.float32), 'rel_pair_idx': jax.random.randint(ks[2], (E, 2), 0, N, dtype=jnp.int32), 'Wm': jax.random.normal(ks[3], (D, D // 2), jnp.float32) * s, 'bm': jnp.zeros((D // 2,), jnp.float32), 'W1': jax.random.normal(ks[4], (D, D // 4), jnp.float32) * s, 'b1': jnp.zeros((D // 4,), jnp.float32), 'gamma': jnp.ones((D // 4,), jnp.float32), 'beta': jnp.zeros((D // 4,), jnp.float32), 'W2': jax.random.normal(ks[5], (D // 4, H), jnp.float32) * s, 'b2': jnp.zeros((H,), jnp.float32)}
    _L1_gnn_all = _L1_gnn_setup()
    _L1_gnn_in = {k: v for k, v in _L1_gnn_all.items() if k in ('Wm', 'bm', 'W1', 'b1', 'gamma', 'beta', 'W2', 'b2')}
    del _L1_gnn_all

    def _L1_ffn_setup():
        import jax, jax.numpy as jnp
        import numpy as np
        D = 512
        H = 64
        E = 8
        TOPK = 2
        key = jax.random.key(seed)
        ks = jax.random.split(key, 5)
        s = 0.02
        x = jax.random.normal(ks[0], (4, 256, D), dtype=jnp.float32)
        gate_w = jax.random.normal(ks[1], (D, E), dtype=jnp.float32) * s
        W1 = jax.random.normal(ks[2], (E, D, H), dtype=jnp.float32) * s
        W3 = jax.random.normal(ks[3], (E, D, H), dtype=jnp.float32) * s
        W2 = jax.random.normal(ks[4], (E, H, D), dtype=jnp.float32) * s
        return {'x': x, 'gate_w': gate_w, 'W1': W1, 'W2': W2, 'W3': W3}
    _L1_ffn_all = _L1_ffn_setup()
    _L1_ffn_in = {k: v for k, v in _L1_ffn_all.items() if k in ('gate_w', 'W1', 'W2', 'W3')}
    del _L1_ffn_all

    def _L2_gnn_setup():
        import jax, jax.numpy as jnp
        import numpy as np
        N_NODES = 50000
        N_EDGES = 5000
        NODE_DIM = 512
        EDGE_DIM = 64
        NUM_LAYERS = 3
        LN_EPS = 1e-05

        def _layer_norm(x, gamma, beta):
            mu = jnp.mean(x, axis=-1, keepdims=True)
            var = jnp.mean((x - mu) ** 2, axis=-1, keepdims=True)
            return (x - mu) * jax.lax.rsqrt(var + LN_EPS) * gamma + beta
        key = jax.random.key(seed)
        k1, k2, k3, k4 = jax.random.split(key, 4)
        node_features = jax.random.normal(k1, (N_NODES, NODE_DIM), dtype=jnp.float32)
        edge_index = jax.random.randint(k2, (2, N_EDGES), 0, N_NODES, dtype=jnp.int32)
        edge_features = jax.random.normal(k3, (N_EDGES, EDGE_DIM), dtype=jnp.float32)
        Ws = jax.random.normal(k4, (NUM_LAYERS, NODE_DIM + EDGE_DIM, NODE_DIM), dtype=jnp.float32) * (1.0 / np.sqrt(NODE_DIM + EDGE_DIM))
        bs = jnp.zeros((NUM_LAYERS, NODE_DIM), dtype=jnp.float32)
        gammas = jnp.ones((NUM_LAYERS, NODE_DIM), dtype=jnp.float32)
        betas = jnp.zeros((NUM_LAYERS, NODE_DIM), dtype=jnp.float32)
        return {'node_features': node_features, 'edge_index': edge_index, 'edge_features': edge_features, 'Ws': Ws, 'bs': bs, 'gammas': gammas, 'betas': betas}
    _L2_gnn_all = _L2_gnn_setup()
    _L2_gnn_in = {k: v for k, v in _L2_gnn_all.items() if k in ('Ws', 'bs', 'gammas', 'betas')}
    del _L2_gnn_all

    def _L2_ffn_setup():
        import jax, jax.numpy as jnp
        import numpy as np
        K = 2
        key = jax.random.key(seed)
        ks = jax.random.split(key, 6)
        B, T, d, E, dff = (2, 64, 512, 8, 64)
        x = jax.random.normal(ks[0], (B, T, d), dtype=jnp.float32)
        Wg = jax.random.normal(ks[1], (d, E), dtype=jnp.float32) * 0.02
        W1 = jax.random.normal(ks[2], (E, d, dff), dtype=jnp.float32) * 0.02
        b1 = jnp.zeros((E, dff), dtype=jnp.float32)
        W2 = jax.random.normal(ks[3], (E, dff, d), dtype=jnp.float32) * 0.02
        b2 = jnp.zeros((E, d), dtype=jnp.float32)
        return {'x': x, 'Wg': Wg, 'W1': W1, 'b1': b1, 'W2': W2, 'b2': b2}
    _L2_ffn_all = _L2_ffn_setup()
    _L2_ffn_in = {k: v for k, v in _L2_ffn_all.items() if k in ('Wg', 'W1', 'b1', 'W2', 'b2')}
    del _L2_ffn_all

    def _L3_gnn_setup():
        import jax, jax.numpy as jnp
        import numpy as np
        N_NODES = 40962
        LATENT_DIM = 512
        N_EDGES = 20481
        NUM_BLOCKS = 4
        NUM_HEADS = 4
        NUM_FREQ = 32
        BASE_PERIOD = 16
        NOISE_EMB_DIM = 16
        EPS = 1e-05

        def _cond_layer_norm(x, cond, sw, sb, bw, bb):
            mu = jnp.mean(x, axis=-1, keepdims=True)
            var = jnp.var(x, axis=-1, keepdims=True)
            xn = (x - mu) * jax.lax.rsqrt(var + EPS)
            scale = cond @ sw + sb
            bias = cond @ bw + bb
            return xn * (1.0 + scale) + bias

        def _sparse_attention(x, src, dst, wq, bq, wk, bk, wv, bv, wo, bo):
            N, D = x.shape
            H, Dh = (NUM_HEADS, D // NUM_HEADS)
            q = (x @ wq + bq).reshape(N, H, Dh) * Dh ** (-0.5)
            k = (x @ wk + bk).reshape(N, H, Dh)
            v = (x @ wv + bv).reshape(N, H, Dh)
            scores = jnp.einsum('ehd,ehd->eh', q[src], k[dst])
            smax = jax.ops.segment_max(scores, src, num_segments=N)
            ex = jnp.exp(scores - smax[src])
            denom = jax.ops.segment_sum(ex, src, num_segments=N)
            attn = ex / denom[src]
            out = jax.ops.segment_sum(attn[:, :, None] * v[dst], src, num_segments=N)
            return out.reshape(N, D) @ wo + bo

        def _forward(x, edge_index, noise_levels, f_w1, f_b1, f_w2, f_b2, s1_w, s1_b, b1_w, b1_b, wq, bq, wk, bk, wv, bv, wo, bo, s2_w, s2_b, b2_w, b2_b, m_w1, m_b1, m_w2, m_b2):
            src, dst = (edge_index[0], edge_index[1])
            freqs = jnp.arange(1, NUM_FREQ + 1, dtype=x.dtype) * (2.0 * np.pi / BASE_PERIOD)
            ph = noise_levels * freqs
            emb = jnp.concatenate([jnp.sin(ph), jnp.cos(ph)], axis=-1)
            cond = jax.nn.silu(emb @ f_w1 + f_b1) @ f_w2 + f_b2
            for i in range(NUM_BLOCKS):
                y = _cond_layer_norm(x, cond, s1_w[i], s1_b[i], b1_w[i], b1_b[i])
                y = _sparse_attention(y, src, dst, wq[i], bq[i], wk[i], bk[i], wv[i], bv[i], wo[i], bo[i])
                x = x + y
                y = _cond_layer_norm(x, cond, s2_w[i], s2_b[i], b2_w[i], b2_b[i])
                y = jax.nn.relu(y @ m_w1[i] + m_b1[i]) @ m_w2[i] + m_b2[i]
                x = x + y
            return x
        key = jax.random.key(seed)
        ks = jax.random.split(key, 20)

        def w(k, shape, s=0.02):
            return jax.random.normal(k, shape, dtype=jnp.float32) * s
        D, B, C = (LATENT_DIM, NUM_BLOCKS, NOISE_EMB_DIM)
        z = lambda *s: jnp.zeros(s, jnp.float32)
        return {'latent_mesh_nodes': jax.random.normal(ks[0], (N_NODES, D), dtype=jnp.float32), 'edge_index': jax.random.randint(ks[1], (2, N_EDGES), 0, N_NODES, dtype=jnp.int32), 'noise_levels': jax.random.uniform(ks[2], (N_NODES, 1), dtype=jnp.float32), 'f_w1': w(ks[3], (2 * NUM_FREQ, C)), 'f_b1': z(C), 'f_w2': w(ks[4], (C, C)), 'f_b2': z(C), 's1_w': w(ks[5], (B, C, D)), 's1_b': z(B, D), 'b1_w': w(ks[6], (B, C, D)), 'b1_b': z(B, D), 'wq': w(ks[7], (B, D, D)), 'bq': z(B, D), 'wk': w(ks[8], (B, D, D)), 'bk': z(B, D), 'wv': w(ks[9], (B, D, D)), 'bv': z(B, D), 'wo': w(ks[10], (B, D, D)), 'bo': z(B, D), 's2_w': w(ks[11], (B, C, D)), 's2_b': z(B, D), 'b2_w': w(ks[12], (B, C, D)), 'b2_b': z(B, D), 'm_w1': w(ks[13], (B, D, D)), 'm_b1': z(B, D), 'm_w2': w(ks[14], (B, D, D)), 'm_b2': z(B, D)}
    _L3_gnn_all = _L3_gnn_setup()
    _L3_gnn_in = {k: v for k, v in _L3_gnn_all.items() if k in ('f_w1', 'f_b1', 'f_w2', 'f_b2', 's1_w', 's1_b', 'b1_w', 'b1_b', 'wq', 'bq', 'wk', 'bk', 'wv', 'bv', 'wo', 'bo', 's2_w', 's2_b', 'b2_w', 'b2_b', 'm_w1', 'm_b1', 'm_w2', 'm_b2')}
    del _L3_gnn_all

    def _L3_ffn_setup():
        import jax, jax.numpy as jnp
        import numpy as np
        DIM = 512
        HID = 1024
        E = 8
        K = 2
        B, S = (4, 64)
        key = jax.random.key(seed)
        ks = jax.random.split(key, 10)
        sd = DIM ** (-0.5)
        sh = HID ** (-0.5)
        return {'x': jax.random.normal(ks[0], (B, S, DIM), dtype=jnp.float32), 'gate_w': jax.random.normal(ks[1], (E, DIM), dtype=jnp.float32) * sd, 'biases': jnp.zeros((E,), dtype=jnp.float32), 'w1': jax.random.normal(ks[2], (E, DIM, HID), dtype=jnp.float32) * sd, 'w3': jax.random.normal(ks[3], (E, DIM, HID), dtype=jnp.float32) * sd, 'w2': jax.random.normal(ks[4], (E, HID, DIM), dtype=jnp.float32) * sh, 'sw1': jax.random.normal(ks[5], (DIM, HID), dtype=jnp.float32) * sd, 'sw3': jax.random.normal(ks[6], (DIM, HID), dtype=jnp.float32) * sd, 'sw2': jax.random.normal(ks[7], (HID, DIM), dtype=jnp.float32) * sh}
    _L3_ffn_all = _L3_ffn_setup()
    _L3_ffn_in = {k: v for k, v in _L3_ffn_all.items() if k in ('gate_w', 'biases', 'w1', 'w3', 'w2', 'sw1', 'sw3', 'sw2')}
    del _L3_ffn_all
    return {'x': x, 'src': src, 'dst': dst, 'edge_attr_64': edge_attr_64, 'edge_weight': edge_weight, 'node_vec1': node_vec1, 'L0_gnn_W_e': _L0_gnn_in['W_e'], 'L0_gnn_W_r': _L0_gnn_in['W_r'], 'L0_gnn_a': _L0_gnn_in['a'], 'L0_ffn_w_gate': _L0_ffn_in['w_gate'], 'L0_ffn_w_up': _L0_ffn_in['w_up'], 'L0_ffn_w_down': _L0_ffn_in['w_down'], 'L1_gnn_Wm': _L1_gnn_in['Wm'], 'L1_gnn_bm': _L1_gnn_in['bm'], 'L1_gnn_W1': _L1_gnn_in['W1'], 'L1_gnn_b1': _L1_gnn_in['b1'], 'L1_gnn_gamma': _L1_gnn_in['gamma'], 'L1_gnn_beta': _L1_gnn_in['beta'], 'L1_gnn_W2': _L1_gnn_in['W2'], 'L1_gnn_b2': _L1_gnn_in['b2'], 'L1_ffn_gate_w': _L1_ffn_in['gate_w'], 'L1_ffn_W1': _L1_ffn_in['W1'], 'L1_ffn_W2': _L1_ffn_in['W2'], 'L1_ffn_W3': _L1_ffn_in['W3'], 'L2_gnn_Ws': _L2_gnn_in['Ws'], 'L2_gnn_bs': _L2_gnn_in['bs'], 'L2_gnn_gammas': _L2_gnn_in['gammas'], 'L2_gnn_betas': _L2_gnn_in['betas'], 'L2_ffn_Wg': _L2_ffn_in['Wg'], 'L2_ffn_W1': _L2_ffn_in['W1'], 'L2_ffn_b1': _L2_ffn_in['b1'], 'L2_ffn_W2': _L2_ffn_in['W2'], 'L2_ffn_b2': _L2_ffn_in['b2'], 'L3_gnn_f_w1': _L3_gnn_in['f_w1'], 'L3_gnn_f_b1': _L3_gnn_in['f_b1'], 'L3_gnn_f_w2': _L3_gnn_in['f_w2'], 'L3_gnn_f_b2': _L3_gnn_in['f_b2'], 'L3_gnn_s1_w': _L3_gnn_in['s1_w'], 'L3_gnn_s1_b': _L3_gnn_in['s1_b'], 'L3_gnn_b1_w': _L3_gnn_in['b1_w'], 'L3_gnn_b1_b': _L3_gnn_in['b1_b'], 'L3_gnn_wq': _L3_gnn_in['wq'], 'L3_gnn_bq': _L3_gnn_in['bq'], 'L3_gnn_wk': _L3_gnn_in['wk'], 'L3_gnn_bk': _L3_gnn_in['bk'], 'L3_gnn_wv': _L3_gnn_in['wv'], 'L3_gnn_bv': _L3_gnn_in['bv'], 'L3_gnn_wo': _L3_gnn_in['wo'], 'L3_gnn_bo': _L3_gnn_in['bo'], 'L3_gnn_s2_w': _L3_gnn_in['s2_w'], 'L3_gnn_s2_b': _L3_gnn_in['s2_b'], 'L3_gnn_b2_w': _L3_gnn_in['b2_w'], 'L3_gnn_b2_b': _L3_gnn_in['b2_b'], 'L3_gnn_m_w1': _L3_gnn_in['m_w1'], 'L3_gnn_m_b1': _L3_gnn_in['m_b1'], 'L3_gnn_m_w2': _L3_gnn_in['m_w2'], 'L3_gnn_m_b2': _L3_gnn_in['m_b2'], 'L3_ffn_gate_w': _L3_ffn_in['gate_w'], 'L3_ffn_biases': _L3_ffn_in['biases'], 'L3_ffn_w1': _L3_ffn_in['w1'], 'L3_ffn_w3': _L3_ffn_in['w3'], 'L3_ffn_w2': _L3_ffn_in['w2'], 'L3_ffn_sw1': _L3_ffn_in['sw1'], 'L3_ffn_sw3': _L3_ffn_in['sw3'], 'L3_ffn_sw2': _L3_ffn_in['sw2']}

def reference(x, src, dst, edge_attr_64, edge_weight, node_vec1, L0_gnn_W_e, L0_gnn_W_r, L0_gnn_a, L0_ffn_w_gate, L0_ffn_w_up, L0_ffn_w_down, L1_gnn_Wm, L1_gnn_bm, L1_gnn_W1, L1_gnn_b1, L1_gnn_gamma, L1_gnn_beta, L1_gnn_W2, L1_gnn_b2, L1_ffn_gate_w, L1_ffn_W1, L1_ffn_W2, L1_ffn_W3, L2_gnn_Ws, L2_gnn_bs, L2_gnn_gammas, L2_gnn_betas, L2_ffn_Wg, L2_ffn_W1, L2_ffn_b1, L2_ffn_W2, L2_ffn_b2, L3_gnn_f_w1, L3_gnn_f_b1, L3_gnn_f_w2, L3_gnn_f_b2, L3_gnn_s1_w, L3_gnn_s1_b, L3_gnn_b1_w, L3_gnn_b1_b, L3_gnn_wq, L3_gnn_bq, L3_gnn_wk, L3_gnn_bk, L3_gnn_wv, L3_gnn_bv, L3_gnn_wo, L3_gnn_bo, L3_gnn_s2_w, L3_gnn_s2_b, L3_gnn_b2_w, L3_gnn_b2_b, L3_gnn_m_w1, L3_gnn_m_b1, L3_gnn_m_w2, L3_gnn_m_b2, L3_ffn_gate_w, L3_ffn_biases, L3_ffn_w1, L3_ffn_w3, L3_ffn_w2, L3_ffn_sw1, L3_ffn_sw3, L3_ffn_sw2):
    import jax
    import jax.numpy as jnp

    def _L0_gnn_ref(x, edge_index, W_e, W_r, a):
        import jax, jax.numpy as jnp
        import numpy as np
        N = 625
        E = 10000
        F_IN = 512
        HEADS = 8
        D = 64
        ALPHA = 0.2
        EPS = 1e-16

        def _gat_forward(x, edge_index, W_e, W_r, a):
            src = edge_index[0]
            dst = edge_index[1]
            h_e = jnp.einsum('nf,hfd->hnd', x, W_e)
            h_r = jnp.einsum('nf,hfd->hnd', x, W_r)
            a_src, a_dst, a_dif, a_abs, a_prd = jnp.split(a, 5, axis=1)
            s_src = jnp.einsum('hnd,hd->hn', h_e, a_src)[:, src]
            s_dst = jnp.einsum('hnd,hd->hn', h_e, a_dst)[:, dst]
            hr_src = h_r[:, src]
            hr_dst = h_r[:, dst]
            diff = hr_dst - hr_src
            score = s_src + s_dst + jnp.einsum('hed,hd->he', diff, a_dif) + jnp.einsum('hed,hd->he', jnp.abs(diff), a_abs) + jnp.einsum('hed,hd->he', hr_src * hr_dst, a_prd)
            alpha = jax.nn.leaky_relu(score, negative_slope=ALPHA)
            alpha_t = alpha.T
            m = jax.ops.segment_max(alpha_t, src, num_segments=N)
            ex = jnp.exp(alpha_t - m[src])
            denom = jax.ops.segment_sum(ex, src, num_segments=N)[src]
            att = ex / (denom + EPS)
            msg = att[:, :, None] * jnp.transpose(h_e[:, dst], (1, 0, 2))
            out = jax.ops.segment_sum(msg, src, num_segments=N)
            return out.reshape(N, HEADS * D)
        return _gat_forward(x, edge_index, W_e, W_r, a)

    def _L0_ffn_ref(x, w_gate, w_up, w_down):
        import jax, jax.numpy as jnp
        import numpy as np
        DIM = 512
        FFN_DIM = 1408
        GROUP = 128
        EPS = 1e-05

        def _quantize_weight(w, group_size):
            o, i = w.shape
            wg = w.reshape(o, i // group_size, group_size)
            scale = jnp.mean(jnp.abs(wg), axis=-1, keepdims=True) + EPS
            wq = jnp.clip(jnp.round(wg / scale), -1.0, 1.0) * scale
            return wq.reshape(o, i)

        def _bitlinear(x, w, group_size=GROUP):
            wq = w + jax.lax.stop_gradient(_quantize_weight(w, group_size) - w)
            return jnp.einsum('bsd,fd->bsf', x, wq)
        gate = _bitlinear(x, w_gate)
        up = _bitlinear(x, w_up)
        h = jax.nn.silu(gate) * up
        return _bitlinear(h, w_down)

    def _L1_gnn_ref(source_features, weighting_gate, rel_pair_idx, Wm, bm, W1, b1, gamma, beta, W2, b2):
        import jax, jax.numpy as jnp
        import numpy as np
        N = 625
        E = 6250
        D = 512
        H = 512

        def _layernorm(x, gamma, beta, eps=1e-05):
            mu = jnp.mean(x, axis=-1, keepdims=True)
            var = jnp.mean((x - mu) ** 2, axis=-1, keepdims=True)
            return (x - mu) * jax.lax.rsqrt(var + eps) * gamma + beta
        src = rel_pair_idx[:, 0]
        dst = rel_pair_idx[:, 1]
        n_nodes = source_features.shape[0]
        m = jnp.maximum(jnp.max(weighting_gate), jnp.float32(0.0))
        exp_e = jnp.exp(weighting_gate - m)
        row_sum = jax.ops.segment_sum(exp_e, src, num_segments=n_nodes)
        atten_e = exp_e / (row_sum[src] + 1e-06)
        Mfeat = source_features @ Wm + bm
        out0 = jax.ops.segment_sum(atten_e[:, None] * Mfeat[dst], src, num_segments=n_nodes)
        out1 = jax.ops.segment_sum(atten_e[:, None] * Mfeat[src], dst, num_segments=n_nodes)
        message_feats = jnp.concatenate([out0, out1], axis=-1)
        h = message_feats @ W1 + b1
        h = jax.nn.relu(_layernorm(h, gamma, beta))
        h = jax.nn.relu(h @ W2 + b2)
        valid = (row_sum > 0)[:, None]
        return jnp.where(valid, h, jnp.float32(0.0))

    def _L1_ffn_ref(x, gate_w, W1, W2, W3):
        import jax, jax.numpy as jnp
        import numpy as np
        D = 512
        H = 64
        E = 8
        TOPK = 2
        B, S, _ = x.shape
        xt = x.reshape(-1, D)
        T = xt.shape[0]
        gate_logits = xt @ gate_w
        w, idx = jax.lax.top_k(gate_logits, TOPK)
        w = jax.nn.softmax(w, axis=1).astype(xt.dtype)
        comb = jnp.zeros((T, E), dtype=xt.dtype).at[jnp.arange(T)[:, None], idx].add(w)
        out = jnp.zeros_like(xt)
        for e in range(E):
            h = jax.nn.silu(xt @ W1[e]) * (xt @ W3[e])
            out = out + h @ W2[e] * comb[:, e:e + 1]
        return out.reshape(B, S, D)

    def _L2_gnn_ref(node_features, edge_index, edge_features, Ws, bs, gammas, betas):
        import jax, jax.numpy as jnp
        import numpy as np
        N_NODES = 50000
        N_EDGES = 5000
        NODE_DIM = 512
        EDGE_DIM = 64
        NUM_LAYERS = 3
        LN_EPS = 1e-05

        def _layer_norm(x, gamma, beta):
            mu = jnp.mean(x, axis=-1, keepdims=True)
            var = jnp.mean((x - mu) ** 2, axis=-1, keepdims=True)
            return (x - mu) * jax.lax.rsqrt(var + LN_EPS) * gamma + beta
        src, tgt = (edge_index[0], edge_index[1])
        x = node_features
        n = x.shape[0]
        for i in range(NUM_LAYERS):
            msg = jnp.concatenate([x[src], edge_features], axis=-1)
            msg = msg @ Ws[i] + bs[i]
            agg = jax.ops.segment_sum(msg, tgt, num_segments=n)
            x = x + agg
            x = _layer_norm(x, gammas[i], betas[i])
            x = jax.nn.relu(x)
        return x

    def _L2_ffn_ref(x, Wg, W1, b1, W2, b2):
        import jax, jax.numpy as jnp
        import numpy as np
        K = 2
        logits = jnp.einsum('btd,de->bte', x, Wg)
        probs = jax.nn.softmax(logits, axis=-1)
        top_p, _top_i = jax.lax.top_k(probs, K)
        top_p = top_p / jnp.sum(top_p, axis=-1, keepdims=True)
        b2_sum = jnp.sum(b2, axis=0)
        out = jnp.zeros_like(x)
        for i in range(K):
            w_in = x * top_p[..., i:i + 1]
            h = jax.nn.gelu(jnp.einsum('btd,edf->ebtf', w_in, W1) + b1[:, None, None, :], approximate=False)
            out = out + jnp.einsum('ebtf,efd->btd', h, W2) + b2_sum
        return out

    def _L3_gnn_ref(latent_mesh_nodes, edge_index, noise_levels, f_w1, f_b1, f_w2, f_b2, s1_w, s1_b, b1_w, b1_b, wq, bq, wk, bk, wv, bv, wo, bo, s2_w, s2_b, b2_w, b2_b, m_w1, m_b1, m_w2, m_b2):
        import jax, jax.numpy as jnp
        import numpy as np
        N_NODES = 40962
        LATENT_DIM = 512
        N_EDGES = 20481
        NUM_BLOCKS = 4
        NUM_HEADS = 4
        NUM_FREQ = 32
        BASE_PERIOD = 16
        NOISE_EMB_DIM = 16
        EPS = 1e-05

        def _cond_layer_norm(x, cond, sw, sb, bw, bb):
            mu = jnp.mean(x, axis=-1, keepdims=True)
            var = jnp.var(x, axis=-1, keepdims=True)
            xn = (x - mu) * jax.lax.rsqrt(var + EPS)
            scale = cond @ sw + sb
            bias = cond @ bw + bb
            return xn * (1.0 + scale) + bias

        def _sparse_attention(x, src, dst, wq, bq, wk, bk, wv, bv, wo, bo):
            N, D = x.shape
            H, Dh = (NUM_HEADS, D // NUM_HEADS)
            q = (x @ wq + bq).reshape(N, H, Dh) * Dh ** (-0.5)
            k = (x @ wk + bk).reshape(N, H, Dh)
            v = (x @ wv + bv).reshape(N, H, Dh)
            scores = jnp.einsum('ehd,ehd->eh', q[src], k[dst])
            smax = jax.ops.segment_max(scores, src, num_segments=N)
            ex = jnp.exp(scores - smax[src])
            denom = jax.ops.segment_sum(ex, src, num_segments=N)
            attn = ex / denom[src]
            out = jax.ops.segment_sum(attn[:, :, None] * v[dst], src, num_segments=N)
            return out.reshape(N, D) @ wo + bo

        def _forward(x, edge_index, noise_levels, f_w1, f_b1, f_w2, f_b2, s1_w, s1_b, b1_w, b1_b, wq, bq, wk, bk, wv, bv, wo, bo, s2_w, s2_b, b2_w, b2_b, m_w1, m_b1, m_w2, m_b2):
            src, dst = (edge_index[0], edge_index[1])
            freqs = jnp.arange(1, NUM_FREQ + 1, dtype=x.dtype) * (2.0 * np.pi / BASE_PERIOD)
            ph = noise_levels * freqs
            emb = jnp.concatenate([jnp.sin(ph), jnp.cos(ph)], axis=-1)
            cond = jax.nn.silu(emb @ f_w1 + f_b1) @ f_w2 + f_b2
            for i in range(NUM_BLOCKS):
                y = _cond_layer_norm(x, cond, s1_w[i], s1_b[i], b1_w[i], b1_b[i])
                y = _sparse_attention(y, src, dst, wq[i], bq[i], wk[i], bk[i], wv[i], bv[i], wo[i], bo[i])
                x = x + y
                y = _cond_layer_norm(x, cond, s2_w[i], s2_b[i], b2_w[i], b2_b[i])
                y = jax.nn.relu(y @ m_w1[i] + m_b1[i]) @ m_w2[i] + m_b2[i]
                x = x + y
            return x
        return _forward(latent_mesh_nodes, edge_index, noise_levels, f_w1, f_b1, f_w2, f_b2, s1_w, s1_b, b1_w, b1_b, wq, bq, wk, bk, wv, bv, wo, bo, s2_w, s2_b, b2_w, b2_b, m_w1, m_b1, m_w2, m_b2)

    def _L3_ffn_ref(x, gate_w, biases, w1, w3, w2, sw1, sw3, sw2):
        import jax, jax.numpy as jnp
        import numpy as np
        DIM = 512
        HID = 1024
        E = 8
        K = 2
        B, S = (4, 64)
        Bb, Ss, D = x.shape
        xt = x.reshape(Bb * Ss, D)
        shared = jax.nn.silu(xt @ sw1) * (xt @ sw3) @ sw2
        scores = xt @ gate_w.T
        _, idx = jax.lax.top_k(scores + biases, K)
        topv, _ = jax.lax.top_k(scores, K)
        p = jax.nn.sigmoid(topv)
        p = p / jnp.sum(p, axis=-1, keepdims=True)
        h = jax.nn.silu(jnp.einsum('td,edh->eth', xt, w1)) * jnp.einsum('td,edh->eth', xt, w3)
        y = jnp.einsum('eth,ehd->etd', h, w2)
        onehot = jax.nn.one_hot(idx, E, dtype=xt.dtype)
        comb = jnp.einsum('tk,tke->te', p, onehot)
        out = jnp.einsum('te,etd->td', comb, y) + shared
        return out.reshape(Bb, Ss, D)
    edge_index = jnp.stack([src, dst])
    edge_index_t = jnp.stack([src, dst], axis=1)
    x = x + _L0_gnn_ref(_layernorm(x, axis=-1), edge_index, L0_gnn_W_e, L0_gnn_W_r, L0_gnn_a)
    x = x + _L0_ffn_ref(_layernorm(x, axis=-1)[None], L0_ffn_w_gate, L0_ffn_w_up, L0_ffn_w_down)[0]
    x = x + _L1_gnn_ref(_layernorm(x, axis=-1), edge_weight, edge_index_t, L1_gnn_Wm, L1_gnn_bm, L1_gnn_W1, L1_gnn_b1, L1_gnn_gamma, L1_gnn_beta, L1_gnn_W2, L1_gnn_b2)
    x = x + _L1_ffn_ref(_layernorm(x, axis=-1)[None], L1_ffn_gate_w, L1_ffn_W1, L1_ffn_W2, L1_ffn_W3)[0]
    x = x + _L2_gnn_ref(_layernorm(x, axis=-1), edge_index, edge_attr_64, L2_gnn_Ws, L2_gnn_bs, L2_gnn_gammas, L2_gnn_betas)
    x = x + _L2_ffn_ref(_layernorm(x, axis=-1)[None], L2_ffn_Wg, L2_ffn_W1, L2_ffn_b1, L2_ffn_W2, L2_ffn_b2)[0]
    x = x + _L3_gnn_ref(_layernorm(x, axis=-1), edge_index, node_vec1, L3_gnn_f_w1, L3_gnn_f_b1, L3_gnn_f_w2, L3_gnn_f_b2, L3_gnn_s1_w, L3_gnn_s1_b, L3_gnn_b1_w, L3_gnn_b1_b, L3_gnn_wq, L3_gnn_bq, L3_gnn_wk, L3_gnn_bk, L3_gnn_wv, L3_gnn_bv, L3_gnn_wo, L3_gnn_bo, L3_gnn_s2_w, L3_gnn_s2_b, L3_gnn_b2_w, L3_gnn_b2_b, L3_gnn_m_w1, L3_gnn_m_b1, L3_gnn_m_w2, L3_gnn_m_b2)
    x = x + _L3_ffn_ref(_layernorm(x, axis=-1)[None], L3_ffn_gate_w, L3_ffn_biases, L3_ffn_w1, L3_ffn_w3, L3_ffn_w2, L3_ffn_sw1, L3_ffn_sw3, L3_ffn_sw2)[0]
    return x

_drawn_inputs = setup_inputs


def setup_inputs(seed=0):
    import zlib

    import numpy as np

    out = dict(_drawn_inputs(seed))
    spreads = {'L1_gnn_bm': (0.0, 0.1),
     'L1_gnn_b1': (0.0, 0.1),
     'L1_gnn_gamma': (1.0, 0.2),
     'L1_gnn_beta': (0.0, 0.34),
     'L1_gnn_b2': (0.0, 0.1),
     'L2_gnn_bs': (0.0, 0.1),
     'L2_gnn_gammas': (1.0, 0.2),
     'L2_gnn_betas': (0.0, 0.1),
     'L2_ffn_b1': (0.0, 0.1),
     'L2_ffn_b2': (0.0, 0.1),
     'L3_gnn_f_b1': (0.0, 0.8),
     'L3_gnn_f_b2': (0.0, 0.8),
     'L3_gnn_s1_b': (0.0, 0.403),
     'L3_gnn_b1_b': (0.0, 0.292),
     'L3_gnn_bq': (0.0, 0.8),
     'L3_gnn_bk': (0.0, 0.8),
     'L3_gnn_bv': (0.0, 0.1),
     'L3_gnn_bo': (0.0, 0.1),
     'L3_gnn_s2_b': (0.0, 0.561),
     'L3_gnn_b2_b': (0.0, 0.439),
     'L3_gnn_m_b1': (0.0, 0.1),
     'L3_gnn_m_b2': (0.0, 0.1),
     'L3_ffn_biases': (0.0, 0.1)}
    factors = {'node_vec1': 8.0,
     'L1_ffn_gate_w': 4.542,
     'L1_ffn_W1': 4.081,
     'L1_ffn_W2': 4.169,
     'L1_ffn_W3': 3.954,
     'L2_ffn_Wg': 8.0,
     'L3_gnn_f_w1': 8.0,
     'L3_gnn_f_w2': 8.0,
     'L3_gnn_s1_w': 8.0,
     'L3_gnn_b1_w': 8.0,
     'L3_gnn_wq': 6.995,
     'L3_gnn_wk': 5.8,
     'L3_gnn_s2_w': 8.0,
     'L3_gnn_b2_w': 8.0}
    for name, (base, spread) in spreads.items():
        noise = np.random.default_rng([zlib.crc32(name.encode()), seed]).standard_normal(out[name].shape)
        drawn = base * np.exp(spread * noise) if base else spread * noise
        out[name] = jnp.asarray(drawn.astype(out[name].dtype))
    for name, factor in factors.items():
        out[name] = (out[name] * factor).astype(out[name].dtype)
    return out
```

```python
from contextlib import ExitStack, contextmanager

import numpy as np
import concourse.bass as bass
from concourse import mybir

F32, BF16, I16, I32, U32 = (mybir.dt.float32, mybir.dt.bfloat16, mybir.dt.int16, mybir.dt.int32,
                            mybir.dt.uint32)
ALU, ACT, AX = mybir.AluOpType, mybir.ActivationFunctionType, mybir.AxisListType

N, E, D = 625, 10000, 512
P, NT = 125, 5
ET = E // P
K4 = D // 128
HEADS0, DH0 = 8, 64
HEADS3 = 4
BLOCKS = 4
FREQS = 32
NEG = -1.0e30
BANK = 512
MAIN, TAIL = BANK, N - BANK
MAGIC = 12582912.0
STEP = 8
TURNS = ET // STEP
GATHERS_A, GATHERS_B = 2, 6

C_ID, C_TRI, C_I8, C_FREQ, C_SHIFT, C_FRAC, C_DUMP, C_SEL = 0, 128, 253, 261, 262, 263, 264, 265
C_END = C_SEL + D
R_BM, R_B1, R_G1, R_BE1, R_B2, R_G2, R_BE2, R_FB1 = 0, 256, 384, 512, 640, 1152, 2688, 4224
R_END = 4736


class Tally:

    def __init__(self, engine):
        self.engine, self.count, self.turn, self.per, self.base = engine, {}, None, {}, {}

    def add(self, sem, n=1):
        self.count[sem.name] = self.count.get(sem.name, 0) + n
        return self.now(sem)

    def now(self, sem):
        c = self.count.get(sem.name, 0)
        if self.turn is None:
            return c
        return self.turn * self.per.get(sem.name, 0) + c

    @contextmanager
    def loop(self, turn, trips, loops, name):
        per = loops[name].get(self.engine, {})
        self.turn, self.per, before = turn, per, dict(self.count)
        yield
        grew = {k: c - before.get(k, 0) for k, c in self.count.items() if c != before.get(k, 0)}
        for k, c in grew.items():
            self.count[k] += (trips - 1) * c
        wrong = grew != {k: v for k, v in per.items() if v}
        self.turn, self.per = None, {}
        assert not wrong, (name, self.engine, grew)


LOOPS = {
    "count": {
        "pe": {"onehot_ready": 8},
        "dve": {"vector_step": 2, "onehot_used": 8, "gathered_0": 32, "gathered_1": 32, "abs_ready":
               2, "score_taken": 2},
    },
    "weight": {
        "pe": {"onehot_ready": 8},
        "dve": {"vector_step": 6, "onehot_used": 8, "gathered_0": 96, "gathered_1": 96, "abs_ready":
               6, "score_taken": 6},
    },
    "edge": {
        "pe": {"onehot_ready": 8},
        "dve": {"vector_step": 8, "onehot_used": 8, "edge_in_0": 16, "edge_read": 2, "edge_in_1": 16},
    },
    "gather": {
        "pool": {"pool_step": 4, "score_ready": 2, "scattered": 32, "score_taken": 2},
    },
    "block": {
        "pe": {"filled_T0": 5, "y_ready": 10, "filled_T1": 5, "weights_in_0": 48, "filled_N0": 18,
               "filled_N1": 17, "filled_W0": 28, "filled_W1": 28, "prob_ready": 20, "weights_in_1":
               48, "modw_in": 16, "mod2_in": 16},
        "act": {"filled_T0": 5, "filled_T1": 5, "filled_N0": 18, "filled_N1": 17, "filled_W0": 28,
               "filled_W1": 28, "negmax_ready": 20},
        "dve": {"vector_step": 66, "y_ready": 10, "rstd_ready": 10, "filled_T0": 5, "filled_T1": 5,
               "filled_N0": 18, "filled_N1": 17, "filled_W0": 28, "filled_W1": 28, "exp_ready": 20,
               "br_in": 16, "attn_rows_free": 1, "br2_in": 16, "mlp_rows_free": 1},
        "pool": {"var_ready": 10},
    },
    "expert": {
        "pe": {"weights_in_0": 48, "filled_N0": 5, "filled_N1": 5, "filled_W0": 8, "filled_W1": 8,
               "weights_in_1": 48},
        "act": {"filled_N0": 5, "filled_N1": 5, "filled_W0": 8, "filled_W1": 8},
        "dve": {"filled_N0": 5, "filled_N1": 5, "filled_W0": 8, "filled_W1": 8},
    },
    "abs": {
        "act": {"diff_ready": 2},
    },
}
TWO_PI = (6.28125, 2029.0 / 2 ** 20, 2.0 * np.pi - 6.28125 - 2029.0 / 2 ** 20)


WIDTHS = (D, D, 1408 - 2 * D)
SMALLS = 8


def groups_of(u):
    return ([(j, c, WIDTHS[u]) for j in range(2) for c in range(K4)]
            + [(2, c, D) for c in range(WIDTHS[u] // 128)])


def bcast(row, at, n, parts):
    return row[bass.ds(at, n)].partition_broadcast(parts)


class Slot:
    def __init__(self, ap, filled, taken):
        self.ap, self.filled, self.taken = ap, filled, taken


class Slots:

    def __init__(self, slots, tally):
        self.slots, self.tally, self.turn = slots, tally, {"T": 0, "W": 0, "N": 0}

    def next(self, kind):
        s = self.slots[kind][self.turn[kind] % 2]
        self.turn[kind] += 1
        first = self.tally.turn is None and self.tally.count.get(s.filled.name, 0) == 0
        before = None if first else self.tally.now(s.filled)
        return s, self.tally.add(s.filled), before

    def skip(self, **kinds):
        for kind, n in kinds.items():
            for _ in range(n):
                self.next(kind)

    def align(self):
        self.turn = {"T": 0, "W": 0, "N": 0}


def program(nc, a, out, loops):
    ctx = ExitStack()

    def sb(name, shape, dt=F32):
        return ctx.enter_context(nc.sbuf_tensor(name, shape, dt))

    def sem(name):
        return ctx.enter_context(nc.semaphore(name))

    hr_rows = nc.dram_tensor("hr_rows", [N, D], F32, kind="Internal").ap()
    pair_scores = nc.dram_tensor("pair_scores", [N * N + 128, HEADS0], F32, kind="Internal").ap()

    with ctx:

        X = sb("X", [128, NT, D])
        Y = sb("Y", [128, NT, D])
        XT = sb("XT", [128, K4, N])
        WR = sb("WR", [128, 2, 3, K4 * D])
        CNT = sb("CNT", [P, NT, N])
        MASK = sb("MASK", [P, NT, N], BF16)
        G = sb("G", [P, NT, N])
        EA1 = sb("EA1", [128, N])
        EA2 = sb("EA2", [128, N])
        MODW = sb("MODW", [128, 4, D])
        BR = sb("BR", [128, 3, D])
        CS = sb("CS", [128, C_END])
        PC = sb("PC", [128, 3 * K4 * BLOCKS])
        FW = sb("FW", [64, 34])
        APRD = sb("APRD", [128, 2 * K4])
        IOTA = sb("IOTA", [P, N], I16)
        ONES = sb("ONES", [128, 128])
        HALF = sb("HALF", [P, 1])
        ST = sb("ST", [P, NT, 6])
        MV = sb("MV", [P, NT, 2])
        VE = sb("VE", [P, NT])
        RSTD = sb("RSTD", [P, NT])
        SM = sb("SM", [P, 64])
        DEN = sb("DEN", [P, 2, 4, NT])
        DIAG = sb("DIAG", [P, 2, NT, P])
        LG = sb("LG", [P, NT, 8])
        M8 = sb("M8", [P, NT, 8])
        I8 = sb("I8", [P, NT, 8], U32)
        TW = sb("TW", [P, NT, 6])
        COMB = sb("COMB", [P, NT, 9])
        ISRC = sb("ISRC", [P, ET], U32)
        IDST = sb("IDST", [P, ET], U32)
        SIDX = sb("SIDX", [P, ET], U32)
        FS = sb("FS", [P, 9, ET])
        IDS = sb("IDS", [P, 6], U32)
        TS = sb("TS", [P, 2, HEADS0])
        UV = sb("UV", [128, K4, 16])
        UU = sb("UU", [P, NT, HEADS0])
        WG = sb("WG", [128, 3, K4, 8])
        BI = sb("BI", [P, 8])
        TWOS = sb("TWOS", [8, P])
        UVT = sb("UVT", [128, 3, 4 * HEADS0])
        EB = sb("EB", [P, ET], BF16)
        HT_, XL_, PT_, KT_, V_, PR_ = 0, 2500, 5060, 8185, 10745, 13305
        AR = sb("AR", [128, PR_ + R_END])

        def view(at, parts, *shape, dt=F32):
            n = 1
            for s in shape:
                n *= s
            words = n if dt in (F32, I32, U32) else (n + 1) // 2
            v = AR[0:parts, at:at + words]
            if dt != F32:
                v = v.bitcast(dt)[:, 0:n]
            if len(shape) == 1:
                return v
            names = "abc"[:len(shape)]
            return v.rearrange(f"p ({' '.join(names)}) -> p {' '.join(names)}",
                               **{k: s for k, s in zip(names[1:], shape[1:])})

        HT = view(HT_, 128, K4, N)
        HRT = HT
        HRA = Y[:, :, :].rearrange("p a b -> p (a b)")[:, 0:K4 * N].rearrange(
            "p (a b) -> p a b", a=K4)
        XL = view(XL_, P, NT, D)
        HE = XL
        PT = view(PT_, P, NT, N)
        KT = view(KT_, 128, HEADS3, N)
        V = view(V_, P, NT, D)
        PRB = view(PR_, P, NT, N)
        ROWS = view(PR_, P, R_END)
        HRN = view(KT_, P, NT, D)
        HS = [view(PT_ + 1024 * b, P, D) for b in range(2)]
        HD = [view(PT_ + 1024 * b + 512, P, D) for b in range(2)]
        PRD = [view(PT_ + 2048 + 512 * b, P, D) for b in range(2)]
        OS = [view(V_ + 313 * b, P, N, dt=BF16) for b in range(2)]
        OD = [[view(V_ + 313 * (2 + 3 * b + r), P, N, dt=BF16) for r in range(3)] for b in range(2)]
        ZROW = view(PR_, P, 2500)
        ZB = view(PR_ + 2500, P, BANK, dt=BF16)
        ER = [view(PR_ + 2500 + 256 + 256 * b, P, 4, 64) for b in range(2)]
        ERR = view(PR_ + 3268, P, 4, 64)
        S1 = [view(PR_ + 3524 + 256 * b, P, 4, 128, dt=BF16) for b in range(2)]
        S2 = [view(PR_ + 4036 + 132 * b, P, 4, 66, dt=BF16) for b in range(2)]
        SROW = view(V_, P, 2500, dt=I32)
        GF = G[:, :, :].rearrange("p a b -> p (a b)")
        CF = CNT[:, :, :].rearrange("p a b -> p (a b)")
        DROW = GF[:, 0:2500].bitcast(I32)
        KROW = CF[:, 0:2500]
        TSC = [view(PT_ + 5000 * b, P, N * HEADS0) for b in range(2)]
        SP0 = [view(PT_ + 10000 + 625 * b, P, N) for b in range(2)]
        PTS = [view(PT_ + 11250 + 625 * b, P, NT, P) for b in range(2)]
        SG = [view(PT_ + 625 * b, 128, N) for b in range(2)]
        ROW = [view(PT_ + 1250 + 512 * b, P, D) for b in range(2)]
        MF = view(KT_, P, NT, 256)
        HB = view(V_, P, NT, 128)
        HBT = view(V_ + 640, 128, N)
        GE = [[view(PT_ + 1250 + 512 * (2 * b + i), P, D) for i in range(2)] for b in range(2)]
        EMB = view(PT_, 64, N)
        EMN = view(PT_ + 625, 64, N)
        EMR = view(PT_ + 1250, 64, N)
        ZC = view(PT_ + 1875, 16, N)
        CONDT = EA1[0:17, :]
        CT8 = view(V_, 8, N)
        VT = XT[0:8, 0, :]
        WTMP = view(HT_, 128, K4, D)
        AW = [view(XL_ + 512 * b, 128, D) for b in range(2)]
        SGN = [view(XL_ + 1024 + 512 * b, 128, D) for b in range(2)]
        SCL = [view(KT_ + 512 * b, 128, D) for b in range(2)]

        ID = CS[:, C_ID:C_ID + 128]
        SEL = CS[0:8, C_SEL:C_SEL + D]

        def wm(s, j, n=D):
            return WR[:, s, j, :].rearrange("p (c n) -> p c n", c=K4)[:, :, 0:n]


        PS = ctx.enter_context(nc.psum_tensor("PS", [128, 8 * BANK], F32))
        slots = {}
        for kind, at, size in (("T", 0, BANK), ("W", 2 * BANK, 2 * BANK), ("N", 6 * BANK, BANK)):
            slots[kind] = [Slot(PS[:, at + k * size:at + (k + 1) * size], sem(f"filled_{kind}{k}"),
                                sem(f"taken_{kind}{k}")) for k in range(2)]

        def main_of(c):
            return PS[0:P, BANK * c:BANK * c + MAIN]

        def tail_of(c):
            at = 5 * BANK + TAIL * c if c < 4 else 6 * BANK
            return PS[0:P, at:at + TAIL]


        x_in, consts_in, index_in, arow_in, small_in = map(sem, (
            "x_in", "consts_in", "index_in", "arow_in", "small_in"))
        loaded = [sem("weights_in_0"), sem("weights_in_1")]
        rowpair_in, rows_in, edge_in = sem("rowpair_in"), sem("rows_in"), [sem("edge_in_0"), sem("edge_in_1")]
        modw_in, br_in, mod2_in, br2_in, noise_in = map(sem, ("modw_in", "br_in", "mod2_in", "br2_in", "noise_in"))
        weights_used = sem("weights_used")
        vector_step, pool_step, scalar_step = sem("vector_step"), sem("pool_step"), sem("scalar_step")
        start_done = sem("pool_constants")
        var_ready, rstd_ready = sem("var_ready"), sem("rstd_ready")
        y_ready = sem("y_ready")
        uv_ready, hra_ready = sem("uv_ready"), sem("hra_ready")
        hrn_ready, hr_stored = sem("hrn_ready"), sem("hr_stored")
        onehot_ready, onehot_used = sem("onehot_ready"), sem("onehot_used")
        gathered = [sem("gathered_0"), sem("gathered_1")]
        score_ready, scattered = sem("score_ready"), sem("scattered")
        zeroed, zrow_ready = sem("zeroed"), sem("zrow_ready")
        sidx_ready, rowpair_read = sem("sidx_ready"), sem("rowpair_read")
        graph_filled, graph_taken = sem("graph_filled"), sem("graph_taken")
        edge_read = sem("edge_read")
        pairs_in = [sem("pair_scores_in_0"), sem("pair_scores_in_1")]
        pairs_read = sem("pair_scores_read")
        negmax_ready, exp_ready, prob_ready = sem("negmax_ready"), sem("exp_ready"), sem("prob_ready")
        absw_ready, kept_ready, quant_ready = sem("absw_ready"), sem("kept_ready"), sem("quant_ready")
        diff_ready, abs_ready = sem("diff_ready"), sem("abs_ready")
        score_taken = sem("score_taken")
        layer_ready = sem("layer_ready")
        attn_rows_free, mlp_rows_free = sem("attn_rows_free"), sem("mlp_rows_free")
        emb_ready, sin_ready = sem("emb_ready"), sem("sin_ready")
        out_ready, out_done = sem("out_ready"), sem("out_done")

        def store_x(eng):
            eng.drain().then_inc(out_ready, 1)

        block = ctx.enter_context(nc.Block())
        def loads(sp):
            n = Tally("sp")
            sp.dma_start(X[0:P, :, :], a["x"].rearrange("(t p) d -> p t d", p=P)).then_inc(x_in, 16)
            sp.dma_start(CS[:, :], a["consts"]).then_inc(consts_in, 16)
            batch = [0]

            def load(mats):
                k = batch[0]
                batch[0] += 1
                if k >= 2:
                    sp.wait_ge(weights_used, k - 1)
                for dst, src in mats:
                    sp.dma_start(dst, src).then_inc(loaded[k % 2], 16)

            def mat(s, j, name, at=None):
                src = a[name] if at is None else a[name][at]
                return WR[:, s, j, :], src

            load([mat(0, 0, "W_e"), mat(0, 1, "W_r")])
            for q in range(4):
                if q:
                    sp.wait_ge(rowpair_read, q)
                sp.dma_start(SROW, bcast(a["src_t"], 2500 * q, 2500, P)).then_inc(rowpair_in, 16)
                sp.dma_start(DROW, bcast(a["dst_t"], 2500 * q, 2500, P)).then_inc(rowpair_in, 16)
            load([mat(1, 0, "gate", 0), mat(1, 1, "up", 0), mat(1, 2, "down", 0)])
            sp.wait_ge(zrow_ready, 1)
            for t in range(NT):
                dst = pair_scores[N * P * t:N * P * (t + 1), :].rearrange("(p q) h -> p (q h)", p=P)
                for half in range(2):
                    sp.dma_start(dst[:, 2500 * half:2500 * (half + 1)], ZROW).then_inc(zeroed, 16)
            with sp.Fori(0, ET // 8) as i:
                for b in range(2):
                    sp.wait_ge(edge_read, i * 2 + b + 1)
                    sp.dma_start(ER[b].rearrange("p a b -> p (a b)"),
                                 a["edge_attr"][:, bass.ds(i * 512 + 256 * b, 256)]).then_inc(edge_in[b], 16)
            load([mat(0, 0, "gate", 1), mat(0, 1, "up", 1), mat(0, 2, "down", 1)])
            sp.wait_ge(scattered, 16 * ET)
            sp.wait_ge(graph_taken, 3)
            for t in range(NT):
                if t >= 2:
                    sp.wait_ge(pairs_read, HEADS0 * (t - 1))
                src = pair_scores[N * P * t:N * P * (t + 1), :].rearrange("(p q) h -> p (q h)", p=P)
                sp.dma_start(TSC[t % 2], src).then_inc(pairs_in[t % 2], 16)
            load([mat(1, 0, "gate", 2), mat(1, 1, "up", 2), mat(1, 2, "down", 2)])
            sp.dma_start(ROWS, bcast(a["rows"], 0, R_END, P)).then_inc(rows_in, 16)
            load([(WR[:, 0, 0, 0:K4 * 256], a["Wm"]), (WR[:, 0, 1, 0:K4 * 128], a["W1"]),
                  (WR[:, 0, 2, 0:D], a["W2"])])
            load([mat(1, j, x) for j, x in enumerate(("e_W1", "e_W3", "e_W2"))])
            load([mat(0, j, "Wtop", j) for j in range(3)])
            load([(WR[0:64, 1, 0, 0:3 * D], a["Wbot"]), (WR[64:128, 1, 0, 0:3 * D], a["Wbot"]),
                  (WR[0:65, 1, 1, 0:3 * D], a["Wlast"])])
            load([mat(0, 0, "f_W1"), mat(0, 1, "f_W2"), (WR[0:8, 0, 2, 0:D], a["f_b2"])])
            def attn_rows(i):
                sp.dma_start(MODW[0:17, 0:2, :], a["modw"][bass.ds(i, 1), :, 0:2, :].rearrange(
                    "a p b n -> (a p) b n")).then_inc(modw_in, 16)
                sp.dma_start(BR[0:P, 0:2, :], bcast(a["brow"], i * 3 * D, 2 * D, P).rearrange(
                    "p (a b) -> p a b", a=2)).then_inc(br_in, 16)

            def mlp_rows(i):
                sp.dma_start(MODW[0:17, 2:4, :], a["modw"][bass.ds(i, 1), :, 2:4, :].rearrange(
                    "a p b n -> (a p) b n")).then_inc(mod2_in, 16)
                sp.dma_start(BR[0:P, 2, :], bcast(a["brow"], i * 3 * D + 2 * D, D, P)).then_inc(br2_in, 16)

            sp.dma_start(EMN, bcast(a["noise"], 0, N, 64)).then_inc(noise_in, 16)
            k0 = batch[0]
            with sp.Fori(0, BLOCKS) as i:
                sp.wait_ge(attn_rows_free, i + 1)
                attn_rows(i)
                sp.wait_ge(weights_used, i * 2 + k0 - 1)
                for j in range(3):
                    sp.dma_start(WR[:, 1, j, :], a["qkv"][bass.ds(i * 3 + j, 1)].rearrange(
                        "a p n -> (a p) n")).then_inc(loaded[1], 16)
                sp.wait_ge(mlp_rows_free, i + 1)
                mlp_rows(i)
                sp.wait_ge(weights_used, i * 2 + k0)
                for j in range(3):
                    sp.dma_start(WR[:, 0, j, :], a["omm"][bass.ds(i * 3 + j, 1)].rearrange(
                        "a p n -> (a p) n")).then_inc(loaded[0], 16)
            k1 = k0 + 2 * BLOCKS
            with sp.Fori(0, 9) as i:
                for u in range(2):
                    sp.wait_ge(weights_used, i * 2 + k1 + u - 1)
                    for j, x in enumerate(("x_a", "x_b", "x_c")):
                        sp.dma_start(WR[:, 1 - u, j, :], a[x][bass.ds(i * 2 + u, 1)].rearrange(
                            "a p n -> (a p) n")).then_inc(loaded[1 - u], 16)

        @block.sync
        def _(sp):
            loads(sp)
            sp.wait_ge(out_ready, 1)
            sp.dma_start(out.rearrange("(t p) d -> p t d", p=P), X[0:P, :, :]).then_inc(out_done, 16)
            sp.wait_ge(out_done, 16)

        @block.tensor
        def _(pe):
            n = Tally("pe")
            psum = Slots(slots, n)
            mm = nc.tensor.matmul

            def fill(kind):
                s, _, before = psum.next(kind)
                if before is not None:
                    pe.wait_ge(s.taken, before)
                return s

            def weights(s, mats):
                pe.wait_ge(loaded[s], n.add(loaded[s], 16 * mats))

            def weights_done():
                pe.drain().then_inc(weights_used, 1)

            def wide(s, parts, terms, lhs, rhs):
                for c0, c1 in ((0, MAIN), (MAIN, N)):
                    for k in range(terms):
                        last = mm(s.ap[0:parts, c0:c1], lhs(k), rhs(k)[:, c0:c1],
                                  start=(k == 0), stop=(k == terms - 1))
                last.then_inc(s.filled, 1)

            def narrow(s, cols, pairs):
                for k, (lhs, rhs) in enumerate(pairs):
                    last = mm(s.ap[0:P, 0:cols], lhs, rhs, start=(k == 0), stop=(k == len(pairs) - 1))
                last.then_inc(s.filled, 1)

            def tile(t):
                return slice(P * t, P * (t + 1))

            def transpose_y():
                for t in range(NT):
                    s = fill("T")
                    pe.wait_ge(y_ready, n.add(y_ready))
                    for c in range(K4):
                        last = nc.tensor.transpose(s.ap[:, P * c:P * (c + 1)],
                                                   Y[0:P, t, 128 * c:128 * (c + 1)], ID[0:P, 0:P])
                    last.then_inc(s.filled, 1)
                all_taken("T")

            def all_taken(kinds):
                for kind in kinds:
                    for s in slots[kind]:
                        pe.wait_ge(s.taken, n.now(s.filled))

            def project_wide(w, m):
                s = fill("W")
                wide(s, 128, K4, lambda k: w[:, k, 128 * m:128 * (m + 1)], lambda k: XT[:, k, :])
                return s, n.now(s.filled)

            def project_narrow(w, t, cols=D, extra=()):
                s = fill("N")
                narrow(s, cols, list(extra) + [(XT[:, k, tile(t)], w[:, k, 0:cols]) for k in range(K4)])


            pe.wait_ge(consts_in, 16)
            pe.wait_ge(start_done, 6)
            transpose_y()
            weights(0, 2)
            we, wr = wm(0, 0), wm(0, 1)
            for t in range(NT):
                project_narrow(wr, t)
            for m in range(K4):
                project_wide(wr, m)
            for t in range(NT):
                project_narrow(we, t)
            pe.wait_ge(uv_ready, 1)
            s = fill("N")
            for t in range(NT):
                for k in range(K4):
                    last = mm(s.ap[0:P, 8 * t:8 * t + 8], XT[:, k, tile(t)], UV[:, k, 0:8],
                              start=(k == 0), stop=(k == K4 - 1))
            last.then_inc(s.filled, 1)
            s = fill("W")
            wide(s, 8, K4, lambda k: UV[:, k, 8:16], lambda k: XT[:, k, :])
            weights_done()
            s = fill("N")
            pe.wait_ge(layer_ready, n.add(layer_ready))
            nc.tensor.transpose(s.ap[0:1, 0:P], SM[:, 0:1], ID[0:P, 0:P]).then_inc(s.filled, 1)
            s = fill("N")
            pe.wait_ge(layer_ready, n.add(layer_ready))
            mm(s.ap[0:P, 0:1], ONES[0:1, 0:P], SM[0:1, 1:2], start=True, stop=True).then_inc(s.filled, 1)


            banks = [(BANK * c, MAIN) for c in range(5)] + [(5 * BANK, 4 * TAIL), (6 * BANK, TAIL)]

            def zero(banks, signal):
                for k, (at, size) in enumerate(banks):
                    last = mm(PS[0:128, at:at + size], ZB[:, 0:128], ZB[:, 0:size], start=True,
                              stop=False, skip_group_check=True)
                    if signal and k >= len(banks) - 2:
                        last.then_inc(onehot_used, 1)

            def close(banks):
                for at, size in banks:
                    last = mm(PS[0:128, at:at + size], ZB[:, 0:128], ZB[:, 0:size], start=False,
                              stop=True, skip_group_check=True)
                last.then_inc(graph_filled, 1)

            def pair_pass(name, parts):
                with pe.Fori(0, TURNS) as i, n.loop(i, TURNS, loops, name):
                    for k in range(STEP):
                        pe.wait_ge(onehot_ready, n.add(onehot_ready))
                        for c in range(NT):
                            for r in range(parts):
                                mm(main_of(c), OS[k % 2][:, tile(c)], OD[k % 2][r][:, 0:MAIN],
                                   start=False, stop=False, skip_group_check=True)
                                last = mm(tail_of(c), OS[k % 2][:, tile(c)], OD[k % 2][r][:, MAIN:N],
                                          start=False, stop=False, skip_group_check=True)
                        last.then_inc(onehot_used, 1)

            all_taken("TWN")
            pe.wait_ge(zrow_ready, 1)
            zero(banks, True)
            pair_pass("count", 1)
            close(banks)
            pe.wait_ge(graph_taken, 1)
            zero(banks, False)
            pair_pass("weight", 3)
            close(banks)
            pe.wait_ge(graph_taken, 2)
            ea = [(2 * BANK, MAIN), (3 * BANK, TAIL), (4 * BANK, MAIN), (5 * BANK, TAIL)]
            zero(ea, False)
            with pe.Fori(0, TURNS) as i, n.loop(i, TURNS, loops, "edge"):
                for k in range(STEP):
                    pe.wait_ge(onehot_ready, n.add(onehot_ready))
                    b = k // 4
                    for part, rows, at in ((S1[b][:, k % 4, :], 128, 2), (S2[b][:, k % 4, 0:65], 65, 4)):
                        mm(PS[0:rows, at * BANK:at * BANK + MAIN], part, OD[k % 2][0][:, 0:MAIN],
                           start=False, stop=False, skip_group_check=True)
                        last = mm(PS[0:rows, (at + 1) * BANK:(at + 1) * BANK + TAIL], part,
                                  OD[k % 2][0][:, MAIN:N], start=False, stop=False, skip_group_check=True)
                    last.then_inc(onehot_used, 1)
            close(ea)
            pe.wait_ge(graph_taken, 3)

            def pair_scores_of(t, h):
                s = fill("W")
                r = 64 * (h % 2)
                for c0, c1 in ((0, MAIN), (MAIN, N)):
                    mm(s.ap[0:P, c0:c1], HRA[r:r + 64, h // 2, tile(t)], HRT[r:r + 64, h // 2, c0:c1],
                       start=True, stop=False)
                    last = mm(s.ap[0:P, c0:c1], ID[0:8, h:h + 1].broadcast_to([8, P]),
                              VT[:, c0:c1], start=False, stop=True)
                last.then_inc(s.filled, 1)

            pe.wait_ge(hra_ready, K4)
            todo = [(t, h) for t in range(NT) for h in range(HEADS0)]
            pair_scores_of(*todo[0])
            for k, (t, h) in enumerate(todo):
                if k + 1 < len(todo):
                    pair_scores_of(*todo[k + 1])
                s = fill("W")
                pe.wait_ge(prob_ready, n.add(prob_ready))
                for c in range(NT):
                    last = mm(s.ap[0:P, 128 * c:128 * c + P], SP0[k % 2][:, tile(c)], DIAG[:, k % 2, 0, :],
                              start=True, stop=True)
                last.then_inc(s.filled, 1)
                if h == 0:
                    o = fill("N")
                pe.wait_ge(s.taken, n.now(s.filled))
                for c in range(NT):
                    last = mm(o.ap[0:P, DH0 * h:DH0 * (h + 1)], PTS[k % 2][:, c, :],
                              HE[:, c, DH0 * h:DH0 * (h + 1)], start=(c == 0), stop=(c == NT - 1))
                if h == HEADS0 - 1:
                    last.then_inc(o.filled, 1)
            psum.align()

            def ffn_unit(s, chunks=K4, scaled=False, between=lambda: None):
                wa, wb, wc = wm(s, 0), wm(s, 1), wm(s, 2)
                hidden = []
                for m in range(chunks):
                    project_wide(wa, m)
                    between()
                    if scaled:
                        b = fill("W")
                        wide(b, 128, 1, lambda k: SEL[:, 128 * m:128 * (m + 1)], lambda k: CT8)
                    hidden.append(project_wide(wb, m))
                    between()
                    between()
                for t in range(NT):
                    o = fill("N")
                    for m in range(chunks):
                        if t == 0:
                            pe.wait_ge(hidden[m][0].taken, hidden[m][1])
                        last = mm(o.ap[0:P, :], HT[:, m, tile(t)], wc[:, m, :],
                                  start=(m == 0), stop=(m == chunks - 1))
                    last.then_inc(o.filled, 1)

            def quantized(u):
                for k, (j, c, width) in enumerate(groups_of(u)):
                    g = fill("N")
                    pe.wait_ge(absw_ready, n.add(absw_ready))
                    mm(g.ap[:, 0:width], ONES[:, :], AW[k % 2][:, 0:width], start=True, stop=True)\
                        .then_inc(g.filled, 1)
                    yield

            for _ in quantized(0):
                pass
            transpose_y()
            for u in range(3):
                weights((u + 1) % 2, 3)
                pe.wait_ge(quant_ready, n.add(quant_ready, len(groups_of(u))))
                ahead = quantized(u + 1) if u < 2 else iter(())
                ffn_unit((u + 1) % 2, WIDTHS[u] // 128, between=lambda: next(ahead, None))
                weights_done()

            transpose_y()
            weights(0, 3)
            w_m = WR[:, 0, 0, 0:K4 * 256].rearrange("p (c n) -> p c n", c=K4)
            w_1 = WR[:, 0, 1, 0:K4 * 128].rearrange("p (c n) -> p c n", c=K4)
            w_2 = WR[:, 0, 2, 0:D]
            for t in range(NT):
                project_narrow(w_m, t, 256)
            pe.wait_ge(layer_ready, n.add(layer_ready))
            for c in range(NT):
                s = fill("W")
                for t in range(NT):
                    last = nc.tensor.transpose(s.ap[0:P, 128 * t:128 * t + P], G[:, t, tile(c)], ID[0:P, 0:P])
                last.then_inc(s.filled, 1)
            all_taken("WN")
            for f in range(4):
                s = fill("W")
                by = PT if f < 2 else G
                wide(s, 128, NT, lambda k: MF[:, k, 128 * (f % 2):128 * (f % 2 + 1)], lambda k: by[:, k, :])
            all_taken("W")
            for t in range(NT):
                s = fill("N")
                narrow(s, 128, [(HT[:, f, tile(t)], w_1[:, f, :]) for f in range(4)])
            for t in range(NT):
                s = fill("T")
                pe.wait_ge(layer_ready, n.add(layer_ready))
                nc.tensor.transpose(s.ap[:, 0:P], HB[:, t, :], ID[0:P, 0:P]).then_inc(s.filled, 1)
            all_taken("T")
            for t in range(NT):
                s = fill("N")
                narrow(s, D, [(HBT[:, tile(t)], w_2)])
            weights_done()

            transpose_y()
            pe.wait_ge(small_in, 16 * SMALLS)
            for t in range(NT):
                project_narrow(WG[:, 0], t, 8)
            for t in range(NT):
                s = fill("T")
                pe.wait_ge(layer_ready, n.add(layer_ready))
                nc.tensor.transpose(s.ap[0:8, 0:P], COMB[:, t, 0:8], ID[0:P, 0:P]).then_inc(s.filled, 1)
            all_taken("T")
            weights(1, 3)
            ffn_unit(1, scaled=True)
            weights_done()

            weights(0, 3)
            weights(1, 3)
            for l in range(3):
                pe.wait_ge(layer_ready, n.add(layer_ready))
                for f in range(K4):
                    s = fill("W")
                    wide(s, 128, NT, lambda k: XL[:, k, 128 * f:128 * (f + 1)], lambda k: CNT[:, k, :])
                all_taken("W")
                for t in range(NT):
                    s = fill("N")
                    narrow(s, D, [(EA1[:, tile(t)], WR[:, 1, 0, D * l:D * (l + 1)]),
                                  (EA2[0:65, tile(t)], WR[0:65, 1, 1, D * l:D * (l + 1)])]
                           + [(HT[:, f, tile(t)], wm(0, l)[:, f, :]) for f in range(K4)])
            weights_done()
            weights_done()

            transpose_y()
            for t in range(NT):
                project_narrow(WG[:, 1], t, 8)
            weights(0, 3)
            for t in range(NT):
                project_narrow(wm(0, 0), t)
            for t in range(NT):
                s = fill("T")
                pe.wait_ge(y_ready, n.add(y_ready))
                for c in range(K4):
                    last = nc.tensor.transpose(s.ap[:, P * c:P * (c + 1)],
                                               Y[0:P, t, 128 * c:128 * (c + 1)], ID[0:P, 0:P])
                last.then_inc(s.filled, 1)
            all_taken("T")
            for t in range(NT):
                s = fill("N")
                narrow(s, D, [(TWOS[:, :], WR[0:8, 0, 2, 0:D])]
                       + [(HT[:, k, tile(t)], wm(0, 1)[:, k, :]) for k in range(K4)])
            weights_done()

            s = fill("W")
            pe.wait_ge(sin_ready, 1)
            wide(s, 16, 1, lambda k: FW[0:64, 0:16], lambda k: EMR)
            pe.wait_ge(s.taken, n.now(s.filled))
            s = fill("W")
            wide(s, 16, 1, lambda k: FW[0:16, 16:32], lambda k: ZC)
            pe.wait_ge(s.taken, n.now(s.filled))
            psum.align()

            def modulation(j, rows_in_):
                pe.wait_ge(rows_in_, n.add(rows_in_, 16))
                for t in range(NT):
                    for q in range(2):
                        s = fill("N")
                        mm(s.ap[0:P, :], CONDT[:, tile(t)], MODW[0:17, j + q, :], start=True, stop=True)\
                            .then_inc(s.filled, 1)
                transpose_y()

            with pe.Fori(0, BLOCKS) as i, n.loop(i, BLOCKS, loops, "block"):
                modulation(0, modw_in)
                weights(1, 3)
                for h in range(HEADS3):
                    project_wide(wm(1, 0), h)
                    project_wide(wm(1, 1), h)
                for t in range(NT):
                    project_narrow(wm(1, 2), t)
                weights_done()
                all_taken("WN")

                def scores(h, ts):
                    for t in ts:
                        s = fill("W")
                        wide(s, P, 1, lambda k: HT[:, h, tile(t)], lambda k: KT[:, h, :])

                scores(0, range(NT))
                for h in range(HEADS3):
                    probs = G if h % 2 == 0 else PRB
                    if h + 1 < HEADS3:
                        scores(h + 1, range(NT))
                    pe.wait_ge(prob_ready, n.add(prob_ready, NT))
                    for c in range(NT):
                        s = fill("W")
                        for t in range(NT):
                            last = mm(s.ap[0:P, 128 * t:128 * t + P], probs[:, t, tile(c)],
                                      DIAG[:, h % 2, t, :], start=True, stop=True)
                        last.then_inc(s.filled, 1)
                    all_taken("W")
                    s = fill("W")
                    wide(s, 128, NT, lambda k: V[:, k, 128 * h:128 * (h + 1)], lambda k: PT[:, k, :])
                all_taken("W")
                weights(0, 3)
                for t in range(NT):
                    project_narrow(wm(0, 0), t)
                modulation(2, mod2_in)
                for m in range(K4):
                    project_wide(wm(0, 1), m)
                all_taken("W")
                for t in range(NT):
                    s = fill("N")
                    narrow(s, D, [(HT[:, k, tile(t)], wm(0, 2)[:, k, :]) for k in range(K4)])
                weights_done()
                psum.align()

            transpose_y()
            for t in range(NT):
                project_narrow(WG[:, 2], t, 8)
            psum.align()
            with pe.Fori(0, 9) as i, n.loop(i, 9, loops, "expert"):
                for u in range(2):
                    weights(1 - u, 3)
                    ffn_unit(1 - u)
                    weights_done()

        @block.scalar
        def _(act):
            n = Tally("act")
            psum = Slots(slots, n)
            fn = nc.scalar.activation

            def take(kind):
                s, k, _ = psum.next(kind)
                act.wait_ge(s.filled, k)
                return s

            def tile(t):
                return slice(P * t, P * (t + 1))

            act.dma_start(ISRC[:, :], a["src_p"].bitcast(U32)).then_inc(index_in, 16)
            act.dma_start(IDST[:, :], a["dst_p"].bitcast(U32)).then_inc(index_in, 16)
            act.dma_start(FS[:, 7, :], a["edge_weight"]).then_inc(index_in, 16)
            act.dma_start(MODW[:, :, :], bcast(a["arow"], 0, 4 * D, 128).rearrange(
                "p (a b) -> p a b", a=4)).then_inc(arow_in, 16)
            act.dma_start(APRD[:, 0:K4], a["a_prd"]).then_inc(arow_in, 16)
            for j in range(3):
                act.dma_start(WG[:, j], a[f"gate_{j}"].rearrange("p (c n) -> p c n", c=K4))\
                   .then_inc(small_in, 16)
            act.dma_start(BI[:, :], bcast(a["biases"], 0, 8, P)).then_inc(small_in, 16)
            act.dma_start(PC[:, :], a["columns"]).then_inc(small_in, 16)
            act.dma_start(FW[:, 0:16], a["f_w1"]).then_inc(small_in, 16)
            act.dma_start(FW[0:16, 16:32], a["f_w2"]).then_inc(small_in, 16)
            act.dma_start(FW[0:16, 32:34], a["f_cols"]).then_inc(small_in, 16)

            def transpose_y():
                for t in range(NT):
                    s = take("T")
                    fn(XT[:, :, tile(t)], s.ap[:, 0:4 * P].rearrange("p (c n) -> p c n", c=K4), ACT.Copy)\
                        .then_inc(s.taken, 1)


            transpose_y()
            for t in range(NT):
                s = take("N")
                fn(HRN[:, t, :], s.ap[0:P, :], ACT.Copy).then_inc(s.taken, 1)
                act.wait_ge(s.taken, n.now(s.filled))
                act.dma_start(hr_rows[tile(t), :], HRN[:, t, :]).then_inc(hr_stored, 16)
            psum.skip(W=K4)
            for t in range(NT):
                s = take("N")
                fn(HE[:, t, :], s.ap[0:P, :], ACT.Copy).then_inc(s.taken, 1)
            s = take("N")
            fn(UU[:, :, :], s.ap[0:P, 0:8 * NT].rearrange("p (t h) -> p t h", t=NT), ACT.Copy)\
                .then_inc(s.taken, 1)
            s = take("W")
            fn(VT, s.ap[0:8, 0:N], ACT.Copy).then_inc(s.taken, 1)
            psum.skip(N=1)
            s, k, _ = psum.next("N")
            act.wait_ge(s.taken, k)
            fn(FS[:, 8, :], FS[:, 7, :], ACT.Exp, bias=SM[:, 3:4]).then_inc(exp_ready, 1)
            n.add(exp_ready)


            for k, (dst, tiles) in enumerate(((CNT, GATHERS_A * TURNS), (G, GATHERS_B * TURNS))):
                with act.Fori(0, tiles // 2) as i, n.loop(i, tiles // 2, loops, "abs"):
                    for b in range(2):
                        act.wait_ge(diff_ready, n.add(diff_ready))
                        fn(PRD[b], PRD[b], ACT.Abs).then_inc(abs_ready, 1)
                act.wait_ge(graph_filled, k + 1)
                fn(dst[:, :, 0:MAIN], PS[0:P, 0:5 * BANK].rearrange("p (c n) -> p c n", c=NT), ACT.Copy)
                fn(dst[:, 0:4, MAIN:N], PS[0:P, 5 * BANK:5 * BANK + 4 * TAIL].rearrange(
                    "p (c n) -> p c n", c=4), ACT.Copy)
                fn(dst[:, 4, MAIN:N], tail_of(4), ACT.Copy).then_inc(graph_taken, 1)
            act.wait_ge(graph_filled, 3)
            fn(EA1[:, :], PS[:, 2 * BANK:2 * BANK + N], ACT.Copy)
            fn(EA2[0:65, :], PS[0:65, 4 * BANK:4 * BANK + N], ACT.Copy).then_inc(graph_taken, 1)

            def exp_scores(k):
                act.wait_ge(negmax_ready, n.add(negmax_ready))
                fn(SP0[k % 2], SP0[k % 2], ACT.Exp, bias=DEN[:, k % 2, 1, 0:1]).then_inc(exp_ready, 1)

            exp_scores(0)
            psum.skip(W=1)
            for k in range(NT * HEADS0):
                if k + 1 < NT * HEADS0:
                    exp_scores(k + 1)
                    psum.skip(W=1)
                s = take("W")
                fn(PTS[k % 2], s.ap[0:P, 0:640].rearrange("p (c n) -> p c n", c=NT)[:, :, 0:P], ACT.Copy)\
                    .then_inc(s.taken, 1)
            psum.skip(N=NT)
            for s in slots["N"]:
                act.wait_ge(s.filled, n.now(s.filled))
            psum.align()

            def ffn_unit(chunks=K4, scaled=False, between=lambda: None):
                for m in range(chunks):
                    s = take("W")
                    fn(SG[m % 2], s.ap[:, 0:N], ACT.Silu).then_inc(s.taken, 1)
                    between()
                    psum.skip(W=2 if scaled else 1)
                    between()
                    between()
                psum.skip(N=NT)

            done = [0]

            def quantized(u):
                def magnitudes(k):
                    j, c, width = groups[k]
                    if done[0] + k >= 2:
                        act.wait_ge(quant_ready, done[0] + k - 1)
                    w = wm((u + 1) % 2, j)[:, c, 0:width]
                    fn(AW[k % 2][:, 0:width], w, ACT.Abs).then_inc(absw_ready, 1)
                    fn(SGN[k % 2][:, 0:width], w, ACT.Sign).then_inc(scalar_step, 1)

                groups = groups_of(u)
                act.wait_ge(loaded[(u + 1) % 2], n.now(loaded[(u + 1) % 2]) + 48)
                magnitudes(0)
                for k, (j, c, width) in enumerate(groups):
                    if k + 1 < len(groups):
                        magnitudes(k + 1)
                    s = take("N")
                    fn(SCL[k % 2][:, 0:width], s.ap[:, 0:width], ACT.Copy, bias=1e-5, scale=1.0 / 128)\
                        .then_inc(s.taken, 1)
                    if k == len(groups) - 1:
                        done[0] += len(groups)
                    yield

            n.add(loaded[0], 32)
            for _ in quantized(0):
                pass
            transpose_y()
            for u in range(3):
                n.add(loaded[(u + 1) % 2], 48)
                ahead = quantized(u + 1) if u < 2 else iter(())
                ffn_unit(WIDTHS[u] // 128, between=lambda: next(ahead, None))

            transpose_y()
            psum.skip(N=NT)
            for c in range(NT):
                s = take("W")
                fn(PT[:, c, :].rearrange("p (c n) -> p c n", c=NT),
                   s.ap[0:P, 0:640].rearrange("p (c n) -> p c n", c=NT)[:, :, 0:P], ACT.Copy)\
                    .then_inc(s.taken, 1)
            for f in range(4):
                s = take("W")
                fn(HT[:, f, :], s.ap[:, 0:N], ACT.Copy).then_inc(s.taken, 1)
            psum.skip(N=NT)
            for t in range(NT):
                s = take("T")
                fn(HBT[:, tile(t)], s.ap[:, 0:P], ACT.Copy).then_inc(s.taken, 1)
            psum.skip(N=NT)

            def router_exp(cols, scale=1.0):
                act.wait_ge(negmax_ready, n.add(negmax_ready))
                fn(cols, cols, ACT.Exp, scale=scale).then_inc(exp_ready, 1)

            transpose_y()
            psum.skip(N=NT)
            router_exp(TW[:, :, 0])
            for t in range(NT):
                s = take("T")
                fn(CT8[:, tile(t)], s.ap[0:8, 0:P], ACT.Copy).then_inc(s.taken, 1)
            ffn_unit(scaled=True)

            for l in range(3):
                for f in range(K4):
                    s = take("W")
                    fn(HT[:, f, :], s.ap[:, 0:N], ACT.Copy).then_inc(s.taken, 1)
                psum.skip(N=NT)

            transpose_y()
            psum.skip(N=NT)
            router_exp(TW[:, :, 0])
            for t in range(NT):
                s, k, _ = psum.next("N")
                for i in range(2):
                    if i == 0:
                        act.wait_ge(negmax_ready, n.add(negmax_ready))
                    else:
                        act.wait_ge(s.taken, k)
                    fn(GE[t % 2][i], GE[t % 2][i], ACT.Gelu).then_inc(exp_ready, 1)
            for t in range(NT):
                s = take("T")
                fn(HT[:, :, tile(t)], s.ap[:, 0:4 * P].rearrange("p (c n) -> p c n", c=K4), ACT.Copy)\
                    .then_inc(s.taken, 1)
            psum.skip(N=NT)

            act.wait_ge(emb_ready, 1)
            fn(EMR, EMR, ACT.Sin).then_inc(sin_ready, 1)
            s = take("W")
            act.wait_ge(small_in, 16 * SMALLS)
            fn(ZC, s.ap[0:16, 0:N], ACT.Silu, bias=FW[0:16, 32:33]).then_inc(s.taken, 1)
            s = take("W")
            act.wait_ge(emb_ready, 2)
            fn(CONDT[0:16, :], s.ap[0:16, 0:N], ACT.Identity, bias=FW[0:16, 33:34]).then_inc(s.taken, 1)
            psum.align()

            with act.Fori(0, BLOCKS) as i, n.loop(i, BLOCKS, loops, "block"):
                psum.skip(N=2 * NT)
                transpose_y()
                for h in range(HEADS3):
                    psum.skip(W=1)
                    s = take("W")
                    fn(KT[:, h, :], s.ap[:, 0:N], ACT.Identity,
                       bias=PC[:, bass.ds(i * 12 + 4 + h, 1)]).then_inc(s.taken, 1)
                psum.skip(N=NT)

                def exp_head(h):
                    probs = G if h % 2 == 0 else PRB
                    for t in range(NT):
                        psum.skip(W=1)
                        act.wait_ge(negmax_ready, n.add(negmax_ready))
                        fn(probs[:, t, :], probs[:, t, :], ACT.Exp, bias=DEN[:, h % 2, 1, t:t + 1])\
                            .then_inc(exp_ready, 1)

                exp_head(0)
                for h in range(HEADS3):
                    if h + 1 < HEADS3:
                        exp_head(h + 1)
                    for c in range(NT):
                        s = take("W")
                        fn(PT[:, c, :].rearrange("p (c n) -> p c n", c=NT),
                           s.ap[0:P, 0:640].rearrange("p (c n) -> p c n", c=NT)[:, :, 0:P], ACT.Copy)\
                            .then_inc(s.taken, 1)
                    s = take("W")
                    fn(XT[:, h, :], s.ap[:, 0:N], ACT.Copy).then_inc(s.taken, 1)
                psum.skip(N=NT)
                psum.skip(N=2 * NT)
                transpose_y()
                for m in range(K4):
                    s = take("W")
                    fn(HT[:, m, :], s.ap[:, 0:N], ACT.Relu,
                       bias=PC[:, bass.ds(i * 12 + 8 + m, 1)]).then_inc(s.taken, 1)
                psum.skip(N=NT)
                psum.align()

            transpose_y()
            psum.skip(N=NT)
            router_exp(TW[:, :, 0:2], scale=-1.0)
            psum.align()
            with act.Fori(0, 9) as i, n.loop(i, 9, loops, "expert"):
                for u in range(2):
                    ffn_unit()

        @block.gpsimd
        def _(pool):
            n = Tally("pool")
            g = nc.gpsimd
            g.memset(ONES[:, :], 1.0).then_inc(start_done, 1)
            g.memset(TWOS[:, :], 2.0).then_inc(start_done, 1)
            g.memset(HALF[:, :], -0.5).then_inc(start_done, 1)
            g.memset(COMB[:, :, :], 1.0).then_inc(start_done, 1)
            g.memset(EA2[:, :], 0.0).then_inc(start_done, 1)
            g.iota(IOTA[:, :], pattern=[[1, N]], base=0, channel_multiplier=0).then_inc(start_done, 1)
            g.memset(ZB, 0.0).then_inc(pool_step, 1)
            g.memset(TS[:, :, :], 0.0).then_inc(score_taken, 1)
            n.add(score_taken)
            pool.wait_ge(pool_step, n.add(pool_step))
            g.memset(ZROW, 0.0).then_inc(zrow_ready, 1)

            def inverse_roots():
                for t in range(NT):
                    pool.wait_ge(var_ready, n.add(var_ready))
                    g.tensor_tensor(RSTD[:, t:t + 1], VE[:, t:t + 1], HALF[:, :], ALU.pow)\
                        .then_inc(rstd_ready, 1)

            inverse_roots()
            pool.wait_ge(index_in, 48)
            pool.wait_ge(hr_stored, 16 * NT)
            pool.wait_ge(uv_ready, 1)

            def gather(m, b):
                g.tensor_copy(IDS[:, 2 * b:2 * b + 1], ISRC[:, bass.ds(m, 1)]).then_inc(pool_step, 1)
                g.tensor_copy(IDS[:, 2 * b + 1:2 * b + 2], IDST[:, bass.ds(m, 1)]).then_inc(pool_step, 1)
                pool.wait_ge(pool_step, n.add(pool_step, 2))
                g.tensor_tensor(SM[0:1, 10:11], HALF[0:1, :], HALF[0:1, :], ALU.add)
                for k, dst in enumerate((HS[b], HD[b])):
                    g.indirect_dma_start(
                        out=dst, out_offset=None, in_=hr_rows,
                        in_offset=bass.IndirectOffsetOnAxis(ap=IDS[:, 2 * b + k:2 * b + k + 1], axis=0))\
                     .then_inc(gathered[b], 16)

            def scatter(m, b, first=False):
                pool.wait_ge(score_ready, n.add(score_ready))
                if not first:
                    pool.wait_ge(scattered, n.now(scattered))
                n.add(scattered, 16)
                g.tensor_copy(IDS[:, 4 + b:5 + b], SIDX[:, bass.ds(m, 1)]).then_inc(score_taken, 1)
                pool.wait_ge(score_taken, n.add(score_taken))
                g.tensor_tensor(SM[0:1, 10:11], HALF[0:1, :], HALF[0:1, :], ALU.add)
                g.indirect_dma_start(
                    out=pair_scores, out_offset=bass.IndirectOffsetOnAxis(ap=IDS[:, 4 + b:5 + b], axis=0),
                    in_=TS[:, b, :], in_offset=None).then_inc(scattered, 16)

            gather(0, 0)
            gather(1, 1)
            pool.wait_ge(zeroed, 16 * 2 * NT)
            pool.wait_ge(sidx_ready, 1)
            for m in range(2):
                scatter(m, m, first=(m == 0))
                gather(m + 2, m)
            with pool.Fori(1, ET // 2 - 1) as i, n.loop(i - 1, ET // 2 - 2, loops, "gather"):
                for b in range(2):
                    scatter(i * 2 + b, b)
                    gather(i * 2 + b + 2, b)
            scatter(ET - 2, 0)
            scatter(ET - 1, 1)
            inverse_roots()
            for u in range(3):
                for k, (j, c, width) in enumerate(groups_of(u)):
                    w = wm((u + 1) % 2, j)[:, c, 0:width]
                    pool.wait_ge(kept_ready, n.add(kept_ready))
                    g.tensor_tensor(w, SCL[k % 2][:, 0:width], SGN[k % 2][:, 0:width], ALU.mult)\
                     .then_inc(quant_ready, 1)
            inverse_roots()
            inverse_roots()
            inverse_roots()
            inverse_roots()
            for l in range(3):
                inverse_roots()
            inverse_roots()
            inverse_roots()
            inverse_roots()
            with pool.Fori(0, BLOCKS) as i, n.loop(i, BLOCKS, loops, "block"):
                inverse_roots()
                inverse_roots()
            inverse_roots()

        @block.vector
        def _(dve):
            n = Tally("dve")
            psum = Slots(slots, n)
            v = nc.vector

            def take(kind):
                s, k, _ = psum.next(kind)
                dve.wait_ge(s.filled, k)
                return s

            def step(ins):
                ins.then_inc(vector_step, 1)
                dve.wait_ge(vector_step, n.add(vector_step))

            def signal(ins, sem):
                ins.then_inc(sem, 1)
                dve.wait_ge(sem, n.add(sem))

            def carry():
                if n.turn is not None:
                    v.tensor_copy(SM[0:1, 5:6], ONES[0:1, 0:1])

            def tile(t):
                return slice(P * t, P * (t + 1))

            def stats(t, src):
                step(v.bn_stats(ST[:, t, :], src))
                carry()
                step(v.bn_aggr(MV[:, t, :], ST[:, t, :]))
                v.tensor_scalar(VE[:, t:t + 1], MV[:, t, 1:2], 1e-5, None, ALU.add).then_inc(var_ready, 1)

            def norm(t, dst, src):
                dve.wait_ge(rstd_ready, n.add(rstd_ready))
                return v.tensor_scalar(dst, src, MV[:, t, 0:1], RSTD[:, t:t + 1], ALU.subtract, ALU.mult)

            def norm_y(src=X):
                n.add(y_ready, NT)
                for t in range(NT):
                    norm(t, Y[0:P, t, :], src[0:P, t, :]).then_inc(y_ready, 1)

            def add_to_stream(t, s, scalar=None, dst=X):
                if scalar is None:
                    v.tensor_tensor(dst[0:P, t, :], s.ap[0:P, :], dst[0:P, t, :], ALU.add)\
                     .then_inc(s.taken, 1)
                else:
                    v.scalar_tensor_tensor(dst[0:P, t, :], s.ap[0:P, :], scalar, dst[0:P, t, :],
                                           ALU.mult, ALU.add).then_inc(s.taken, 1)
                dve.wait_ge(s.taken, n.now(s.filled))

            v.memset(S2[0][:, :, 64:65], 1.0)
            signal(v.memset(S2[1][:, :, 64:65], 1.0), edge_read)


            dve.wait_ge(x_in, 16)
            for t in range(NT):
                stats(t, X[0:P, t, :])
            norm_y()
            psum.skip(T=NT, N=NT)
            dve.wait_ge(arow_in, 32)
            dve.wait_ge(loaded[0], 32)
            for k, (w, r) in enumerate(((0, 0), (1, 2), (0, 1))):
                step(v.tensor_tensor(WTMP, wm(0, w), MODW[:, r, :].unsqueeze(1).broadcast_to([128, K4, D]),
                                     ALU.mult))
                step(v.tensor_reduce(UVT[:, k, :], WTMP.rearrange("p c (h d) -> p (c h) d", d=DH0),
                                     AX.X, ALU.add))
            part = [UVT[:, k, :].rearrange("p (c h) -> p c h", c=K4) for k in range(3)]
            step(v.tensor_tensor(UV[:, :, 0:8], part[0], part[1], ALU.subtract))
            v.tensor_tensor(UV[:, :, 8:16], part[2], part[1], ALU.add).then_inc(uv_ready, 1)
            dve.wait_ge(uv_ready, 1)
            for m in range(K4):
                s = take("W")
                v.tensor_copy(HRT[:, m, :], s.ap[:, 0:N]).then_inc(s.taken, 1)
                dve.wait_ge(s.taken, n.now(s.filled))
                v.tensor_scalar(HRA[:, m, :], HRT[:, m, :], APRD[:, m:m + 1], None, ALU.mult)\
                 .then_inc(hra_ready, 1)
            psum.skip(N=NT + 1, W=1)
            dve.wait_ge(index_in, 48)
            step(v.tensor_copy(FS[:, 0, :], ISRC[:, :]))
            step(v.tensor_copy(FS[:, 1, :], IDST[:, :]))
            step(v.scalar_tensor_tensor(FS[:, 2, :], FS[:, 0, :], float(N), FS[:, 1, :], ALU.mult, ALU.add))
            v.reduce_max(SM[:, 0:1], FS[:, 7, :], AX.X).then_inc(layer_ready, 1)
            s = take("N")
            v.reduce_max(SM[0:1, 2:3], s.ap[0:1, 0:P], AX.X).then_inc(s.taken, 1)
            dve.wait_ge(s.taken, n.now(s.filled))
            v.tensor_scalar(SM[0:1, 1:2], SM[0:1, 2:3], 0.0, None, ALU.max).then_inc(layer_ready, 1)
            s = take("N")
            v.tensor_scalar(SM[:, 3:4], s.ap[0:P, 0:1], -1.0, None, ALU.mult).then_inc(s.taken, 1)
            dve.wait_ge(exp_ready, n.add(exp_ready))
            for r in range(3):
                step(v.tensor_copy(EB[:, :], FS[:, 8, :]))
                step(v.tensor_copy(FS[:, 4 + r, :], EB[:, :]))
                if r < 2:
                    step(v.tensor_tensor(FS[:, 8, :], FS[:, 8, :], FS[:, 4 + r, :], ALU.subtract))

            dve.wait_ge(consts_in, 16)
            for q in range(4):
                dve.wait_ge(rowpair_in, 32 * (q + 1))
                step(v.scalar_tensor_tensor(KROW, SROW, float(N), DROW, ALU.mult, ALU.add))
                rows = KROW.rearrange("p (t k) -> p t k", k=P)
                keys = FS[:, 2, 20 * q:20 * (q + 1)].unsqueeze(2).broadcast_to([P, 20, P])
                step(v.tensor_tensor(rows, rows, keys, ALU.is_equal))
                step(v.tensor_tensor(rows, rows, CS[0:P, C_TRI:C_TRI + P].unsqueeze(1)
                                     .broadcast_to([P, 20, P]), ALU.mult))
                v.tensor_reduce(FS[:, 3, 20 * q:20 * (q + 1)], rows, AX.X, ALU.max)\
                 .then_inc(rowpair_read, 1)
            dve.wait_ge(rowpair_read, 4)
            step(v.tensor_scalar(FS[:, 8, :], FS[:, 2, :], -1.0, CS[0:P, C_DUMP:C_DUMP + 1],
                                 ALU.mult, ALU.add))
            step(v.tensor_tensor(FS[:, 8, :], FS[:, 8, :], FS[:, 3, :], ALU.mult))
            step(v.tensor_tensor(FS[:, 8, :], FS[:, 8, :], FS[:, 2, :], ALU.add))
            v.tensor_copy(SIDX[:, :], FS[:, 8, :]).then_inc(sidx_ready, 1)


            def onehot(dst, m, row, scale=None):
                if scale is None:
                    return v.tensor_scalar(dst, IOTA[:, :], FS[:, row, bass.ds(m, 1)], None, ALU.is_equal)
                return v.tensor_scalar(dst, IOTA[:, :], FS[:, row, bass.ds(m, 1)],
                                       FS[:, scale, bass.ds(m, 1)], ALU.is_equal, ALU.mult)

            def differences(b):
                dve.wait_ge(gathered[b], n.add(gathered[b], 32))
                v.tensor_tensor(PRD[b], HD[b], HS[b], ALU.subtract).then_inc(diff_ready, 1)

            def edge_scores(b):
                dve.wait_ge(abs_ready, n.add(abs_ready))
                step(v.tensor_tensor(PRD[b], PRD[b], MODW[0:P, 3, :], ALU.mult))
                dve.wait_ge(score_taken, n.add(score_taken))
                v.tensor_reduce(TS[:, b, :], PRD[b].rearrange("p (h d) -> p h d", d=DH0), AX.X, ALU.add)\
                 .then_inc(score_ready, 1)

            dve.wait_ge(start_done, 6)
            for name, parts, scores in (("count", 0, GATHERS_A), ("weight", 3, GATHERS_B)):
                with dve.Fori(0, TURNS) as i, n.loop(i, TURNS, loops, name):
                    done = 0
                    for k in range(STEP):
                        dve.wait_ge(onehot_used, n.add(onehot_used))
                        onehot(OS[k % 2], i * STEP + k, 0)
                        if parts:
                            for r in range(parts):
                                last = onehot(OD[k % 2][r], i * STEP + k, 1, 4 + r)
                        else:
                            last = onehot(OD[k % 2][0], i * STEP + k, 1)
                        last.then_inc(onehot_ready, 1)
                        while done * STEP < (k + 1) * scores and done < scores:
                            differences(done % 2)
                            if done:
                                edge_scores((done - 1) % 2)
                            done += 1
                    edge_scores((done - 1) % 2)
                if name == "count":
                    dve.wait_ge(graph_taken, 1)
                    step(v.tensor_scalar(MASK[:, :, :], CNT[:, :, :], 0.5, NEG, ALU.is_lt, ALU.mult))
            with dve.Fori(0, TURNS) as i, n.loop(i, TURNS, loops, "edge"):
                for b in range(2):
                    dve.wait_ge(edge_in[b], n.add(edge_in[b], 16))
                    dve.wait_ge(onehot_used, n.now(onehot_used))
                    step(v.tensor_copy(S1[b][:, :, 0:64], ER[b]))
                    signal(v.tensor_tensor(ERR, ER[b], S1[b][:, :, 0:64], ALU.subtract), edge_read)
                    step(v.tensor_copy(S1[b][:, :, 64:128], ERR))
                    step(v.tensor_tensor(ERR, ERR, S1[b][:, :, 64:128], ALU.subtract))
                    step(v.tensor_copy(S2[b][:, :, 0:64], ERR))
                    for k in range(4):
                        dve.wait_ge(onehot_used, n.add(onehot_used))
                        onehot(OD[k % 2][0], i * STEP + 4 * b + k, 1).then_inc(onehot_ready, 1)

            todo = [(t, h) for t in range(NT) for h in range(HEADS0)]

            def pair_maxima(k):
                t, h = todo[k]
                if h == 0:
                    dve.wait_ge(pairs_in[t % 2], 16 * (t // 2 + 1))
                s = take("W")
                z = SP0[k % 2]
                extra = TSC[t % 2].rearrange("p (d h) -> p d h", h=HEADS0)[:, :, h]
                v.scalar_tensor_tensor(z, s.ap[0:P, 0:N], UU[:, t, h:h + 1], extra, ALU.add, ALU.add)\
                 .then_inc(s.taken, 1)
                dve.wait_ge(s.taken, n.now(s.filled))
                v.scalar_tensor_tensor(z, z, 0.2, z, ALU.mult, ALU.max).then_inc(pairs_read, 1)
                dve.wait_ge(pairs_read, n.add(pairs_read))
                step(v.tensor_tensor_reduce(out=z, in0=z, in1=MASK[:, t, :], scale=1.0, scalar=-3.0e38,
                                            op0=ALU.add, op1=ALU.max, accum_out=DEN[:, k % 2, 0, 0:1]))
                v.tensor_scalar(DEN[:, k % 2, 1, 0:1], DEN[:, k % 2, 0, 0:1], -1.0, None, ALU.mult)\
                 .then_inc(negmax_ready, 1)

            pair_maxima(0)
            for k, (t, h) in enumerate(todo):
                if k + 1 < len(todo):
                    pair_maxima(k + 1)
                psum.skip(W=1)
                z = SP0[k % 2]
                dve.wait_ge(exp_ready, n.add(exp_ready))
                step(v.tensor_tensor_reduce(out=z, in0=z, in1=CNT[:, t, :], scale=1.0, scalar=0.0,
                                            op0=ALU.mult, op1=ALU.add, accum_out=DEN[:, k % 2, 2, 0:1]))
                step(v.tensor_scalar(DEN[:, k % 2, 3, 0:1], DEN[:, k % 2, 2, 0:1], 1e-16, None, ALU.add))
                step(v.reciprocal(DEN[:, k % 2, 3, 0:1], DEN[:, k % 2, 3, 0:1]))
                v.tensor_scalar(DIAG[:, k % 2, 0, :], ID[0:P, 0:P], DEN[:, k % 2, 3, 0:1], None, ALU.mult)\
                 .then_inc(prob_ready, 1)
                if h == HEADS0 - 1:
                    s = take("N")
                    add_to_stream(t, s)
                    stats(t, X[0:P, t, :])
            psum.align()

            def ffn_unit(chunks=K4, scaled=False, scalar=None, with_stats=True, between=lambda: None):
                for m in range(chunks):
                    s, k, _ = psum.next("W")
                    between()
                    h = SG[m % 2]
                    if scaled:
                        c = take("W")
                        dve.wait_ge(s.taken, k)
                        v.tensor_tensor(h, h, c.ap[:, 0:N], ALU.mult).then_inc(c.taken, 1)
                        dve.wait_ge(c.taken, n.now(c.filled))
                    b = take("W")
                    dve.wait_ge(s.taken, k)
                    v.tensor_tensor(HT[:, m, :], h, b.ap[:, 0:N], ALU.mult).then_inc(b.taken, 1)
                    between()
                    between()
                for t in range(NT):
                    add_to_stream(t, take("N"), None if scalar is None else scalar(t))
                    if with_stats:
                        stats(t, X[0:P, t, :])

            def quantized(u):
                for k, (j, c, width) in enumerate(groups_of(u)):
                    s = psum.next("N")
                    dve.wait_ge(s[0].taken, s[1])
                    w, z = AW[k % 2][:, 0:width], SCL[k % 2][:, 0:width]
                    step(v.scalar_tensor_tensor(w, w, 2.0, z, ALU.mult, ALU.is_gt))
                    v.tensor_tensor(z, z, w, ALU.mult).then_inc(kept_ready, 1)
                    yield

            for _ in quantized(0):
                pass
            norm_y()
            psum.skip(T=NT)
            for u in range(3):
                ahead = quantized(u + 1) if u < 2 else iter(())
                ffn_unit(WIDTHS[u] // 128, with_stats=(u == 2), between=lambda: next(ahead, None))

            norm_y()
            psum.skip(T=NT)
            step(v.tensor_reduce(TW[:, :, 0], G[:, :, :], AX.X, ALU.add))
            step(v.tensor_scalar(TW[:, :, 1], TW[:, :, 0], 1e-6, None, ALU.add))
            step(v.reciprocal(TW[:, :, 1], TW[:, :, 1]))
            step(v.tensor_scalar(TW[:, :, 2], TW[:, :, 0], 0.0, None, ALU.is_gt))
            for t in range(NT):
                last = v.tensor_scalar(G[:, t, :], G[:, t, :], TW[:, t, 1:2], None, ALU.mult)
            last.then_inc(layer_ready, 1)
            n.add(layer_ready)
            dve.wait_ge(rows_in, 16)
            for t in range(NT):
                s = take("N")
                v.tensor_tensor(MF[:, t, :], s.ap[0:P, 0:256], ROWS[:, R_BM:R_BM + 256], ALU.add)\
                 .then_inc(s.taken, 1)
            psum.skip(W=NT + 4)
            for t in range(NT):
                s = take("N")
                v.tensor_tensor(HB[:, t, :], s.ap[0:P, 0:128], ROWS[:, R_B1:R_B1 + 128], ALU.add)\
                 .then_inc(s.taken, 1)
                dve.wait_ge(s.taken, n.now(s.filled))
                stats(t, HB[:, t, :])
            for t in range(NT):
                step(norm(t, HB[:, t, :], HB[:, t, :]))
                step(v.tensor_tensor(HB[:, t, :], HB[:, t, :], ROWS[:, R_G1:R_G1 + 128], ALU.mult))
                step(v.tensor_tensor(HB[:, t, :], HB[:, t, :], ROWS[:, R_BE1:R_BE1 + 128], ALU.add))
                v.tensor_scalar(HB[:, t, :], HB[:, t, :], 0.0, None, ALU.max).then_inc(layer_ready, 1)
            psum.skip(T=NT)
            for t in range(NT):
                s = take("N")
                z = ROW[t % 2]
                v.tensor_tensor(z, s.ap[0:P, :], ROWS[:, R_B2:R_B2 + D], ALU.add).then_inc(s.taken, 1)
                dve.wait_ge(s.taken, n.now(s.filled))
                step(v.tensor_scalar(z, z, 0.0, TW[:, t, 2:3], ALU.max, ALU.mult))
                step(v.tensor_tensor(X[0:P, t, :], X[0:P, t, :], z, ALU.add))
                stats(t, X[0:P, t, :])

            def best_two(values, t):
                step(v.max(M8[:, t, :], values))
                step(v.max_index(I8[:, t, :], M8[:, t, :], values))

            def shares(t, first, second):
                step(v.tensor_copy(TW[:, t, 3:5], I8[:, t, 0:2]))
                step(v.tensor_scalar(M8[:, t, :], CS[0:P, C_I8:C_I8 + 8], TW[:, t, 3:4], first,
                                     ALU.is_equal, ALU.mult))
                step(v.tensor_scalar(LG[:, t, :], CS[0:P, C_I8:C_I8 + 8], TW[:, t, 4:5], second,
                                     ALU.is_equal, ALU.mult))
                return v.tensor_tensor(COMB[:, t, 0:8], M8[:, t, :], LG[:, t, :], ALU.add)

            def logits():
                for t in range(NT):
                    s = take("N")
                    v.tensor_copy(LG[:, t, :], s.ap[0:P, 0:8]).then_inc(s.taken, 1)
                    dve.wait_ge(s.taken, n.now(s.filled))

            def softmax_of_two():
                v.tensor_tensor(TW[:, :, 0], M8[:, :, 1], M8[:, :, 0], ALU.subtract).then_inc(negmax_ready, 1)
                dve.wait_ge(exp_ready, n.add(exp_ready))
                step(v.tensor_scalar(TW[:, :, 1], TW[:, :, 0], 1.0, None, ALU.add))
                step(v.reciprocal(TW[:, :, 1], TW[:, :, 1]))
                step(v.tensor_tensor(TW[:, :, 2], TW[:, :, 0], TW[:, :, 1], ALU.mult))

            norm_y()
            psum.skip(T=NT)
            logits()
            for t in range(NT):
                best_two(LG[:, t, :], t)
            softmax_of_two()
            for t in range(NT):
                shares(t, TW[:, t, 1:2], TW[:, t, 2:3]).then_inc(layer_ready, 1)
            psum.skip(T=NT)
            ffn_unit(scaled=True)

            for t in range(NT):
                last = norm(t, XL[:, t, :], X[0:P, t, :])
            last.then_inc(layer_ready, 1)
            n.add(layer_ready)
            for l in range(3):
                psum.skip(W=K4)
                for t in range(NT):
                    add_to_stream(t, take("N"), dst=XL)
                    stats(t, XL[:, t, :])
                for t in range(NT):
                    z = XL[:, t, :]
                    step(norm(t, z, z))
                    step(v.tensor_tensor(z, z, ROWS[:, R_G2 + D * l:R_G2 + D * (l + 1)], ALU.mult))
                    step(v.tensor_tensor(z, z, ROWS[:, R_BE2 + D * l:R_BE2 + D * (l + 1)], ALU.add))
                    last = v.tensor_scalar(z, z, 0.0, None, ALU.max)
                    if t < NT - 1 or l == 2:
                        step(last)
                if l < 2:
                    last.then_inc(layer_ready, 1)
            for t in range(NT):
                add = v.tensor_tensor(X[0:P, t, :], X[0:P, t, :], XL[:, t, :], ALU.add)
                if t == 0:
                    signal(add, attn_rows_free)
                elif t == 1:
                    signal(add, mlp_rows_free)
                else:
                    step(add)
                stats(t, X[0:P, t, :])

            norm_y()
            psum.skip(T=NT)
            logits()
            for t in range(NT):
                step(v.max(M8[:, t, :], LG[:, t, :]))
            softmax_of_two()

            def hidden_inputs(t):
                s = take("N")
                for i in range(2):
                    last = v.scalar_tensor_tensor(GE[t % 2][i], s.ap[0:P, :], TW[:, t, 1 + i:2 + i],
                                                  ROWS[:, R_FB1:R_FB1 + D], ALU.mult, ALU.add)
                    if i == 0:
                        last.then_inc(negmax_ready, 1)
                last.then_inc(s.taken, 1)

            for t in range(NT + 1):
                if t < NT:
                    if t >= 2:
                        dve.wait_ge(y_ready, n.now(y_ready))
                    hidden_inputs(t)
                if t:
                    dve.wait_ge(exp_ready, n.add(exp_ready, 2))
                    n.add(y_ready)
                    v.tensor_tensor(Y[0:P, t - 1, :], GE[(t - 1) % 2][0], GE[(t - 1) % 2][1], ALU.add)\
                     .then_inc(y_ready, 1)
            psum.skip(T=NT)
            for t in range(NT):
                add_to_stream(t, take("N"))
                stats(t, X[0:P, t, :])

            dve.wait_ge(noise_in, 16)
            col = lambda c: CS[0:64, c:c + 1]
            step(v.memset(CONDT, 1.0))
            step(v.tensor_scalar(EMN, EMN, col(C_FREQ), None, ALU.mult))
            step(v.tensor_scalar(EMB, EMN, 1.0 / (2.0 * np.pi), col(C_FRAC), ALU.mult, ALU.add))
            step(v.tensor_scalar(EMB, EMB, MAGIC, -MAGIC, ALU.add, ALU.add))
            for c in TWO_PI:
                step(v.scalar_tensor_tensor(EMN, EMB, -c, EMN, ALU.mult, ALU.add))
            step(v.tensor_scalar(EMN, EMN, col(C_SHIFT), 3.1415925, ALU.add, ALU.min))
            v.tensor_scalar(EMR, EMN, -3.1415925, None, ALU.max).then_inc(emb_ready, 2)
            for t in range(NT):
                step(norm(t, XL[:, t, :], X[0:P, t, :]))
                stats(t, XL[:, t, :])
            psum.skip(W=2)
            psum.align()

            def modulated_norm(br):
                for t in range(NT):
                    y = Y[0:P, t, :]
                    step(norm(t, y, XL[:, t, :]))
                    s = take("N")
                    v.scalar_tensor_tensor(y, s.ap[0:P, :], 1.0, y, ALU.add, ALU.mult).then_inc(s.taken, 1)
                    dve.wait_ge(s.taken, n.now(s.filled))
                    s = take("N")
                    step_y = v.tensor_tensor(y, y, s.ap[0:P, :], ALU.add)
                    step_y.then_inc(s.taken, 1)
                    dve.wait_ge(s.taken, n.now(s.filled))
                    v.tensor_copy(SM[:, 4:5], SM[:, 3:4]).then_inc(y_ready, 1)
                    n.add(y_ready)
                psum.skip(T=NT)

            with dve.Fori(0, BLOCKS) as i, n.loop(i, BLOCKS, loops, "block"):
                modulated_norm(0)
                for h in range(HEADS3):
                    s = take("W")
                    v.tensor_scalar(HT[:, h, :], s.ap[:, 0:N], PC[:, bass.ds(i * 12 + h, 1)],
                                    128.0 ** -0.5, ALU.add, ALU.mult).then_inc(s.taken, 1)
                    psum.skip(W=1)
                dve.wait_ge(br_in, n.add(br_in, 16))
                for t in range(NT):
                    s = take("N")
                    v.tensor_tensor(V[:, t, :], s.ap[0:P, :], BR[0:P, 0, :], ALU.add).then_inc(s.taken, 1)

                def maxima(h):
                    probs = G if h % 2 == 0 else PRB
                    for t in range(NT):
                        s = take("W")
                        carry()
                        v.tensor_tensor_reduce(out=probs[:, t, :], in0=s.ap[0:P, 0:N], in1=MASK[:, t, :],
                                               scale=1.0, scalar=-3.0e38, op0=ALU.add, op1=ALU.max,
                                               accum_out=DEN[:, h % 2, 0, t:t + 1]).then_inc(s.taken, 1)
                        dve.wait_ge(s.taken, n.now(s.filled))
                        v.tensor_scalar(DEN[:, h % 2, 1, t:t + 1], DEN[:, h % 2, 0, t:t + 1], -1.0, None,
                                        ALU.mult).then_inc(negmax_ready, 1)

                maxima(0)
                for h in range(HEADS3):
                    probs = G if h % 2 == 0 else PRB
                    for t in range(NT):
                        dve.wait_ge(exp_ready, n.add(exp_ready))
                        step(v.tensor_tensor_reduce(
                            out=probs[:, t, :], in0=probs[:, t, :], in1=CNT[:, t, :], scale=1.0,
                            scalar=0.0, op0=ALU.mult, op1=ALU.add, accum_out=DEN[:, h % 2, 2, t:t + 1]))
                    step(v.tensor_scalar(DEN[:, h % 2, 3, :], DEN[:, h % 2, 2, :], 1e-30, None, ALU.max))
                    step(v.reciprocal(DEN[:, h % 2, 3, :], DEN[:, h % 2, 3, :]))
                    for t in range(NT):
                        v.tensor_scalar(DIAG[:, h % 2, t, :], ID[0:P, 0:P], DEN[:, h % 2, 3, t:t + 1],
                                        None, ALU.mult).then_inc(prob_ready, 1)
                    if h + 1 < HEADS3:
                        maxima(h + 1)
                    psum.skip(W=NT + 1)
                for t in range(NT):
                    add_to_stream(t, take("N"), dst=XL)
                    last = v.tensor_tensor(XL[:, t, :], XL[:, t, :], BR[0:P, 1, :], ALU.add)
                    if t < NT - 1:
                        step(last)
                    else:
                        signal(last, attn_rows_free)
                    stats(t, XL[:, t, :])
                modulated_norm(2)
                psum.skip(W=K4)
                dve.wait_ge(br2_in, n.add(br2_in, 16))
                for t in range(NT):
                    add_to_stream(t, take("N"), dst=XL)
                    last = v.tensor_tensor(XL[:, t, :], XL[:, t, :], BR[0:P, 2, :], ALU.add)
                    if t < NT - 1:
                        step(last)
                    else:
                        signal(last, mlp_rows_free)
                    stats(t, XL[:, t, :])
                psum.align()
            dve.wait_ge(rstd_ready, n.add(rstd_ready, NT))
            for t in range(NT):
                step(v.tensor_tensor(X[0:P, t, :], X[0:P, t, :], XL[:, t, :], ALU.add))
                stats(t, X[0:P, t, :])

            norm_y()
            psum.skip(T=NT)
            logits()
            dve.wait_ge(small_in, 16 * SMALLS)
            for t in range(NT):
                step(v.max(M8[:, t, :], LG[:, t, :]))
            step(v.tensor_copy(TW[:, :, 0:2], M8[:, :, 0:2]))
            for t in range(NT):
                step(v.tensor_tensor(LG[:, t, :], LG[:, t, :], BI[:, :], ALU.add))
                best_two(LG[:, t, :], t)
            v.tensor_copy(SM[:, 4:5], SM[:, 3:4]).then_inc(negmax_ready, 1)
            dve.wait_ge(exp_ready, n.add(exp_ready))
            step(v.tensor_scalar(TW[:, :, 0:2], TW[:, :, 0:2], 1.0, None, ALU.add))
            step(v.reciprocal(TW[:, :, 0:2], TW[:, :, 0:2]))
            step(v.tensor_tensor(TW[:, :, 2], TW[:, :, 0], TW[:, :, 1], ALU.add))
            step(v.reciprocal(TW[:, :, 2], TW[:, :, 2]))
            for t in range(NT):
                step(v.tensor_scalar(TW[:, t, 0:2], TW[:, t, 0:2], TW[:, t, 2:3], None, ALU.mult))
                step(shares(t, TW[:, t, 0:1], TW[:, t, 1:2]))
            psum.align()
            with dve.Fori(0, 9) as i, n.loop(i, 9, loops, "expert"):
                for u in range(2):
                    ffn_unit(scalar=lambda t: COMB[:, t, bass.ds(i, 1)], with_stats=False)
            store_x(dve)
    return nc



def mat(w):
    return np.ascontiguousarray(w.reshape(K4, 128, -1).transpose(1, 0, 2)).reshape(128, -1)


def padded(w, rows, cols):
    out = np.zeros((rows, cols), w.dtype)
    out[:w.shape[0], :w.shape[1]] = w
    return out


def constants():
    c = np.zeros((128, C_END), np.float32)
    c[:, C_ID:C_ID + 128] = np.eye(128)
    c[:P, C_TRI:C_TRI + P] = np.tril(np.ones((P, P)), -1)
    c[:, C_I8:C_I8 + 8] = np.arange(8)
    freqs = np.arange(1, FREQS + 1, dtype=np.float32) * np.float32(2.0 * np.pi / 16)
    c[:2 * FREQS, C_FREQ] = np.concatenate([freqs, freqs])
    c[FREQS:2 * FREQS, C_SHIFT] = np.pi / 2
    c[FREQS:2 * FREQS, C_FRAC] = 0.25
    c[:, C_DUMP] = N * N + np.arange(128)
    for e in range(8):
        c[e, C_SEL + 64 * e:C_SEL + 64 * (e + 1)] = 1.0
    return c


def laid_out(i):
    i = {k: np.asarray(x) for k, x in i.items()}
    heads = lambda w: w.transpose(1, 0, 2).reshape(D, -1)
    col = lambda b: b.reshape(K4, 128).T
    a5 = i["L0_gnn_a"].reshape(HEADS0, 5, DH0)
    a = {
        "x": i["x"], "consts": constants(),
        "src_p": i["src"].reshape(P, ET), "dst_p": i["dst"].reshape(P, ET),
        "src_t": i["src"].reshape(P, ET).T.reshape(-1), "dst_t": i["dst"].reshape(P, ET).T.reshape(-1),
        "edge_weight": i["edge_weight"].reshape(P, ET),
        "edge_attr": i["edge_attr_64"].reshape(P, ET * 64),
        "noise": i["node_vec1"].reshape(-1),
        "W_e": mat(heads(i["L0_gnn_W_e"])), "W_r": mat(heads(i["L0_gnn_W_r"])),
        "arow": a5[:, 0:4].transpose(1, 0, 2).reshape(-1),
        "a_prd": col(a5[:, 4].reshape(-1)),
        "Wm": mat(i["L1_gnn_Wm"]), "W1": mat(i["L1_gnn_W1"]), "W2": i["L1_gnn_W2"],
        "e_W1": mat(heads(i["L1_ffn_W1"])), "e_W3": mat(heads(i["L1_ffn_W3"])),
        "e_W2": mat(i["L1_ffn_W2"].reshape(D, D)),
        "Wtop": np.stack([mat(w[:D]) for w in i["L2_gnn_Ws"]]),
        "Wbot": i["L2_gnn_Ws"][:, D:].transpose(1, 0, 2).reshape(64, -1),
        "f_W1": mat(heads(i["L2_ffn_W1"])), "f_W2": mat(i["L2_ffn_W2"].reshape(D, D)),
        "f_b2": i["L2_ffn_b2"],
        "gate_0": mat(i["L1_ffn_gate_w"]), "gate_1": mat(i["L2_ffn_Wg"]),
        "gate_2": mat(i["L3_ffn_gate_w"].T), "biases": i["L3_ffn_biases"],
        "f_w1": i["L3_gnn_f_w1"], "f_w2": i["L3_gnn_f_w2"],
        "f_cols": np.stack([i["L3_gnn_f_b1"], i["L3_gnn_f_b2"]], 1),
    }
    a["Wlast"] = np.concatenate([a["Wbot"], i["L2_gnn_bs"].reshape(1, -1)])
    a["rows"] = np.concatenate([i[f"L1_gnn_{k}"] for k in ("bm", "b1", "gamma", "beta", "b2")]
                               + [i["L2_gnn_gammas"].reshape(-1), i["L2_gnn_betas"].reshape(-1),
                                  i["L2_ffn_b1"].reshape(-1)])
    halves = lambda w: [w[:, D * u:D * (u + 1)] for u in range(3)]
    for name, w in (("gate", i["L0_ffn_w_gate"].T), ("up", i["L0_ffn_w_up"].T)):
        a[name] = np.stack([mat(padded(h, D, D)) for h in halves(w)])
    a["down"] = np.stack([mat(padded(h.T, D, D)) for h in halves(i["L0_ffn_w_down"])])
    g = lambda k: i[f"L3_gnn_{k}"]
    a["modw"] = np.stack([np.stack([np.concatenate([g(f"{k}_w")[b], g(f"{k}_b")[b][None]])
                                    for k in ("s1", "b1", "s2", "b2")], 1) for b in range(BLOCKS)])
    a["brow"] = np.stack([g(k) for k in ("bv", "bo", "m_b2")], 1).reshape(-1)
    a["columns"] = np.concatenate([col(g(k)[b]) for b in range(BLOCKS) for k in ("bq", "bk", "m_b1")], 1)
    a["qkv"] = np.stack([mat(g(k)[b]) for b in range(BLOCKS) for k in ("wq", "wk", "wv")])
    a["omm"] = np.stack([mat(g(k)[b]) for b in range(BLOCKS) for k in ("wo", "m_w1", "m_w2")])
    f = lambda k: i[f"L3_ffn_{k}"]
    for name, routed, shared in (("x_a", "w1", "sw1"), ("x_b", "w3", "sw3")):
        a[name] = np.stack([mat(w[:, D * u:D * (u + 1)]) for w in (*f(routed), f(shared)) for u in range(2)])
    a["x_c"] = np.stack([mat(w[D * u:D * (u + 1)]) for w in (*f("w2"), f("sw2")) for u in range(2)])
    return {k: np.ascontiguousarray(x) for k, x in a.items()}


def build(nc, arrays):
    aps = {k: nc.dram_tensor(f"in_{k}", x.shape, mybir.dt.from_np(x.dtype), kind="ExternalInput").ap()
           for k, x in arrays.items()}
    out = nc.dram_tensor("out_0", (N, D), F32, kind="ExternalOutput").ap()
    program(nc, aps, out, LOOPS)


def kernel(**inputs):
    import concourse.bacc as _bacc
    from concourse.bass_utils import run_bass_kernel_spmd as _run

    arrays = laid_out(inputs)
    nc = _bacc.Bacc("TRN2", target_bir_lowering=False, num_devices=1, dynamic_dma_scratch_size=8192)
    build(nc, arrays)
    r = _run(nc, [{f"in_{k}": x for k, x in arrays.items()}], core_ids=[0])
    return r.results[0]["out_0"]
```

```python
from contextlib import ExitStack, contextmanager

import numpy as np
import concourse.bass as bass
from concourse import mybir

F32, BF16, I16, I32, U32 = (mybir.dt.float32, mybir.dt.bfloat16, mybir.dt.int16, mybir.dt.int32,
                            mybir.dt.uint32)
ALU, ACT, AX = mybir.AluOpType, mybir.ActivationFunctionType, mybir.AxisListType

N, E, D = 625, 10000, 512
P, NT = 125, 5
ET = E // P
K4 = D // 128
HEADS0, DH0 = 8, 64
HEADS3 = 4
BLOCKS = 4
FREQS = 32
NEG = -1.0e30
BANK = 512
MAIN, TAIL = BANK, N - BANK
MAGIC = 12582912.0
STEP = 16
TURNS = ET // STEP
GATHERS_A, GATHERS_B = 4, 12
AHEAD = 4
ROWLEN = D + 2 * HEADS0

C_ID, C_TRI, C_I8, C_FREQ, C_SHIFT, C_FRAC, C_DUMP, C_SEL = 0, 128, 253, 261, 262, 263, 264, 265
C_END = C_SEL + D
R_BM, R_B1, R_G1, R_BE1, R_B2, R_G2, R_BE2, R_FB1 = 0, 256, 384, 512, 640, 1152, 2688, 4224
R_END = 4736


class Tally:

    def __init__(self, engine):
        self.engine, self.count, self.turn, self.per, self.base = engine, {}, None, {}, {}

    def add(self, sem, n=1):
        self.count[sem.name] = self.count.get(sem.name, 0) + n
        return self.now(sem)

    def now(self, sem):
        c = self.count.get(sem.name, 0)
        if self.turn is None:
            return c
        return self.turn * self.per.get(sem.name, 0) + c

    @contextmanager
    def loop(self, turn, trips, loops, name):
        per = loops[name].get(self.engine, {})
        self.turn, self.per, before = turn, per, dict(self.count)
        yield
        grew = {k: c - before.get(k, 0) for k, c in self.count.items() if c != before.get(k, 0)}
        for k, c in grew.items():
            self.count[k] += (trips - 1) * c
        wrong = grew != {k: v for k, v in per.items() if v}
        self.turn, self.per = None, {}
        assert not wrong, (name, self.engine, grew)


LOOPS = {
    "count": {
        "pe": {"onehot_ready": 16},
        "dve": {"vector_step": 20, "onehot_used": 16, "gathered_0": 32, "gathered_1": 32, "abs_ready":
               4, "score_taken": 4, "gathered_2": 32, "gathered_3": 32},
    },
    "weight": {
        "pe": {"onehot_ready": 16},
        "dve": {"vector_step": 60, "onehot_used": 16, "gathered_0": 96, "gathered_1": 96, "abs_ready":
               12, "score_taken": 12, "gathered_2": 96, "gathered_3": 96},
    },
    "edge": {
        "pe": {"onehot_ready": 16},
        "dve": {"edge_read": 4, "vector_step": 16, "onehot_used": 16, "edge_in_0": 16, "edge_in_1":
               16, "edge_in_2": 16, "edge_in_3": 16},
    },
    "gather": {
        "pool": {"score_taken": 4, "pool_step": 8, "score_ready": 4, "scattered": 64},
    },
    "block": {
        "pe": {"filled_T0": 5, "y_ready": 10, "filled_T1": 5, "weights_in_0": 48, "filled_N0": 18,
               "filled_N1": 17, "filled_W0": 28, "filled_W1": 28, "prob_ready": 20, "weights_in_1":
               48, "modw_in": 16, "mod2_in": 16},
        "act": {"filled_T0": 5, "filled_T1": 5, "filled_N0": 18, "filled_N1": 17, "filled_W0": 28,
               "filled_W1": 28, "negmax_ready": 20},
        "dve": {"vector_step": 66, "y_ready": 10, "rstd_ready": 10, "filled_T0": 5, "filled_T1": 5,
               "filled_N0": 18, "filled_N1": 17, "filled_W0": 28, "filled_W1": 28, "exp_ready": 20,
               "br_in": 16, "attn_rows_free": 1, "br2_in": 16, "mlp_rows_free": 1},
        "pool": {"var_ready": 10},
    },
    "expert": {
        "pe": {"weights_in_0": 48, "filled_N0": 5, "filled_N1": 5, "filled_W0": 8, "filled_W1": 8,
               "weights_in_1": 48},
        "act": {"filled_N0": 5, "filled_N1": 5, "filled_W0": 8, "filled_W1": 8},
        "dve": {"filled_N0": 5, "filled_N1": 5, "filled_W0": 8, "filled_W1": 8},
    },
    "abs": {
        "act": {"diff_ready": 2},
    },
}
TWO_PI = (6.28125, 2029.0 / 2 ** 20, 2.0 * np.pi - 6.28125 - 2029.0 / 2 ** 20)


WIDTHS = (D, D, 1408 - 2 * D)
SMALLS = 8


def groups_of(u):
    return ([(j, c, WIDTHS[u]) for j in range(2) for c in range(K4)]
            + [(2, c, D) for c in range(WIDTHS[u] // 128)])


def bcast(row, at, n, parts):
    return row[bass.ds(at, n)].partition_broadcast(parts)


class Slot:
    def __init__(self, ap, filled, taken):
        self.ap, self.filled, self.taken = ap, filled, taken


class Slots:

    def __init__(self, slots, tally):
        self.slots, self.tally, self.turn = slots, tally, {"T": 0, "W": 0, "N": 0}

    def next(self, kind):
        s = self.slots[kind][self.turn[kind] % 2]
        self.turn[kind] += 1
        first = self.tally.turn is None and self.tally.count.get(s.filled.name, 0) == 0
        before = None if first else self.tally.now(s.filled)
        return s, self.tally.add(s.filled), before

    def skip(self, **kinds):
        for kind, n in kinds.items():
            for _ in range(n):
                self.next(kind)

    def align(self):
        self.turn = {"T": 0, "W": 0, "N": 0}


def program(nc, a, out, loops):
    ctx = ExitStack()

    def sb(name, shape, dt=F32):
        return ctx.enter_context(nc.sbuf_tensor(name, shape, dt))

    def sem(name):
        return ctx.enter_context(nc.semaphore(name))

    hr_rows = nc.dram_tensor("hr_rows", [N, ROWLEN], F32, kind="Internal").ap()
    pair_scores = nc.dram_tensor("pair_scores", [N * N + 128, HEADS0], F32, kind="Internal").ap()

    with ctx:

        X = sb("X", [128, NT, D])
        Y = sb("Y", [128, NT, D])
        XT = sb("XT", [128, K4, N])
        WR = sb("WR", [128, 2, 3, K4 * D])
        CNT = sb("CNT", [P, NT, N])
        MASK = sb("MASK", [P, NT, N], BF16)
        G = sb("G", [P, NT, N])
        EA1 = sb("EA1", [128, N])
        EA2 = sb("EA2", [128, N])
        MODW = sb("MODW", [128, 4, D])
        BR = sb("BR", [128, 3, D])
        CS = sb("CS", [128, C_END])
        PC = sb("PC", [128, 3 * K4 * BLOCKS])
        FW = sb("FW", [64, 34])
        IOTA = sb("IOTA", [P, N], I16)
        ONES = sb("ONES", [128, 128])
        HALF = sb("HALF", [P, 1])
        ST = sb("ST", [P, NT, 6])
        MV = sb("MV", [P, NT, 2])
        VE = sb("VE", [P, NT])
        RSTD = sb("RSTD", [P, NT])
        SM = sb("SM", [P, 64])
        DEN = sb("DEN", [P, 2, 4, NT])
        DIAG = sb("DIAG", [P, 2, NT, P])
        LG = sb("LG", [P, NT, 8])
        M8 = sb("M8", [P, NT, 8])
        I8 = sb("I8", [P, NT, 8], U32)
        TW = sb("TW", [P, NT, 6])
        COMB = sb("COMB", [P, NT, 9])
        ISRC = sb("ISRC", [P, ET], U32)
        IDST = sb("IDST", [P, ET], U32)
        SIDX = sb("SIDX", [P, ET], U32)
        FS = sb("FS", [P, 9, ET])
        IDS = sb("IDS", [P, 3 * AHEAD], U32)
        TS = sb("TS", [P, AHEAD, HEADS0])
        SUMS = sb("SUMS", [P, 2, HEADS0])
        HM = sb("HM", [P, 2, 4, HEADS0])
        KEYT = sb("KEYT", [ET, P])
        UV = sb("UV", [128, K4, 16])
        WG = sb("WG", [128, 3, K4, 8])
        BI = sb("BI", [P, 8])
        TWOS = sb("TWOS", [8, P])
        UVT = sb("UVT", [128, 3, 4 * HEADS0])
        EB = sb("EB", [P, ET], BF16)
        HT_, XL_, PT_, KT_, V_, PR_ = 0, 2500, 5060, 8185, 10745, 13305
        AR = sb("AR", [128, PR_ + R_END])

        def view(at, parts, *shape, dt=F32):
            n = 1
            for s in shape:
                n *= s
            words = n if dt in (F32, I32, U32) else (n + 1) // 2
            v = AR[0:parts, at:at + words]
            if dt != F32:
                v = v.bitcast(dt)[:, 0:n]
            if len(shape) == 1:
                return v
            names = "abc"[:len(shape)]
            return v.rearrange(f"p ({' '.join(names)}) -> p {' '.join(names)}",
                               **{k: s for k, s in zip(names[1:], shape[1:])})

        HT = view(HT_, 128, K4, N)
        XL = view(XL_, P, NT, D)
        HE = XL
        PT = view(PT_, P, NT, N)
        KT = view(KT_, 128, HEADS3, N)
        V = view(V_, P, NT, D)
        PRB = view(PR_, P, NT, N)
        ROWS = view(PR_, P, R_END)
        HS = [view(PT_ + 2 * ROWLEN * b, P, ROWLEN) for b in range(AHEAD)]
        HD = [view(PT_ + 2 * ROWLEN * b + ROWLEN, P, ROWLEN) for b in range(AHEAD)]
        PRD = [view(HT_ + 2 * D * b, P, 2, D) for b in range(2)]
        OS = [view(V_ + 313 * b, P, N, dt=BF16) for b in range(2)]
        OD = [[view(V_ + 313 * (2 + 3 * b + r), P, N, dt=BF16) for r in range(3)] for b in range(2)]
        ZROW = view(PR_, P, 2500)
        ZB = view(PR_ + 2500, P, BANK, dt=BF16)
        ER = [view(PR_ + 256 * b, P, 4, 64) for b in range(4)]
        ERR = view(PR_ + 3268, P, 4, 64)
        S1 = [view(PR_ + 3524 + 256 * b, P, 4, 128, dt=BF16) for b in range(2)]
        S2 = [view(PR_ + 4036 + 132 * b, P, 4, 66, dt=BF16) for b in range(2)]
        GF = G[:, :, :].rearrange("p a b -> p (a b)")
        KROW = GF[:, 0:20 * P].rearrange("p (m e) -> p m e", e=P)
        HRN = CNT[:, :, :].rearrange("p a b -> p (a b)")[:, 0:NT * ROWLEN].rearrange(
            "p (t c) -> p t c", t=NT)
        TSC = [view(PT_ + 5000 * b, P, N * HEADS0) for b in range(2)]
        SP0 = [view(HT_ + 625 * b, P, N) for b in range(4)]
        PTS = [view(PT_ + 10000 + 625 * b, P, NT, P) for b in range(2)]
        SG = [view(PT_ + 625 * b, 128, N) for b in range(2)]
        ROW = [view(PT_ + 1250 + 512 * b, P, D) for b in range(2)]
        MF = view(KT_, P, NT, 256)
        HB = view(V_, P, NT, 128)
        HBT = view(V_ + 640, 128, N)
        GE = [[view(PT_ + 1250 + 512 * (2 * b + i), P, D) for i in range(2)] for b in range(2)]
        EMB = view(PT_, 64, N)
        EMN = view(PT_ + 625, 64, N)
        EMR = view(PT_ + 1250, 64, N)
        ZC = view(PT_ + 1875, 16, N)
        CONDT = EA1[0:17, :]
        CT8 = view(V_, 8, N)
        WTMP = view(HT_, 128, K4, D)
        AW = [MODW[:, b, :] for b in range(2)]
        SGN = [MODW[:, 2 + b, :] for b in range(2)]
        SCL = [BR[:, 1 + b, :] for b in range(2)]

        ID = CS[:, C_ID:C_ID + 128]
        SEL = CS[0:8, C_SEL:C_SEL + D]

        def wm(s, j, n=D):
            return WR[:, s, j, :].rearrange("p (c n) -> p c n", c=K4)[:, :, 0:n]


        PS = ctx.enter_context(nc.psum_tensor("PS", [128, 8 * BANK], F32))
        slots = {}
        for kind, at, size in (("T", 0, BANK), ("W", 2 * BANK, 2 * BANK), ("N", 6 * BANK, BANK)):
            slots[kind] = [Slot(PS[:, at + k * size:at + (k + 1) * size], sem(f"filled_{kind}{k}"),
                                sem(f"taken_{kind}{k}")) for k in range(2)]

        def main_of(c):
            return PS[0:P, BANK * c:BANK * c + MAIN]

        def tail_of(c):
            at = 5 * BANK + TAIL * c if c < 4 else 6 * BANK
            return PS[0:P, at:at + TAIL]


        x_in, consts_in, index_in, arow_in, small_in = map(sem, (
            "x_in", "consts_in", "index_in", "arow_in", "small_in"))
        loaded = [sem("weights_in_0"), sem("weights_in_1")]
        rows_in, edge_in = sem("rows_in"), [sem(f"edge_in_{b}") for b in range(4)]
        modw_in, br_in, mod2_in, br2_in, noise_in = map(sem, ("modw_in", "br_in", "mod2_in", "br2_in", "noise_in"))
        weights_used = sem("weights_used")
        vector_step, pool_step, scalar_step = sem("vector_step"), sem("pool_step"), sem("scalar_step")
        start_done = sem("pool_constants")
        var_ready, rstd_ready = sem("var_ready"), sem("rstd_ready")
        y_ready = sem("y_ready")
        uv_ready, hr_stored = sem("uv_ready"), sem("hr_stored")
        onehot_ready, onehot_used = sem("onehot_ready"), sem("onehot_used")
        gathered = [sem(f"gathered_{b}") for b in range(AHEAD)]
        score_ready, scattered = sem("score_ready"), sem("scattered")
        cleared, clear_row_ready = sem("cleared"), sem("clear_row_ready")
        keys_ready, sidx_ready = sem("keys_ready"), sem("sidx_ready")
        graph_filled, graph_taken = sem("graph_filled"), sem("graph_taken")
        edge_read = sem("edge_read")
        pairs_in = [sem("pair_scores_in_0"), sem("pair_scores_in_1")]
        negmax_ready, exp_ready, prob_ready = sem("negmax_ready"), sem("exp_ready"), sem("prob_ready")
        absw_ready, kept_ready, quant_ready = sem("absw_ready"), sem("kept_ready"), sem("quant_ready")
        diff_ready, abs_ready = sem("diff_ready"), sem("abs_ready")
        score_taken = sem("score_taken")
        layer_ready = sem("layer_ready")
        attn_rows_free, mlp_rows_free = sem("attn_rows_free"), sem("mlp_rows_free")
        emb_ready, sin_ready = sem("emb_ready"), sem("sin_ready")
        out_ready, out_done = sem("out_ready"), sem("out_done")

        def store_x(eng):
            eng.drain().then_inc(out_ready, 1)

        block = ctx.enter_context(nc.Block())
        def loads(sp):
            n = Tally("sp")
            sp.dma_start(X[0:P, :, :], a["x"].rearrange("(t p) d -> p t d", p=P)).then_inc(x_in, 16)
            sp.dma_start(CS[:, :], a["consts"]).then_inc(consts_in, 16)
            batch = [0]

            def load(mats):
                k = batch[0]
                batch[0] += 1
                if k >= 2:
                    sp.wait_ge(weights_used, k - 1)
                for dst, src in mats:
                    sp.dma_start(dst, src).then_inc(loaded[k % 2], 16)

            def mat(s, j, name, at=None):
                src = a[name] if at is None else a[name][at]
                return WR[:, s, j, :], src

            load([mat(0, 0, "W_e"), mat(0, 1, "W_r")])
            load([mat(1, 0, "gate", 0), mat(1, 1, "up", 0), mat(1, 2, "down", 0)])
            sp.wait_ge(clear_row_ready, 1)
            for t in range(NT):
                dst = pair_scores[N * P * t:N * P * (t + 1), :].rearrange("(p q) h -> p (q h)", p=P)
                for half in range(2):
                    sp.dma_start(dst[:, 2500 * half:2500 * (half + 1)], ZROW).then_inc(cleared, 16)
            sp.wait_ge(cleared, 16 * 2 * NT)
            with sp.Fori(0, TURNS) as i:
                for b in range(4):
                    sp.wait_ge(edge_read, i * 4 + b + 1)
                    sp.dma_start(ER[b].rearrange("p a b -> p (a b)"),
                                 a["edge_attr"][:, bass.ds(i * 1024 + 256 * b, 256)]).then_inc(edge_in[b], 16)
            load([mat(0, 0, "gate", 1), mat(0, 1, "up", 1), mat(0, 2, "down", 1)])
            sp.wait_ge(scattered, 16 * ET)
            for t in range(NT):
                if t == 1:
                    sp.wait_ge(graph_taken, 3)
                if t >= 2:
                    sp.wait_ge(exp_ready, 1 + HEADS0 * (t - 1))
                src = pair_scores[N * P * t:N * P * (t + 1), :].rearrange("(p q) h -> p (q h)", p=P)
                sp.dma_start(TSC[t % 2], src).then_inc(pairs_in[t % 2], 16)
            load([mat(1, 0, "gate", 2), mat(1, 1, "up", 2), mat(1, 2, "down", 2)])
            sp.dma_start(ROWS, bcast(a["rows"], 0, R_END, P)).then_inc(rows_in, 16)
            load([(WR[:, 0, 0, 0:K4 * 256], a["Wm"]), (WR[:, 0, 1, 0:K4 * 128], a["W1"]),
                  (WR[:, 0, 2, 0:D], a["W2"])])
            load([mat(1, j, x) for j, x in enumerate(("e_W1", "e_W3", "e_W2"))])
            load([mat(0, j, "Wtop", j) for j in range(3)])
            load([(WR[0:64, 1, 0, 0:3 * D], a["Wbot"]), (WR[64:128, 1, 0, 0:3 * D], a["Wbot"]),
                  (WR[0:65, 1, 1, 0:3 * D], a["Wlast"])])
            load([mat(0, 0, "f_W1"), mat(0, 1, "f_W2"), (WR[0:8, 0, 2, 0:D], a["f_b2"])])
            def attn_rows(i):
                sp.dma_start(MODW[0:17, 0:2, :], a["modw"][bass.ds(i, 1), :, 0:2, :].rearrange(
                    "a p b n -> (a p) b n")).then_inc(modw_in, 16)
                sp.dma_start(BR[0:P, 0:2, :], bcast(a["brow"], i * 3 * D, 2 * D, P).rearrange(
                    "p (a b) -> p a b", a=2)).then_inc(br_in, 16)

            def mlp_rows(i):
                sp.dma_start(MODW[0:17, 2:4, :], a["modw"][bass.ds(i, 1), :, 2:4, :].rearrange(
                    "a p b n -> (a p) b n")).then_inc(mod2_in, 16)
                sp.dma_start(BR[0:P, 2, :], bcast(a["brow"], i * 3 * D + 2 * D, D, P)).then_inc(br2_in, 16)

            sp.dma_start(EMN, bcast(a["noise"], 0, N, 64)).then_inc(noise_in, 16)
            k0 = batch[0]
            with sp.Fori(0, BLOCKS) as i:
                sp.wait_ge(attn_rows_free, i + 1)
                attn_rows(i)
                sp.wait_ge(weights_used, i * 2 + k0 - 1)
                for j in range(3):
                    sp.dma_start(WR[:, 1, j, :], a["qkv"][bass.ds(i * 3 + j, 1)].rearrange(
                        "a p n -> (a p) n")).then_inc(loaded[1], 16)
                sp.wait_ge(mlp_rows_free, i + 1)
                mlp_rows(i)
                sp.wait_ge(weights_used, i * 2 + k0)
                for j in range(3):
                    sp.dma_start(WR[:, 0, j, :], a["omm"][bass.ds(i * 3 + j, 1)].rearrange(
                        "a p n -> (a p) n")).then_inc(loaded[0], 16)
            k1 = k0 + 2 * BLOCKS
            with sp.Fori(0, 9) as i:
                for u in range(2):
                    sp.wait_ge(weights_used, i * 2 + k1 + u - 1)
                    for j, x in enumerate(("x_a", "x_b", "x_c")):
                        sp.dma_start(WR[:, 1 - u, j, :], a[x][bass.ds(i * 2 + u, 1)].rearrange(
                            "a p n -> (a p) n")).then_inc(loaded[1 - u], 16)

        @block.sync
        def _(sp):
            loads(sp)
            sp.wait_ge(out_ready, 1)
            sp.dma_start(out.rearrange("(t p) d -> p t d", p=P), X[0:P, :, :]).then_inc(out_done, 16)
            sp.wait_ge(out_done, 16)

        @block.tensor
        def _(pe):
            n = Tally("pe")
            psum = Slots(slots, n)
            mm = nc.tensor.matmul

            def fill(kind):
                s, _, before = psum.next(kind)
                if before is not None:
                    pe.wait_ge(s.taken, before)
                return s

            def weights(s, mats):
                pe.wait_ge(loaded[s], n.add(loaded[s], 16 * mats))

            def weights_done():
                pe.drain().then_inc(weights_used, 1)

            def wide(s, parts, terms, lhs, rhs):
                for c0, c1 in ((0, MAIN), (MAIN, N)):
                    for k in range(terms):
                        last = mm(s.ap[0:parts, c0:c1], lhs(k), rhs(k)[:, c0:c1],
                                  start=(k == 0), stop=(k == terms - 1))
                last.then_inc(s.filled, 1)

            def narrow(s, cols, pairs):
                for k, (lhs, rhs) in enumerate(pairs):
                    last = mm(s.ap[0:P, 0:cols], lhs, rhs, start=(k == 0), stop=(k == len(pairs) - 1))
                last.then_inc(s.filled, 1)

            def tile(t):
                return slice(P * t, P * (t + 1))

            def transpose_y():
                for t in range(NT):
                    s = fill("T")
                    pe.wait_ge(y_ready, n.add(y_ready))
                    for c in range(K4):
                        last = nc.tensor.transpose(s.ap[:, P * c:P * (c + 1)],
                                                   Y[0:P, t, 128 * c:128 * (c + 1)], ID[0:P, 0:P])
                    last.then_inc(s.filled, 1)
                all_taken("T")

            def all_taken(kinds):
                for kind in kinds:
                    for s in slots[kind]:
                        pe.wait_ge(s.taken, n.now(s.filled))

            def project_wide(w, m):
                s = fill("W")
                wide(s, 128, K4, lambda k: w[:, k, 128 * m:128 * (m + 1)], lambda k: XT[:, k, :])
                return s, n.now(s.filled)

            def project_narrow(w, t, cols=D, extra=()):
                s = fill("N")
                narrow(s, cols, list(extra) + [(XT[:, k, tile(t)], w[:, k, 0:cols]) for k in range(K4)])


            pe.wait_ge(consts_in, 16)
            pe.wait_ge(start_done, 6)
            transpose_y()
            weights(0, 2)
            we, wr = wm(0, 0), wm(0, 1)
            for t in range(NT):
                project_narrow(wr, t)
            for t in range(NT):
                project_narrow(we, t)
            pe.wait_ge(uv_ready, 1)
            s = fill("N")
            for t in range(NT):
                for k in range(K4):
                    last = mm(s.ap[0:P, 16 * t:16 * t + 16], XT[:, k, tile(t)], UV[:, k, :],
                              start=(k == 0), stop=(k == K4 - 1))
            last.then_inc(s.filled, 1)
            weights_done()
            s = fill("N")
            pe.wait_ge(layer_ready, n.add(layer_ready))
            nc.tensor.transpose(s.ap[0:1, 0:P], SM[:, 0:1], ID[0:P, 0:P]).then_inc(s.filled, 1)
            s = fill("N")
            pe.wait_ge(layer_ready, n.add(layer_ready))
            mm(s.ap[0:P, 0:1], ONES[0:1, 0:P], SM[0:1, 1:2], start=True, stop=True).then_inc(s.filled, 1)

            s = fill("T")
            pe.wait_ge(keys_ready, 1)
            nc.tensor.transpose(s.ap[0:ET, 0:P], FS[:, 2, :], ID[0:P, 0:P]).then_inc(s.filled, 1)
            all_taken("T")
            for q in range(ET // 4):
                s = fill("N")
                for k in range(4):
                    m = 4 * q + k
                    last = mm(s.ap[0:P, P * k:P * (k + 1)], ID[0:ET, m:m + 1].broadcast_to([ET, P]),
                              KEYT[:, :], start=True, stop=True)
                last.then_inc(s.filled, 1)


            banks = [(BANK * c, MAIN) for c in range(5)] + [(5 * BANK, 4 * TAIL), (6 * BANK, TAIL)]

            def zero(banks, signal):
                for k, (at, size) in enumerate(banks):
                    last = mm(PS[0:128, at:at + size], ZB[:, 0:128], ZB[:, 0:size], start=True,
                              stop=False, skip_group_check=True)
                    if signal and k >= len(banks) - 2:
                        last.then_inc(onehot_used, 1)

            def close(banks):
                for at, size in banks:
                    last = mm(PS[0:128, at:at + size], ZB[:, 0:128], ZB[:, 0:size], start=False,
                              stop=True, skip_group_check=True)
                last.then_inc(graph_filled, 1)

            def pair_pass(name, parts):
                with pe.Fori(0, TURNS) as i, n.loop(i, TURNS, loops, name):
                    for k in range(STEP):
                        pe.wait_ge(onehot_ready, n.add(onehot_ready))
                        for c in range(NT):
                            for r in range(parts):
                                mm(main_of(c), OS[k % 2][:, tile(c)], OD[k % 2][r][:, 0:MAIN],
                                   start=False, stop=False, skip_group_check=True)
                                last = mm(tail_of(c), OS[k % 2][:, tile(c)], OD[k % 2][r][:, MAIN:N],
                                          start=False, stop=False, skip_group_check=True)
                        last.then_inc(onehot_used, 1)

            all_taken("TN")
            pe.wait_ge(clear_row_ready, 1)
            zero(banks, True)
            pair_pass("count", 1)
            close(banks)
            pe.wait_ge(graph_taken, 1)
            zero(banks, False)
            pair_pass("weight", 3)
            close(banks)
            pe.wait_ge(graph_taken, 2)
            ea = [(2 * BANK, MAIN), (3 * BANK, TAIL), (4 * BANK, MAIN), (5 * BANK, TAIL)]
            zero(ea, False)
            with pe.Fori(0, TURNS) as i, n.loop(i, TURNS, loops, "edge"):
                for k in range(STEP):
                    pe.wait_ge(onehot_ready, n.add(onehot_ready))
                    b = k // 4 % 2
                    for part, rows, at in ((S1[b][:, k % 4, :], 128, 2), (S2[b][:, k % 4, 0:65], 65, 4)):
                        mm(PS[0:rows, at * BANK:at * BANK + MAIN], part, OD[k % 2][0][:, 0:MAIN],
                           start=False, stop=False, skip_group_check=True)
                        last = mm(PS[0:rows, (at + 1) * BANK:(at + 1) * BANK + TAIL], part,
                                  OD[k % 2][0][:, MAIN:N], start=False, stop=False, skip_group_check=True)
                    last.then_inc(onehot_used, 1)
            close(ea)
            pe.wait_ge(graph_taken, 3)

            def quantized(u):
                for k, (j, c, width) in enumerate(groups_of(u)):
                    g = fill("T")
                    pe.wait_ge(absw_ready, n.add(absw_ready))
                    mm(g.ap[:, 0:width], ONES[:, :], AW[k % 2][:, 0:width], start=True, stop=True)\
                        .then_inc(g.filled, 1)
                    yield

            def transposed(k):
                s = fill("W")
                pe.wait_ge(prob_ready, n.add(prob_ready))
                for c in range(NT):
                    last = nc.tensor.transpose(s.ap[0:P, 128 * c:128 * c + P], SP0[k % 4][:, tile(c)],
                                               ID[0:P, 0:P])
                last.then_inc(s.filled, 1)
                return s, n.now(s.filled)

            ahead = quantized(0)
            head = transposed(0)
            for k in range(NT * HEADS0):
                h, now = k % HEADS0, head
                if k + 1 < NT * HEADS0:
                    head = transposed(k + 1)
                if h == 0:
                    o = fill("N")
                pe.wait_ge(now[0].taken, now[1])
                for c in range(NT):
                    last = mm(o.ap[0:P, DH0 * h:DH0 * (h + 1)], PTS[k % 2][:, c, :],
                              HE[:, c, DH0 * h:DH0 * (h + 1)], start=(c == 0), stop=(c == NT - 1))
                if h == HEADS0 - 1:
                    last.then_inc(o.filled, 1)
                if k % 3 == 2:
                    next(ahead, None)
            for _ in ahead:
                pass
            psum.align()

            def ffn_unit(s, chunks=K4, scaled=False, between=lambda: None):
                wa, wb, wc = wm(s, 0), wm(s, 1), wm(s, 2)
                hidden = []
                for m in range(chunks):
                    project_wide(wa, m)
                    between()
                    if scaled:
                        b = fill("W")
                        wide(b, 128, 1, lambda k: SEL[:, 128 * m:128 * (m + 1)], lambda k: CT8)
                    hidden.append(project_wide(wb, m))
                    between()
                    between()
                for t in range(NT):
                    o = fill("N")
                    for m in range(chunks):
                        if t == 0:
                            pe.wait_ge(hidden[m][0].taken, hidden[m][1])
                        last = mm(o.ap[0:P, :], HT[:, m, tile(t)], wc[:, m, :],
                                  start=(m == 0), stop=(m == chunks - 1))
                    last.then_inc(o.filled, 1)

            transpose_y()
            for u in range(3):
                weights((u + 1) % 2, 3)
                pe.wait_ge(quant_ready, n.add(quant_ready, len(groups_of(u))))
                ahead = quantized(u + 1) if u < 2 else iter(())
                ffn_unit((u + 1) % 2, WIDTHS[u] // 128, between=lambda: next(ahead, None))
                weights_done()

            transpose_y()
            weights(0, 3)
            w_m = WR[:, 0, 0, 0:K4 * 256].rearrange("p (c n) -> p c n", c=K4)
            w_1 = WR[:, 0, 1, 0:K4 * 128].rearrange("p (c n) -> p c n", c=K4)
            w_2 = WR[:, 0, 2, 0:D]
            for t in range(NT):
                project_narrow(w_m, t, 256)
            pe.wait_ge(layer_ready, n.add(layer_ready))
            for c in range(NT):
                s = fill("W")
                for t in range(NT):
                    last = nc.tensor.transpose(s.ap[0:P, 128 * t:128 * t + P], G[:, t, tile(c)], ID[0:P, 0:P])
                last.then_inc(s.filled, 1)
            all_taken("WN")
            for f in range(4):
                s = fill("W")
                by = PT if f < 2 else G
                wide(s, 128, NT, lambda k: MF[:, k, 128 * (f % 2):128 * (f % 2 + 1)], lambda k: by[:, k, :])
            all_taken("W")
            for t in range(NT):
                s = fill("N")
                narrow(s, 128, [(HT[:, f, tile(t)], w_1[:, f, :]) for f in range(4)])
            for t in range(NT):
                s = fill("T")
                pe.wait_ge(layer_ready, n.add(layer_ready))
                nc.tensor.transpose(s.ap[:, 0:P], HB[:, t, :], ID[0:P, 0:P]).then_inc(s.filled, 1)
            all_taken("T")
            for t in range(NT):
                s = fill("N")
                narrow(s, D, [(HBT[:, tile(t)], w_2)])
            weights_done()

            transpose_y()
            pe.wait_ge(small_in, 16 * SMALLS)
            for t in range(NT):
                project_narrow(WG[:, 0], t, 8)
            for t in range(NT):
                s = fill("T")
                pe.wait_ge(layer_ready, n.add(layer_ready))
                nc.tensor.transpose(s.ap[0:8, 0:P], COMB[:, t, 0:8], ID[0:P, 0:P]).then_inc(s.filled, 1)
            all_taken("T")
            weights(1, 3)
            ffn_unit(1, scaled=True)
            weights_done()

            weights(0, 3)
            weights(1, 3)
            for l in range(3):
                pe.wait_ge(layer_ready, n.add(layer_ready))
                for f in range(K4):
                    s = fill("W")
                    wide(s, 128, NT, lambda k: XL[:, k, 128 * f:128 * (f + 1)], lambda k: CNT[:, k, :])
                all_taken("W")
                for t in range(NT):
                    s = fill("N")
                    narrow(s, D, [(EA1[:, tile(t)], WR[:, 1, 0, D * l:D * (l + 1)]),
                                  (EA2[0:65, tile(t)], WR[0:65, 1, 1, D * l:D * (l + 1)])]
                           + [(HT[:, f, tile(t)], wm(0, l)[:, f, :]) for f in range(K4)])
            weights_done()
            weights_done()

            transpose_y()
            for t in range(NT):
                project_narrow(WG[:, 1], t, 8)
            weights(0, 3)
            for t in range(NT):
                project_narrow(wm(0, 0), t)
            for t in range(NT):
                s = fill("T")
                pe.wait_ge(y_ready, n.add(y_ready))
                for c in range(K4):
                    last = nc.tensor.transpose(s.ap[:, P * c:P * (c + 1)],
                                               Y[0:P, t, 128 * c:128 * (c + 1)], ID[0:P, 0:P])
                last.then_inc(s.filled, 1)
            all_taken("T")
            for t in range(NT):
                s = fill("N")
                narrow(s, D, [(TWOS[:, :], WR[0:8, 0, 2, 0:D])]
                       + [(HT[:, k, tile(t)], wm(0, 1)[:, k, :]) for k in range(K4)])
            weights_done()

            s = fill("W")
            pe.wait_ge(sin_ready, 1)
            wide(s, 16, 1, lambda k: FW[0:64, 0:16], lambda k: EMR)
            pe.wait_ge(s.taken, n.now(s.filled))
            s = fill("W")
            wide(s, 16, 1, lambda k: FW[0:16, 16:32], lambda k: ZC)
            pe.wait_ge(s.taken, n.now(s.filled))
            psum.align()

            def modulation(j, rows_in_):
                pe.wait_ge(rows_in_, n.add(rows_in_, 16))
                for t in range(NT):
                    for q in range(2):
                        s = fill("N")
                        mm(s.ap[0:P, :], CONDT[:, tile(t)], MODW[0:17, j + q, :], start=True, stop=True)\
                            .then_inc(s.filled, 1)
                transpose_y()

            with pe.Fori(0, BLOCKS) as i, n.loop(i, BLOCKS, loops, "block"):
                modulation(0, modw_in)
                weights(1, 3)
                for h in range(HEADS3):
                    project_wide(wm(1, 0), h)
                    project_wide(wm(1, 1), h)
                for t in range(NT):
                    project_narrow(wm(1, 2), t)
                weights_done()
                all_taken("WN")

                def scores(h, ts):
                    for t in ts:
                        s = fill("W")
                        wide(s, P, 1, lambda k: HT[:, h, tile(t)], lambda k: KT[:, h, :])

                scores(0, range(NT))
                for h in range(HEADS3):
                    probs = G if h % 2 == 0 else PRB
                    if h + 1 < HEADS3:
                        scores(h + 1, range(NT))
                    pe.wait_ge(prob_ready, n.add(prob_ready, NT))
                    for c in range(NT):
                        s = fill("W")
                        for t in range(NT):
                            last = mm(s.ap[0:P, 128 * t:128 * t + P], probs[:, t, tile(c)],
                                      DIAG[:, h % 2, t, :], start=True, stop=True)
                        last.then_inc(s.filled, 1)
                    all_taken("W")
                    s = fill("W")
                    wide(s, 128, NT, lambda k: V[:, k, 128 * h:128 * (h + 1)], lambda k: PT[:, k, :])
                all_taken("W")
                weights(0, 3)
                for t in range(NT):
                    project_narrow(wm(0, 0), t)
                modulation(2, mod2_in)
                for m in range(K4):
                    project_wide(wm(0, 1), m)
                all_taken("W")
                for t in range(NT):
                    s = fill("N")
                    narrow(s, D, [(HT[:, k, tile(t)], wm(0, 2)[:, k, :]) for k in range(K4)])
                weights_done()
                psum.align()

            transpose_y()
            for t in range(NT):
                project_narrow(WG[:, 2], t, 8)
            psum.align()
            with pe.Fori(0, 9) as i, n.loop(i, 9, loops, "expert"):
                for u in range(2):
                    weights(1 - u, 3)
                    ffn_unit(1 - u)
                    weights_done()

        @block.scalar
        def _(act):
            n = Tally("act")
            psum = Slots(slots, n)
            fn = nc.scalar.activation

            def take(kind):
                s, k, _ = psum.next(kind)
                act.wait_ge(s.filled, k)
                return s

            def tile(t):
                return slice(P * t, P * (t + 1))

            act.dma_start(ISRC[:, :], a["src_p"].bitcast(U32)).then_inc(index_in, 16)
            act.dma_start(IDST[:, :], a["dst_p"].bitcast(U32)).then_inc(index_in, 16)
            act.dma_start(FS[:, 7, :], a["edge_weight"]).then_inc(index_in, 16)
            act.dma_start(MODW[:, :, :], bcast(a["arow"], 0, 4 * D, 128).rearrange(
                "p (a b) -> p a b", a=4)).then_inc(arow_in, 16)
            act.dma_start(BR[:, 0, :], bcast(a["arow"], 4 * D, D, 128)).then_inc(arow_in, 16)
            for j in range(3):
                act.dma_start(WG[:, j], a[f"gate_{j}"].rearrange("p (c n) -> p c n", c=K4))\
                   .then_inc(small_in, 16)
            act.dma_start(BI[:, :], bcast(a["biases"], 0, 8, P)).then_inc(small_in, 16)
            act.dma_start(PC[:, :], a["columns"]).then_inc(small_in, 16)
            act.dma_start(FW[:, 0:16], a["f_w1"]).then_inc(small_in, 16)
            act.dma_start(FW[0:16, 16:32], a["f_w2"]).then_inc(small_in, 16)
            act.dma_start(FW[0:16, 32:34], a["f_cols"]).then_inc(small_in, 16)

            def transpose_y():
                for t in range(NT):
                    s = take("T")
                    fn(XT[:, :, tile(t)], s.ap[:, 0:4 * P].rearrange("p (c n) -> p c n", c=K4), ACT.Copy)\
                        .then_inc(s.taken, 1)


            transpose_y()
            for t in range(NT):
                s = take("N")
                fn(HRN[:, t, 0:D], s.ap[0:P, :], ACT.Copy).then_inc(s.taken, 1)
            for t in range(NT):
                s = take("N")
                fn(HE[:, t, :], s.ap[0:P, :], ACT.Copy).then_inc(s.taken, 1)
            s = take("N")
            fn(HRN[:, :, D:ROWLEN], s.ap[0:P, 0:16 * NT].rearrange("p (t h) -> p t h", t=NT), ACT.Copy)\
                .then_inc(s.taken, 1)
            for s in slots["N"]:
                act.wait_ge(s.taken, n.now(s.filled))
            act.dma_start(hr_rows.rearrange("(t p) c -> p t c", p=P), HRN).then_inc(hr_stored, 16)
            psum.skip(N=1)
            s, k, _ = psum.next("N")
            act.wait_ge(s.taken, k)
            fn(FS[:, 8, :], FS[:, 7, :], ACT.Exp, bias=SM[:, 3:4]).then_inc(exp_ready, 1)
            n.add(exp_ready)

            s = take("T")
            fn(KEYT[:, :], s.ap[0:ET, 0:P], ACT.Copy).then_inc(s.taken, 1)
            psum.skip(N=ET // 4)


            for k, (dst, tiles) in enumerate(((CNT, GATHERS_A * TURNS), (G, GATHERS_B * TURNS))):
                with act.Fori(0, tiles // 2) as i, n.loop(i, tiles // 2, loops, "abs"):
                    for b in range(2):
                        act.wait_ge(diff_ready, n.add(diff_ready))
                        fn(PRD[b][:, 0, :], PRD[b][:, 0, :], ACT.Abs).then_inc(abs_ready, 1)
                act.wait_ge(graph_filled, k + 1)
                fn(dst[:, :, 0:MAIN], PS[0:P, 0:5 * BANK].rearrange("p (c n) -> p c n", c=NT), ACT.Copy)
                fn(dst[:, 0:4, MAIN:N], PS[0:P, 5 * BANK:5 * BANK + 4 * TAIL].rearrange(
                    "p (c n) -> p c n", c=4), ACT.Copy)
                fn(dst[:, 4, MAIN:N], tail_of(4), ACT.Copy).then_inc(graph_taken, 1)
            act.wait_ge(graph_filled, 3)
            fn(EA1[:, :], PS[:, 2 * BANK:2 * BANK + N], ACT.Copy)
            fn(EA2[0:65, :], PS[0:65, 4 * BANK:4 * BANK + N], ACT.Copy).then_inc(graph_taken, 1)

            done = [0]

            def quantized(u):
                def magnitudes(k):
                    j, c, width = groups[k]
                    if done[0] + k >= 2:
                        act.wait_ge(quant_ready, done[0] + k - 1)
                    w = wm((u + 1) % 2, j)[:, c, 0:width]
                    fn(AW[k % 2][:, 0:width], w, ACT.Abs).then_inc(absw_ready, 1)
                    fn(SGN[k % 2][:, 0:width], w, ACT.Sign).then_inc(scalar_step, 1)

                groups = groups_of(u)
                act.wait_ge(loaded[(u + 1) % 2], n.now(loaded[(u + 1) % 2]) + 48)
                magnitudes(0)
                for k, (j, c, width) in enumerate(groups):
                    if k + 1 < len(groups):
                        magnitudes(k + 1)
                    s = take("T")
                    fn(SCL[k % 2][:, 0:width], s.ap[:, 0:width], ACT.Copy, bias=1e-5, scale=1.0 / 128)\
                        .then_inc(s.taken, 1)
                    if k == len(groups) - 1:
                        done[0] += len(groups)
                    yield

            n.add(loaded[0], 32)

            def exp_scores(k):
                t, h = divmod(k, HEADS0)
                if h == 0:
                    act.wait_ge(negmax_ready, n.add(negmax_ready))
                pairs = TSC[t % 2].rearrange("p (d h) -> p d h", h=HEADS0)
                fn(SP0[k % 4], pairs[:, :, h], ACT.Exp, bias=HM[:, t % 2, 1, h:h + 1])\
                    .then_inc(exp_ready, 1)
                n.add(exp_ready)

            exp_scores(0)
            exp_scores(1)
            ahead = quantized(0)
            for k in range(NT * HEADS0):
                if k + 2 < NT * HEADS0:
                    exp_scores(k + 2)
                s = take("W")
                fn(PTS[k % 2], s.ap[0:P, 0:640].rearrange("p (c n) -> p c n", c=NT)[:, :, 0:P], ACT.Copy)\
                    .then_inc(s.taken, 1)
                if k % 3 == 2:
                    next(ahead, None)
            for _ in ahead:
                pass
            psum.skip(N=NT)
            for s in slots["N"]:
                act.wait_ge(s.filled, n.now(s.filled))
            psum.align()

            def ffn_unit(chunks=K4, scaled=False, between=lambda: None):
                for m in range(chunks):
                    s = take("W")
                    fn(SG[m % 2], s.ap[:, 0:N], ACT.Silu).then_inc(s.taken, 1)
                    between()
                    psum.skip(W=2 if scaled else 1)
                    between()
                    between()
                psum.skip(N=NT)

            transpose_y()
            for u in range(3):
                n.add(loaded[(u + 1) % 2], 48)
                ahead = quantized(u + 1) if u < 2 else iter(())
                ffn_unit(WIDTHS[u] // 128, between=lambda: next(ahead, None))

            transpose_y()
            psum.skip(N=NT)
            for c in range(NT):
                s = take("W")
                fn(PT[:, c, :].rearrange("p (c n) -> p c n", c=NT),
                   s.ap[0:P, 0:640].rearrange("p (c n) -> p c n", c=NT)[:, :, 0:P], ACT.Copy)\
                    .then_inc(s.taken, 1)
            for f in range(4):
                s = take("W")
                fn(HT[:, f, :], s.ap[:, 0:N], ACT.Copy).then_inc(s.taken, 1)
            psum.skip(N=NT)
            for t in range(NT):
                s = take("T")
                fn(HBT[:, tile(t)], s.ap[:, 0:P], ACT.Copy).then_inc(s.taken, 1)
            psum.skip(N=NT)

            def router_exp(cols, scale=1.0):
                act.wait_ge(negmax_ready, n.add(negmax_ready))
                fn(cols, cols, ACT.Exp, scale=scale).then_inc(exp_ready, 1)

            transpose_y()
            psum.skip(N=NT)
            router_exp(TW[:, :, 0])
            for t in range(NT):
                s = take("T")
                fn(CT8[:, tile(t)], s.ap[0:8, 0:P], ACT.Copy).then_inc(s.taken, 1)
            ffn_unit(scaled=True)

            for l in range(3):
                for f in range(K4):
                    s = take("W")
                    fn(HT[:, f, :], s.ap[:, 0:N], ACT.Copy).then_inc(s.taken, 1)
                psum.skip(N=NT)

            transpose_y()
            psum.skip(N=NT)
            router_exp(TW[:, :, 0])
            for t in range(NT):
                s, k, _ = psum.next("N")
                for i in range(2):
                    if i == 0:
                        act.wait_ge(negmax_ready, n.add(negmax_ready))
                    else:
                        act.wait_ge(s.taken, k)
                    fn(GE[t % 2][i], GE[t % 2][i], ACT.Gelu).then_inc(exp_ready, 1)
            for t in range(NT):
                s = take("T")
                fn(HT[:, :, tile(t)], s.ap[:, 0:4 * P].rearrange("p (c n) -> p c n", c=K4), ACT.Copy)\
                    .then_inc(s.taken, 1)
            psum.skip(N=NT)

            act.wait_ge(emb_ready, 1)
            fn(EMR, EMR, ACT.Sin).then_inc(sin_ready, 1)
            s = take("W")
            act.wait_ge(small_in, 16 * SMALLS)
            fn(ZC, s.ap[0:16, 0:N], ACT.Silu, bias=FW[0:16, 32:33]).then_inc(s.taken, 1)
            s = take("W")
            act.wait_ge(emb_ready, 2)
            fn(CONDT[0:16, :], s.ap[0:16, 0:N], ACT.Identity, bias=FW[0:16, 33:34]).then_inc(s.taken, 1)
            psum.align()

            with act.Fori(0, BLOCKS) as i, n.loop(i, BLOCKS, loops, "block"):
                psum.skip(N=2 * NT)
                transpose_y()
                for h in range(HEADS3):
                    psum.skip(W=1)
                    s = take("W")
                    fn(KT[:, h, :], s.ap[:, 0:N], ACT.Identity,
                       bias=PC[:, bass.ds(i * 12 + 4 + h, 1)]).then_inc(s.taken, 1)
                psum.skip(N=NT)

                def exp_head(h):
                    probs = G if h % 2 == 0 else PRB
                    for t in range(NT):
                        psum.skip(W=1)
                        act.wait_ge(negmax_ready, n.add(negmax_ready))
                        fn(probs[:, t, :], probs[:, t, :], ACT.Exp, bias=DEN[:, h % 2, 1, t:t + 1])\
                            .then_inc(exp_ready, 1)

                exp_head(0)
                for h in range(HEADS3):
                    if h + 1 < HEADS3:
                        exp_head(h + 1)
                    for c in range(NT):
                        s = take("W")
                        fn(PT[:, c, :].rearrange("p (c n) -> p c n", c=NT),
                           s.ap[0:P, 0:640].rearrange("p (c n) -> p c n", c=NT)[:, :, 0:P], ACT.Copy)\
                            .then_inc(s.taken, 1)
                    s = take("W")
                    fn(XT[:, h, :], s.ap[:, 0:N], ACT.Copy).then_inc(s.taken, 1)
                psum.skip(N=NT)
                psum.skip(N=2 * NT)
                transpose_y()
                for m in range(K4):
                    s = take("W")
                    fn(HT[:, m, :], s.ap[:, 0:N], ACT.Relu,
                       bias=PC[:, bass.ds(i * 12 + 8 + m, 1)]).then_inc(s.taken, 1)
                psum.skip(N=NT)
                psum.align()

            transpose_y()
            psum.skip(N=NT)
            router_exp(TW[:, :, 0:2], scale=-1.0)
            psum.align()
            with act.Fori(0, 9) as i, n.loop(i, 9, loops, "expert"):
                for u in range(2):
                    ffn_unit()

        @block.gpsimd
        def _(pool):
            n = Tally("pool")
            g = nc.gpsimd
            g.memset(ONES[:, :], 1.0).then_inc(start_done, 1)
            g.memset(TWOS[:, :], 2.0).then_inc(start_done, 1)
            g.memset(HALF[:, :], -0.5).then_inc(start_done, 1)
            g.memset(COMB[:, :, :], 1.0).then_inc(start_done, 1)
            g.memset(EA2[:, :], 0.0).then_inc(start_done, 1)
            g.iota(IOTA[:, :], pattern=[[1, N]], base=0, channel_multiplier=0).then_inc(start_done, 1)
            g.memset(ZB, 0.0).then_inc(pool_step, 1)
            g.memset(TS[:, :, :], 0.0).then_inc(score_taken, 1)
            n.add(score_taken)
            pool.wait_ge(pool_step, n.add(pool_step))
            g.memset(ZROW, NEG).then_inc(clear_row_ready, 1)

            def inverse_roots(tiles=range(NT)):
                for t in tiles:
                    pool.wait_ge(var_ready, n.add(var_ready))
                    g.tensor_tensor(RSTD[:, t:t + 1], VE[:, t:t + 1], HALF[:, :], ALU.pow)\
                        .then_inc(rstd_ready, 1)

            inverse_roots()
            pool.wait_ge(index_in, 48)
            pool.wait_ge(hr_stored, 16)

            def gather(m, b):
                g.tensor_copy(IDS[:, 2 * b:2 * b + 1], ISRC[:, bass.ds(m, 1)]).then_inc(pool_step, 1)
                g.tensor_copy(IDS[:, 2 * b + 1:2 * b + 2], IDST[:, bass.ds(m, 1)]).then_inc(pool_step, 1)
                pool.wait_ge(pool_step, n.add(pool_step, 2))
                g.tensor_tensor(SM[0:1, 10:11], HALF[0:1, :], HALF[0:1, :], ALU.add)
                for k, dst in enumerate((HS[b], HD[b])):
                    g.indirect_dma_start(
                        out=dst, out_offset=None, in_=hr_rows,
                        in_offset=bass.IndirectOffsetOnAxis(ap=IDS[:, 2 * b + k:2 * b + k + 1], axis=0))\
                     .then_inc(gathered[b], 16)

            def scatter(m, b, first=False):
                pool.wait_ge(score_ready, n.add(score_ready))
                if not first:
                    pool.wait_ge(scattered, n.now(scattered))
                n.add(scattered, 16)
                g.tensor_copy(IDS[:, 2 * AHEAD + b:2 * AHEAD + b + 1], SIDX[:, bass.ds(m, 1)]).then_inc(score_taken, 1)
                pool.wait_ge(score_taken, n.add(score_taken))
                g.tensor_tensor(SM[0:1, 10:11], HALF[0:1, :], HALF[0:1, :], ALU.add)
                g.indirect_dma_start(
                    out=pair_scores, out_offset=bass.IndirectOffsetOnAxis(ap=IDS[:, 2 * AHEAD + b:2 * AHEAD + b + 1], axis=0),
                    in_=TS[:, b, :], in_offset=None).then_inc(scattered, 16)

            for b in range(AHEAD):
                gather(b, b)
            pool.wait_ge(cleared, 16 * 2 * NT)
            pool.wait_ge(sidx_ready, 1)
            for b in range(AHEAD):
                scatter(b, b, first=(b == 0))
                gather(AHEAD + b, b)
            with pool.Fori(1, ET // AHEAD - 1) as i, n.loop(i - 1, ET // AHEAD - 2, loops, "gather"):
                for b in range(AHEAD):
                    scatter(i * AHEAD + b, b)
                    gather(i * AHEAD + b + AHEAD, b)
            for b in range(AHEAD):
                scatter(ET - AHEAD + b, b)
            def signed(u):
                for k, (j, c, width) in enumerate(groups_of(u)):
                    w = wm((u + 1) % 2, j)[:, c, 0:width]
                    pool.wait_ge(kept_ready, n.add(kept_ready))
                    g.tensor_tensor(w, SCL[k % 2][:, 0:width], SGN[k % 2][:, 0:width], ALU.mult)\
                     .then_inc(quant_ready, 1)
                    yield

            ahead = signed(0)
            for k in range(NT * HEADS0):
                t, h = divmod(k, HEADS0)
                if h == 2 and t:
                    inverse_roots([t - 1])
                if k % 3 == 1 and k >= 4:
                    next(ahead, None)
            for _ in ahead:
                pass
            inverse_roots([NT - 1])
            for u in (1, 2):
                for _ in signed(u):
                    pass
            inverse_roots()
            inverse_roots()
            inverse_roots()
            inverse_roots()
            for l in range(3):
                inverse_roots()
            inverse_roots()
            inverse_roots()
            inverse_roots()
            with pool.Fori(0, BLOCKS) as i, n.loop(i, BLOCKS, loops, "block"):
                inverse_roots()
                inverse_roots()
            inverse_roots()

        @block.vector
        def _(dve):
            n = Tally("dve")
            psum = Slots(slots, n)
            v = nc.vector

            def take(kind):
                s, k, _ = psum.next(kind)
                dve.wait_ge(s.filled, k)
                return s

            def step(ins):
                ins.then_inc(vector_step, 1)
                dve.wait_ge(vector_step, n.add(vector_step))

            def signal(ins, sem):
                ins.then_inc(sem, 1)
                dve.wait_ge(sem, n.add(sem))

            def carry():
                if n.turn is not None:
                    v.tensor_copy(SM[0:1, 5:6], ONES[0:1, 0:1])

            def tile(t):
                return slice(P * t, P * (t + 1))

            def stats(t, src):
                step(v.bn_stats(ST[:, t, :], src))
                carry()
                step(v.bn_aggr(MV[:, t, :], ST[:, t, :]))
                v.tensor_scalar(VE[:, t:t + 1], MV[:, t, 1:2], 1e-5, None, ALU.add).then_inc(var_ready, 1)

            def norm(t, dst, src):
                dve.wait_ge(rstd_ready, n.add(rstd_ready))
                return v.tensor_scalar(dst, src, MV[:, t, 0:1], RSTD[:, t:t + 1], ALU.subtract, ALU.mult)

            def norm_y(src=X):
                n.add(y_ready, NT)
                for t in range(NT):
                    norm(t, Y[0:P, t, :], src[0:P, t, :]).then_inc(y_ready, 1)

            def add_to_stream(t, s, scalar=None, dst=X):
                if scalar is None:
                    v.tensor_tensor(dst[0:P, t, :], s.ap[0:P, :], dst[0:P, t, :], ALU.add)\
                     .then_inc(s.taken, 1)
                else:
                    v.scalar_tensor_tensor(dst[0:P, t, :], s.ap[0:P, :], scalar, dst[0:P, t, :],
                                           ALU.mult, ALU.add).then_inc(s.taken, 1)
                dve.wait_ge(s.taken, n.now(s.filled))

            v.memset(S2[0][:, :, 64:65], 1.0)
            v.memset(S2[1][:, :, 64:65], 1.0).then_inc(edge_read, 4)
            dve.wait_ge(edge_read, n.add(edge_read, 4))


            dve.wait_ge(x_in, 16)
            for t in range(NT):
                stats(t, X[0:P, t, :])
            norm_y()
            psum.skip(T=NT, N=NT)
            dve.wait_ge(arow_in, 32)
            dve.wait_ge(loaded[0], 32)
            for k, (w, r) in enumerate(((0, MODW[:, 0, :]), (1, BR[:, 0, :]), (0, MODW[:, 1, :]))):
                step(v.tensor_tensor(WTMP, wm(0, w), r.unsqueeze(1).broadcast_to([128, K4, D]),
                                     ALU.mult))
                step(v.tensor_reduce(UVT[:, k, :], WTMP.rearrange("p c (h d) -> p (c h) d", d=DH0),
                                     AX.X, ALU.add))
            part = [UVT[:, k, :].rearrange("p (c h) -> p c h", c=K4) for k in range(3)]
            step(v.tensor_tensor(UV[:, :, 0:8], part[0], part[1], ALU.subtract))
            v.tensor_tensor(UV[:, :, 8:16], part[2], part[1], ALU.add).then_inc(uv_ready, 1)
            dve.wait_ge(uv_ready, 1)
            psum.skip(N=NT + 1)
            dve.wait_ge(index_in, 48)
            step(v.tensor_copy(FS[:, 0, :], ISRC[:, :]))
            step(v.tensor_copy(FS[:, 1, :], IDST[:, :]))
            v.scalar_tensor_tensor(FS[:, 2, :], FS[:, 0, :], float(N), FS[:, 1, :], ALU.mult, ALU.add)\
             .then_inc(keys_ready, 1)
            dve.wait_ge(keys_ready, 1)
            v.reduce_max(SM[:, 0:1], FS[:, 7, :], AX.X).then_inc(layer_ready, 1)
            s = take("N")
            v.reduce_max(SM[0:1, 2:3], s.ap[0:1, 0:P], AX.X).then_inc(s.taken, 1)
            dve.wait_ge(s.taken, n.now(s.filled))
            v.tensor_scalar(SM[0:1, 1:2], SM[0:1, 2:3], 0.0, None, ALU.max).then_inc(layer_ready, 1)
            s = take("N")
            v.tensor_scalar(SM[:, 3:4], s.ap[0:P, 0:1], -1.0, None, ALU.mult).then_inc(s.taken, 1)
            dve.wait_ge(exp_ready, n.add(exp_ready))
            for r in range(3):
                step(v.tensor_copy(EB[:, :], FS[:, 8, :]))
                step(v.tensor_copy(FS[:, 4 + r, :], EB[:, :]))
                if r < 2:
                    step(v.tensor_tensor(FS[:, 8, :], FS[:, 8, :], FS[:, 4 + r, :], ALU.subtract))

            dve.wait_ge(consts_in, 16)
            psum.skip(T=1)
            for q in range(4):
                for m in range(20):
                    if m % 4 == 0:
                        s = take("N")
                    last = v.scalar_tensor_tensor(
                        KROW[:, m, :], s.ap[0:P, P * (m % 4):P * (m % 4 + 1)],
                        FS[:, 2, 20 * q + m:20 * q + m + 1], CS[0:P, C_TRI:C_TRI + P],
                        ALU.is_equal, ALU.mult)
                    if m % 4 == 3:
                        last.then_inc(s.taken, 1)
                dve.wait_ge(s.taken, n.now(s.filled))
                step(v.tensor_reduce(FS[:, 3, 20 * q:20 * (q + 1)], KROW, AX.X, ALU.max))
            step(v.tensor_scalar(FS[:, 8, :], FS[:, 2, :], -1.0, CS[0:P, C_DUMP:C_DUMP + 1],
                                 ALU.mult, ALU.add))
            step(v.tensor_tensor(FS[:, 8, :], FS[:, 8, :], FS[:, 3, :], ALU.mult))
            step(v.tensor_tensor(FS[:, 8, :], FS[:, 8, :], FS[:, 2, :], ALU.add))
            v.tensor_copy(SIDX[:, :], FS[:, 8, :]).then_inc(sidx_ready, 1)


            def onehot(dst, m, row, scale=None):
                if scale is None:
                    return v.tensor_scalar(dst, IOTA[:, :], FS[:, row, bass.ds(m, 1)], None, ALU.is_equal)
                return v.tensor_scalar(dst, IOTA[:, :], FS[:, row, bass.ds(m, 1)],
                                       FS[:, scale, bass.ds(m, 1)], ALU.is_equal, ALU.mult)

            def differences(m):
                b, z = m % AHEAD, PRD[m % 2]
                dve.wait_ge(gathered[b], n.add(gathered[b], 32))
                v.tensor_tensor(z[:, 1, :], HD[b][:, 0:D], HS[b][:, 0:D], ALU.mult)
                v.tensor_tensor(z[:, 0, :], HD[b][:, 0:D], HS[b][:, 0:D], ALU.subtract)\
                 .then_inc(diff_ready, 1)

            def edge_scores(m):
                b, z = m % AHEAD, PRD[m % 2]
                dve.wait_ge(abs_ready, n.add(abs_ready))
                step(v.tensor_tensor(z, z, MODW[0:P, 2:4, :], ALU.mult))
                step(v.tensor_reduce(SUMS[:, :, :], z.rearrange("p s (h d) -> p (s h) d", d=DH0).rearrange(
                    "p (s h) d -> p s h d", s=2), AX.X, ALU.add))
                x, y = SUMS[:, 0, :], SUMS[:, 1, :]
                step(v.tensor_tensor(x, x, HS[b][:, D:D + HEADS0], ALU.add))
                step(v.tensor_tensor(y, y, HD[b][:, D + HEADS0:ROWLEN], ALU.add))
                step(v.tensor_tensor(x, x, y, ALU.add))
                dve.wait_ge(score_taken, n.add(score_taken))
                v.scalar_tensor_tensor(TS[:, b, :], x, 0.2, x, ALU.mult, ALU.max)\
                 .then_inc(score_ready, 1)

            dve.wait_ge(start_done, 6)
            for name, parts, scores in (("count", 0, GATHERS_A), ("weight", 3, GATHERS_B)):
                with dve.Fori(0, TURNS) as i, n.loop(i, TURNS, loops, name):
                    done = 0
                    for k in range(STEP):
                        dve.wait_ge(onehot_used, n.add(onehot_used))
                        onehot(OS[k % 2], i * STEP + k, 0)
                        if parts:
                            for r in range(parts):
                                last = onehot(OD[k % 2][r], i * STEP + k, 1, 4 + r)
                        else:
                            last = onehot(OD[k % 2][0], i * STEP + k, 1)
                        last.then_inc(onehot_ready, 1)
                        while done * STEP < (k + 1) * scores and done < scores:
                            differences(done)
                            if done:
                                edge_scores(done - 1)
                            done += 1
                    edge_scores(done - 1)
                if name == "count":
                    dve.wait_ge(graph_taken, 1)
                    step(v.tensor_scalar(MASK[:, :, :], CNT[:, :, :], 0.5, NEG, ALU.is_lt, ALU.mult))
            with dve.Fori(0, TURNS) as i, n.loop(i, TURNS, loops, "edge"):
                for q in range(4):
                    b = q % 2
                    dve.wait_ge(edge_in[q], n.add(edge_in[q], 16))
                    dve.wait_ge(onehot_used, n.now(onehot_used))
                    step(v.tensor_copy(S1[b][:, :, 0:64], ER[q]))
                    signal(v.tensor_tensor(ERR, ER[q], S1[b][:, :, 0:64], ALU.subtract), edge_read)
                    step(v.tensor_copy(S1[b][:, :, 64:128], ERR))
                    step(v.tensor_tensor(ERR, ERR, S1[b][:, :, 64:128], ALU.subtract))
                    step(v.tensor_copy(S2[b][:, :, 0:64], ERR))
                    for k in range(4):
                        dve.wait_ge(onehot_used, n.add(onehot_used))
                        onehot(OD[k % 2][0], i * STEP + 4 * q + k, 1).then_inc(onehot_ready, 1)

            def quantized(u):
                for k, (j, c, width) in enumerate(groups_of(u)):
                    s = psum.next("T")
                    dve.wait_ge(s[0].taken, s[1])
                    w, z = AW[k % 2][:, 0:width], SCL[k % 2][:, 0:width]
                    step(v.scalar_tensor_tensor(w, w, 2.0, z, ALU.mult, ALU.is_gt))
                    v.tensor_tensor(z, z, w, ALU.mult).then_inc(kept_ready, 1)
                    yield

            def maxima_of(t):
                dve.wait_ge(pairs_in[t % 2], 16 * (t // 2 + 1))
                step(v.tensor_reduce(HM[:, t % 2, 0, :], TSC[t % 2].rearrange("p (d h) -> p h d", h=HEADS0),
                                     AX.X, ALU.max))
                v.tensor_scalar(HM[:, t % 2, 1, :], HM[:, t % 2, 0, :], -1.0, None, ALU.mult)\
                 .then_inc(negmax_ready, 1)

            def add_heads(t):
                den = HM[:, t % 2, 3, :]
                dve.wait_ge(prob_ready, HEADS0 * (t + 1))
                step(v.tensor_scalar(den, HM[:, t % 2, 2, :], 1e-16, None, ALU.add))
                step(v.reciprocal(den, den))
                s, y = take("N"), Y[0:P, t, :]
                v.tensor_tensor(y.rearrange("p (h d) -> p h d", d=DH0),
                                s.ap[0:P, :].rearrange("p (h d) -> p h d", d=DH0),
                                den.unsqueeze(2).broadcast_to([P, HEADS0, DH0]), ALU.mult)\
                 .then_inc(s.taken, 1)
                dve.wait_ge(s.taken, n.now(s.filled))
                step(v.tensor_tensor(X[0:P, t, :], X[0:P, t, :], y, ALU.add))
                stats(t, X[0:P, t, :])

            maxima_of(0)
            psum.skip(W=NT * HEADS0)
            ahead = quantized(0)
            for k in range(NT * HEADS0):
                t, h = divmod(k, HEADS0)
                z = SP0[k % 4]
                dve.wait_ge(exp_ready, n.add(exp_ready))
                v.tensor_tensor_reduce(out=z, in0=z, in1=CNT[:, t, :], scale=1.0, scalar=0.0,
                                       op0=ALU.mult, op1=ALU.add, accum_out=HM[:, t % 2, 2, h:h + 1])\
                 .then_inc(prob_ready, 1)
                if h == 3 and t + 1 < NT:
                    maxima_of(t + 1)
                if h == 2 and t:
                    add_heads(t - 1)
                if k % 3 == 1 and k >= 4:
                    next(ahead, None)
            for _ in ahead:
                pass
            add_heads(NT - 1)
            psum.align()

            def ffn_unit(chunks=K4, scaled=False, scalar=None, with_stats=True, between=lambda: None):
                for m in range(chunks):
                    s, k, _ = psum.next("W")
                    between()
                    h = SG[m % 2]
                    if scaled:
                        c = take("W")
                        dve.wait_ge(s.taken, k)
                        v.tensor_tensor(h, h, c.ap[:, 0:N], ALU.mult).then_inc(c.taken, 1)
                        dve.wait_ge(c.taken, n.now(c.filled))
                    b = take("W")
                    dve.wait_ge(s.taken, k)
                    v.tensor_tensor(HT[:, m, :], h, b.ap[:, 0:N], ALU.mult).then_inc(b.taken, 1)
                    between()
                    between()
                for t in range(NT):
                    add_to_stream(t, take("N"), None if scalar is None else scalar(t))
                    if with_stats:
                        stats(t, X[0:P, t, :])

            norm_y()
            psum.skip(T=NT)
            for u in range(3):
                ahead = quantized(u + 1) if u < 2 else iter(())
                ffn_unit(WIDTHS[u] // 128, with_stats=(u == 2), between=lambda: next(ahead, None))

            norm_y()
            psum.skip(T=NT)
            step(v.tensor_reduce(TW[:, :, 0], G[:, :, :], AX.X, ALU.add))
            step(v.tensor_scalar(TW[:, :, 1], TW[:, :, 0], 1e-6, None, ALU.add))
            step(v.reciprocal(TW[:, :, 1], TW[:, :, 1]))
            step(v.tensor_scalar(TW[:, :, 2], TW[:, :, 0], 0.0, None, ALU.is_gt))
            for t in range(NT):
                last = v.tensor_scalar(G[:, t, :], G[:, t, :], TW[:, t, 1:2], None, ALU.mult)
            last.then_inc(layer_ready, 1)
            n.add(layer_ready)
            dve.wait_ge(rows_in, 16)
            for t in range(NT):
                s = take("N")
                v.tensor_tensor(MF[:, t, :], s.ap[0:P, 0:256], ROWS[:, R_BM:R_BM + 256], ALU.add)\
                 .then_inc(s.taken, 1)
            psum.skip(W=NT + 4)
            for t in range(NT):
                s = take("N")
                v.tensor_tensor(HB[:, t, :], s.ap[0:P, 0:128], ROWS[:, R_B1:R_B1 + 128], ALU.add)\
                 .then_inc(s.taken, 1)
                dve.wait_ge(s.taken, n.now(s.filled))
                stats(t, HB[:, t, :])
            for t in range(NT):
                step(norm(t, HB[:, t, :], HB[:, t, :]))
                step(v.tensor_tensor(HB[:, t, :], HB[:, t, :], ROWS[:, R_G1:R_G1 + 128], ALU.mult))
                step(v.tensor_tensor(HB[:, t, :], HB[:, t, :], ROWS[:, R_BE1:R_BE1 + 128], ALU.add))
                v.tensor_scalar(HB[:, t, :], HB[:, t, :], 0.0, None, ALU.max).then_inc(layer_ready, 1)
            psum.skip(T=NT)
            for t in range(NT):
                s = take("N")
                z = ROW[t % 2]
                v.tensor_tensor(z, s.ap[0:P, :], ROWS[:, R_B2:R_B2 + D], ALU.add).then_inc(s.taken, 1)
                dve.wait_ge(s.taken, n.now(s.filled))
                step(v.tensor_scalar(z, z, 0.0, TW[:, t, 2:3], ALU.max, ALU.mult))
                step(v.tensor_tensor(X[0:P, t, :], X[0:P, t, :], z, ALU.add))
                stats(t, X[0:P, t, :])

            def best_two(values, t):
                step(v.max(M8[:, t, :], values))
                step(v.max_index(I8[:, t, :], M8[:, t, :], values))

            def shares(t, first, second):
                step(v.tensor_copy(TW[:, t, 3:5], I8[:, t, 0:2]))
                step(v.tensor_scalar(M8[:, t, :], CS[0:P, C_I8:C_I8 + 8], TW[:, t, 3:4], first,
                                     ALU.is_equal, ALU.mult))
                step(v.tensor_scalar(LG[:, t, :], CS[0:P, C_I8:C_I8 + 8], TW[:, t, 4:5], second,
                                     ALU.is_equal, ALU.mult))
                return v.tensor_tensor(COMB[:, t, 0:8], M8[:, t, :], LG[:, t, :], ALU.add)

            def logits():
                for t in range(NT):
                    s = take("N")
                    v.tensor_copy(LG[:, t, :], s.ap[0:P, 0:8]).then_inc(s.taken, 1)
                    dve.wait_ge(s.taken, n.now(s.filled))

            def softmax_of_two():
                v.tensor_tensor(TW[:, :, 0], M8[:, :, 1], M8[:, :, 0], ALU.subtract).then_inc(negmax_ready, 1)
                dve.wait_ge(exp_ready, n.add(exp_ready))
                step(v.tensor_scalar(TW[:, :, 1], TW[:, :, 0], 1.0, None, ALU.add))
                step(v.reciprocal(TW[:, :, 1], TW[:, :, 1]))
                step(v.tensor_tensor(TW[:, :, 2], TW[:, :, 0], TW[:, :, 1], ALU.mult))

            norm_y()
            psum.skip(T=NT)
            logits()
            for t in range(NT):
                best_two(LG[:, t, :], t)
            softmax_of_two()
            for t in range(NT):
                shares(t, TW[:, t, 1:2], TW[:, t, 2:3]).then_inc(layer_ready, 1)
            psum.skip(T=NT)
            ffn_unit(scaled=True)

            for t in range(NT):
                last = norm(t, XL[:, t, :], X[0:P, t, :])
            last.then_inc(layer_ready, 1)
            n.add(layer_ready)
            for l in range(3):
                psum.skip(W=K4)
                for t in range(NT):
                    add_to_stream(t, take("N"), dst=XL)
                    stats(t, XL[:, t, :])
                for t in range(NT):
                    z = XL[:, t, :]
                    step(norm(t, z, z))
                    step(v.tensor_tensor(z, z, ROWS[:, R_G2 + D * l:R_G2 + D * (l + 1)], ALU.mult))
                    step(v.tensor_tensor(z, z, ROWS[:, R_BE2 + D * l:R_BE2 + D * (l + 1)], ALU.add))
                    last = v.tensor_scalar(z, z, 0.0, None, ALU.max)
                    if t < NT - 1 or l == 2:
                        step(last)
                if l < 2:
                    last.then_inc(layer_ready, 1)
            for t in range(NT):
                add = v.tensor_tensor(X[0:P, t, :], X[0:P, t, :], XL[:, t, :], ALU.add)
                if t == 0:
                    signal(add, attn_rows_free)
                elif t == 1:
                    signal(add, mlp_rows_free)
                else:
                    step(add)
                stats(t, X[0:P, t, :])

            norm_y()
            psum.skip(T=NT)
            logits()
            for t in range(NT):
                step(v.max(M8[:, t, :], LG[:, t, :]))
            softmax_of_two()

            def hidden_inputs(t):
                s = take("N")
                for i in range(2):
                    last = v.scalar_tensor_tensor(GE[t % 2][i], s.ap[0:P, :], TW[:, t, 1 + i:2 + i],
                                                  ROWS[:, R_FB1:R_FB1 + D], ALU.mult, ALU.add)
                    if i == 0:
                        last.then_inc(negmax_ready, 1)
                last.then_inc(s.taken, 1)

            for t in range(NT + 1):
                if t < NT:
                    if t >= 2:
                        dve.wait_ge(y_ready, n.now(y_ready))
                    hidden_inputs(t)
                if t:
                    dve.wait_ge(exp_ready, n.add(exp_ready, 2))
                    n.add(y_ready)
                    v.tensor_tensor(Y[0:P, t - 1, :], GE[(t - 1) % 2][0], GE[(t - 1) % 2][1], ALU.add)\
                     .then_inc(y_ready, 1)
            psum.skip(T=NT)
            for t in range(NT):
                add_to_stream(t, take("N"))
                stats(t, X[0:P, t, :])

            dve.wait_ge(noise_in, 16)
            col = lambda c: CS[0:64, c:c + 1]
            step(v.memset(CONDT, 1.0))
            step(v.tensor_scalar(EMN, EMN, col(C_FREQ), None, ALU.mult))
            step(v.tensor_scalar(EMB, EMN, 1.0 / (2.0 * np.pi), col(C_FRAC), ALU.mult, ALU.add))
            step(v.tensor_scalar(EMB, EMB, MAGIC, -MAGIC, ALU.add, ALU.add))
            for c in TWO_PI:
                step(v.scalar_tensor_tensor(EMN, EMB, -c, EMN, ALU.mult, ALU.add))
            step(v.tensor_scalar(EMN, EMN, col(C_SHIFT), 3.1415925, ALU.add, ALU.min))
            v.tensor_scalar(EMR, EMN, -3.1415925, None, ALU.max).then_inc(emb_ready, 2)
            for t in range(NT):
                step(norm(t, XL[:, t, :], X[0:P, t, :]))
                stats(t, XL[:, t, :])
            psum.skip(W=2)
            psum.align()

            def modulated_norm(br):
                for t in range(NT):
                    y = Y[0:P, t, :]
                    step(norm(t, y, XL[:, t, :]))
                    s = take("N")
                    v.scalar_tensor_tensor(y, s.ap[0:P, :], 1.0, y, ALU.add, ALU.mult).then_inc(s.taken, 1)
                    dve.wait_ge(s.taken, n.now(s.filled))
                    s = take("N")
                    step_y = v.tensor_tensor(y, y, s.ap[0:P, :], ALU.add)
                    step_y.then_inc(s.taken, 1)
                    dve.wait_ge(s.taken, n.now(s.filled))
                    v.tensor_copy(SM[:, 4:5], SM[:, 3:4]).then_inc(y_ready, 1)
                    n.add(y_ready)
                psum.skip(T=NT)

            with dve.Fori(0, BLOCKS) as i, n.loop(i, BLOCKS, loops, "block"):
                modulated_norm(0)
                for h in range(HEADS3):
                    s = take("W")
                    v.tensor_scalar(HT[:, h, :], s.ap[:, 0:N], PC[:, bass.ds(i * 12 + h, 1)],
                                    128.0 ** -0.5, ALU.add, ALU.mult).then_inc(s.taken, 1)
                    psum.skip(W=1)
                dve.wait_ge(br_in, n.add(br_in, 16))
                for t in range(NT):
                    s = take("N")
                    v.tensor_tensor(V[:, t, :], s.ap[0:P, :], BR[0:P, 0, :], ALU.add).then_inc(s.taken, 1)

                def maxima(h):
                    probs = G if h % 2 == 0 else PRB
                    for t in range(NT):
                        s = take("W")
                        carry()
                        v.tensor_tensor_reduce(out=probs[:, t, :], in0=s.ap[0:P, 0:N], in1=MASK[:, t, :],
                                               scale=1.0, scalar=-3.0e38, op0=ALU.add, op1=ALU.max,
                                               accum_out=DEN[:, h % 2, 0, t:t + 1]).then_inc(s.taken, 1)
                        dve.wait_ge(s.taken, n.now(s.filled))
                        v.tensor_scalar(DEN[:, h % 2, 1, t:t + 1], DEN[:, h % 2, 0, t:t + 1], -1.0, None,
                                        ALU.mult).then_inc(negmax_ready, 1)

                maxima(0)
                for h in range(HEADS3):
                    probs = G if h % 2 == 0 else PRB
                    for t in range(NT):
                        dve.wait_ge(exp_ready, n.add(exp_ready))
                        step(v.tensor_tensor_reduce(
                            out=probs[:, t, :], in0=probs[:, t, :], in1=CNT[:, t, :], scale=1.0,
                            scalar=0.0, op0=ALU.mult, op1=ALU.add, accum_out=DEN[:, h % 2, 2, t:t + 1]))
                    step(v.tensor_scalar(DEN[:, h % 2, 3, :], DEN[:, h % 2, 2, :], 1e-30, None, ALU.max))
                    step(v.reciprocal(DEN[:, h % 2, 3, :], DEN[:, h % 2, 3, :]))
                    for t in range(NT):
                        v.tensor_scalar(DIAG[:, h % 2, t, :], ID[0:P, 0:P], DEN[:, h % 2, 3, t:t + 1],
                                        None, ALU.mult).then_inc(prob_ready, 1)
                    if h + 1 < HEADS3:
                        maxima(h + 1)
                    psum.skip(W=NT + 1)
                for t in range(NT):
                    add_to_stream(t, take("N"), dst=XL)
                    last = v.tensor_tensor(XL[:, t, :], XL[:, t, :], BR[0:P, 1, :], ALU.add)
                    if t < NT - 1:
                        step(last)
                    else:
                        signal(last, attn_rows_free)
                    stats(t, XL[:, t, :])
                modulated_norm(2)
                psum.skip(W=K4)
                dve.wait_ge(br2_in, n.add(br2_in, 16))
                for t in range(NT):
                    add_to_stream(t, take("N"), dst=XL)
                    last = v.tensor_tensor(XL[:, t, :], XL[:, t, :], BR[0:P, 2, :], ALU.add)
                    if t < NT - 1:
                        step(last)
                    else:
                        signal(last, mlp_rows_free)
                    stats(t, XL[:, t, :])
                psum.align()
            dve.wait_ge(rstd_ready, n.add(rstd_ready, NT))
            for t in range(NT):
                step(v.tensor_tensor(X[0:P, t, :], X[0:P, t, :], XL[:, t, :], ALU.add))
                stats(t, X[0:P, t, :])

            norm_y()
            psum.skip(T=NT)
            logits()
            dve.wait_ge(small_in, 16 * SMALLS)
            for t in range(NT):
                step(v.max(M8[:, t, :], LG[:, t, :]))
            step(v.tensor_copy(TW[:, :, 0:2], M8[:, :, 0:2]))
            for t in range(NT):
                step(v.tensor_tensor(LG[:, t, :], LG[:, t, :], BI[:, :], ALU.add))
                best_two(LG[:, t, :], t)
            v.tensor_copy(SM[:, 4:5], SM[:, 3:4]).then_inc(negmax_ready, 1)
            dve.wait_ge(exp_ready, n.add(exp_ready))
            step(v.tensor_scalar(TW[:, :, 0:2], TW[:, :, 0:2], 1.0, None, ALU.add))
            step(v.reciprocal(TW[:, :, 0:2], TW[:, :, 0:2]))
            step(v.tensor_tensor(TW[:, :, 2], TW[:, :, 0], TW[:, :, 1], ALU.add))
            step(v.reciprocal(TW[:, :, 2], TW[:, :, 2]))
            for t in range(NT):
                step(v.tensor_scalar(TW[:, t, 0:2], TW[:, t, 0:2], TW[:, t, 2:3], None, ALU.mult))
                step(shares(t, TW[:, t, 0:1], TW[:, t, 1:2]))
            psum.align()
            with dve.Fori(0, 9) as i, n.loop(i, 9, loops, "expert"):
                for u in range(2):
                    ffn_unit(scalar=lambda t: COMB[:, t, bass.ds(i, 1)], with_stats=False)
            store_x(dve)
    return nc



def mat(w):
    return np.ascontiguousarray(w.reshape(K4, 128, -1).transpose(1, 0, 2)).reshape(128, -1)


def padded(w, rows, cols):
    out = np.zeros((rows, cols), w.dtype)
    out[:w.shape[0], :w.shape[1]] = w
    return out


def constants():
    c = np.zeros((128, C_END), np.float32)
    c[:, C_ID:C_ID + 128] = np.eye(128)
    c[:P, C_TRI:C_TRI + P] = np.tril(np.ones((P, P)), -1)
    c[:, C_I8:C_I8 + 8] = np.arange(8)
    freqs = np.arange(1, FREQS + 1, dtype=np.float32) * np.float32(2.0 * np.pi / 16)
    c[:2 * FREQS, C_FREQ] = np.concatenate([freqs, freqs])
    c[FREQS:2 * FREQS, C_SHIFT] = np.pi / 2
    c[FREQS:2 * FREQS, C_FRAC] = 0.25
    c[:, C_DUMP] = N * N + np.arange(128)
    for e in range(8):
        c[e, C_SEL + 64 * e:C_SEL + 64 * (e + 1)] = 1.0
    return c


def laid_out(i):
    i = {k: np.asarray(x) for k, x in i.items()}
    heads = lambda w: w.transpose(1, 0, 2).reshape(D, -1)
    col = lambda b: b.reshape(K4, 128).T
    a5 = i["L0_gnn_a"].reshape(HEADS0, 5, DH0)
    a = {
        "x": i["x"], "consts": constants(),
        "src_p": i["src"].reshape(P, ET), "dst_p": i["dst"].reshape(P, ET),
        "edge_weight": i["edge_weight"].reshape(P, ET),
        "edge_attr": i["edge_attr_64"].reshape(P, ET * 64),
        "noise": i["node_vec1"].reshape(-1),
        "W_e": mat(heads(i["L0_gnn_W_e"])), "W_r": mat(heads(i["L0_gnn_W_r"])),
        "arow": a5[:, [0, 1, 3, 4, 2]].transpose(1, 0, 2).reshape(-1),
        "Wm": mat(i["L1_gnn_Wm"]), "W1": mat(i["L1_gnn_W1"]), "W2": i["L1_gnn_W2"],
        "e_W1": mat(heads(i["L1_ffn_W1"])), "e_W3": mat(heads(i["L1_ffn_W3"])),
        "e_W2": mat(i["L1_ffn_W2"].reshape(D, D)),
        "Wtop": np.stack([mat(w[:D]) for w in i["L2_gnn_Ws"]]),
        "Wbot": i["L2_gnn_Ws"][:, D:].transpose(1, 0, 2).reshape(64, -1),
        "f_W1": mat(heads(i["L2_ffn_W1"])), "f_W2": mat(i["L2_ffn_W2"].reshape(D, D)),
        "f_b2": i["L2_ffn_b2"],
        "gate_0": mat(i["L1_ffn_gate_w"]), "gate_1": mat(i["L2_ffn_Wg"]),
        "gate_2": mat(i["L3_ffn_gate_w"].T), "biases": i["L3_ffn_biases"],
        "f_w1": i["L3_gnn_f_w1"], "f_w2": i["L3_gnn_f_w2"],
        "f_cols": np.stack([i["L3_gnn_f_b1"], i["L3_gnn_f_b2"]], 1),
    }
    a["Wlast"] = np.concatenate([a["Wbot"], i["L2_gnn_bs"].reshape(1, -1)])
    a["rows"] = np.concatenate([i[f"L1_gnn_{k}"] for k in ("bm", "b1", "gamma", "beta", "b2")]
                               + [i["L2_gnn_gammas"].reshape(-1), i["L2_gnn_betas"].reshape(-1),
                                  i["L2_ffn_b1"].reshape(-1)])
    halves = lambda w: [w[:, D * u:D * (u + 1)] for u in range(3)]
    for name, w in (("gate", i["L0_ffn_w_gate"].T), ("up", i["L0_ffn_w_up"].T)):
        a[name] = np.stack([mat(padded(h, D, D)) for h in halves(w)])
    a["down"] = np.stack([mat(padded(h.T, D, D)) for h in halves(i["L0_ffn_w_down"])])
    g = lambda k: i[f"L3_gnn_{k}"]
    a["modw"] = np.stack([np.stack([np.concatenate([g(f"{k}_w")[b], g(f"{k}_b")[b][None]])
                                    for k in ("s1", "b1", "s2", "b2")], 1) for b in range(BLOCKS)])
    a["brow"] = np.stack([g(k) for k in ("bv", "bo", "m_b2")], 1).reshape(-1)
    a["columns"] = np.concatenate([col(g(k)[b]) for b in range(BLOCKS) for k in ("bq", "bk", "m_b1")], 1)
    a["qkv"] = np.stack([mat(g(k)[b]) for b in range(BLOCKS) for k in ("wq", "wk", "wv")])
    a["omm"] = np.stack([mat(g(k)[b]) for b in range(BLOCKS) for k in ("wo", "m_w1", "m_w2")])
    f = lambda k: i[f"L3_ffn_{k}"]
    for name, routed, shared in (("x_a", "w1", "sw1"), ("x_b", "w3", "sw3")):
        a[name] = np.stack([mat(w[:, D * u:D * (u + 1)]) for w in (*f(routed), f(shared)) for u in range(2)])
    a["x_c"] = np.stack([mat(w[D * u:D * (u + 1)]) for w in (*f("w2"), f("sw2")) for u in range(2)])
    return {k: np.ascontiguousarray(x) for k, x in a.items()}


def build(nc, arrays):
    aps = {k: nc.dram_tensor(f"in_{k}", x.shape, mybir.dt.from_np(x.dtype), kind="ExternalInput").ap()
           for k, x in arrays.items()}
    out = nc.dram_tensor("out_0", (N, D), F32, kind="ExternalOutput").ap()
    program(nc, aps, out, LOOPS)


def kernel(**inputs):
    import concourse.bacc as _bacc
    from concourse.bass_utils import run_bass_kernel_spmd as _run

    arrays = laid_out(inputs)
    nc = _bacc.Bacc("TRN2", target_bir_lowering=False, num_devices=1, dynamic_dma_scratch_size=8192)
    build(nc, arrays)
    r = _run(nc, [{f"in_{k}": x for k, x in arrays.items()}], core_ids=[0])
    return r.results[0]["out_0"]
```

```python
from contextlib import ExitStack, contextmanager

import numpy as np
import concourse.bass as bass
from concourse import mybir

F32, F32R, BF16, I16, I32, U32 = (mybir.dt.float32, mybir.dt.float32r, mybir.dt.bfloat16,
                                  mybir.dt.int16, mybir.dt.int32, mybir.dt.uint32)
ALU, ACT, AX = mybir.AluOpType, mybir.ActivationFunctionType, mybir.AxisListType

N, E, D = 625, 10000, 512
P, NT = 125, 5
ET = E // P
K4 = D // 128
HEADS0, DH0 = 8, 64
HEADS3 = 4
BLOCKS = 4
FREQS = 32
NEG = -1.0e30
BANK = 512
MAIN, TAIL = BANK, N - BANK
MAGIC = 12582912.0
STEP = 16
TURNS = ET // STEP
GATHERS_A, GATHERS_B = 4, 12
AHEAD = 4
UNITS = 18
HOTS = 4
ROWLEN = D + 2 * HEADS0

C_ID, C_TRI, C_I8, C_FREQ, C_SHIFT, C_FRAC, C_DUMP, C_SEL = 0, 128, 253, 261, 262, 263, 264, 265
C_END = C_SEL + D
R_BM, R_B1, R_G1, R_BE1, R_B2, R_G2, R_BE2, R_FB1 = 0, 256, 384, 512, 640, 1152, 2688, 4224
R_END = 4736


class Tally:

    def __init__(self, engine):
        self.engine, self.count, self.turn, self.per, self.base = engine, {}, None, {}, {}

    def add(self, sem, n=1):
        self.count[sem.name] = self.count.get(sem.name, 0) + n
        return self.now(sem)

    def now(self, sem):
        c = self.count.get(sem.name, 0)
        if self.turn is None:
            return c
        return self.turn * self.per.get(sem.name, 0) + c

    @contextmanager
    def loop(self, turn, trips, loops, name):
        per = loops[name].get(self.engine, {})
        self.turn, self.per, before = turn, per, dict(self.count)
        yield
        grew = {k: c - before.get(k, 0) for k, c in self.count.items() if c != before.get(k, 0)}
        for k, c in grew.items():
            self.count[k] += (trips - 1) * c
        wrong = grew != {k: v for k, v in per.items() if v}
        self.turn, self.per = None, {}
        assert not wrong, (name, self.engine, grew)


LOOPS = {
    "count": {
        "pe": {"onehot_ready": 16},
        "act": {"diff_ready": 4},
        "dve": {"vector_step": 20, "onehot_used": 16, "gathered_0": 32, "gathered_1": 32, "abs_ready":
               4, "score_taken": 4, "gathered_2": 32, "gathered_3": 32},
    },
    "weight": {
        "pe": {"parts_ready": 16},
        "act": {"diff_ready": 12, "plain_ready": 16},
        "dve": {"vector_step": 60, "onehot_used": 16, "gathered_0": 96, "gathered_1": 96, "abs_ready":
               12, "score_taken": 12, "gathered_2": 96, "gathered_3": 96},
    },
    "edge": {
        "pe": {"onehot_ready": 16, "low_ready": 4},
        "act": {"onehot_used": 16, "edge_read": 4, "edge_in_0": 16, "last_ready": 4, "edge_in_1": 16,
               "edge_in_2": 16, "edge_in_3": 16},
        "dve": {"edge_read": 4, "onehot_used": 16, "high_ready": 4, "middle_ready": 4},
    },
    "gather": {
        "pool": {"score_taken": 4, "pool_step": 8, "score_ready": 4, "scattered": 64},
    },
    "block": {
        "pe": {"filled_T0": 5, "y_ready": 10, "filled_T1": 5, "weights_in_0": 48, "filled_N0": 8,
               "filled_N1": 7, "filled_W0": 33, "filled_W1": 33, "weights_in_1": 48, "mod_split": 2,
               "prob_ready": 15, "last_prob_ready": 5},
        "act": {"filled_T0": 5, "filled_T1": 5, "filled_N0": 8, "filled_N1": 7, "negmax_ready": 20,
               "filled_W0": 33, "filled_W1": 33, "modw_in": 64, "mod2_in": 64, "sums_ready": 3},
        "dve": {"vector_step": 65, "rstd_ready": 10, "y_ready": 10, "filled_T0": 5, "filled_T1": 5,
               "filled_N0": 8, "filled_N1": 7, "exp_ready": 20, "filled_W0": 33, "filled_W1": 33,
               "attn_rows_free": 1, "mlp_rows_free": 1, "mod_rounded": 2, "br_in": 16, "bias_added":
               10},
        "pool": {"var_ready": 10, "y_ready": 10, "br_in": 16, "br2_in": 16},
    },
    "expert": {
        "pe": {"filled_T0": 5, "filled_T1": 5, "filled_N0": 15, "filled_N1": 15, "split_ready": 6},
        "act": {"filled_T0": 5, "filled_T1": 5, "filled_N0": 15, "filled_N1": 15, "weights_in_0": 48,
               "weights_in_1": 48},
        "dve": {"filled_T0": 5, "filled_T1": 5, "filled_N0": 15, "filled_N1": 15, "hi_ready": 10,
               "rounded": 6},
    },
    "abs": {
        "act": {"diff_ready": 2},
    },
}
TWO_PI = (6.28125, 2029.0 / 2 ** 20, 2.0 * np.pi - 6.28125 - 2029.0 / 2 ** 20)


WIDTHS = (D, D, 1408 - 2 * D)
SMALLS = 8


def groups_of(u):
    return ([(j, c, WIDTHS[u]) for j in range(2) for c in range(K4)]
            + [(2, c, D) for c in range(WIDTHS[u] // 128)])


def bcast(row, at, n, parts):
    return row[bass.ds(at, n)].partition_broadcast(parts)


class Slot:
    def __init__(self, ap, filled, taken):
        self.ap, self.filled, self.taken = ap, filled, taken


class Slots:

    def __init__(self, slots, tally):
        self.slots, self.tally, self.turn = slots, tally, {"T": 0, "W": 0, "N": 0}

    def next(self, kind):
        s = self.slots[kind][self.turn[kind] % 2]
        self.turn[kind] += 1
        first = self.tally.turn is None and self.tally.count.get(s.filled.name, 0) == 0
        before = None if first else self.tally.now(s.filled)
        return s, self.tally.add(s.filled), before

    def skip(self, **kinds):
        for kind, n in kinds.items():
            for _ in range(n):
                self.next(kind)

    def align(self):
        self.turn = {"T": 0, "W": 0, "N": 0}


def program(nc, a, out, loops):
    ctx = ExitStack()

    def sb(name, shape, dt=F32):
        return ctx.enter_context(nc.sbuf_tensor(name, shape, dt))

    def passing(name, shape, dt=F32):
        with nc.sbuf_tensor(name, shape, dt) as t:
            return t

    def sem(name):
        return ctx.enter_context(nc.semaphore(name))

    hr_rows = nc.dram_tensor("hr_rows", [N, ROWLEN], F32, kind="Internal").ap()
    pair_scores = nc.dram_tensor("pair_scores", [N * N + 128, HEADS0], F32, kind="Internal").ap()

    with ctx:

        X = sb("X", [128, NT, D])
        Y = passing("Y", [128, NT, D])
        HTL = sb("HTL", [128, NT * D], F32R)[:, 0:K4 * N].rearrange("p (c n) -> p c n", c=K4)
        XT = passing("XT", [128, K4, N])
        XTH = sb("XTH", [128, K4, N], F32R)
        WR = sb("WR", [128, 2, 3, K4 * D])
        CNT = sb("CNT", [P, NT, N])
        MASK = sb("MASK", [P, NT, N], BF16)
        G = sb("G", [P, NT, N])
        EA1 = passing("EA1", [128, N])
        CONDR = sb("CONDR", [128, N], F32R)
        EA2 = sb("EA2", [128, N])
        MODW = sb("MODW", [128, 4, D])
        BR = sb("BR", [128, 3, D])
        CS = sb("CS", [128, C_END])
        PC = sb("PC", [128, 3 * K4 * BLOCKS])
        FW = sb("FW", [64, 16 + 128 + 1])
        FB2 = sb("FB2", [128, 1])
        IOTA = sb("IOTA", [P, N], I16)
        ONES = sb("ONES", [128, 128])
        HALF = sb("HALF", [P, 1])
        ST = sb("ST", [P, NT, 6])
        MV = sb("MV", [P, NT, 2])
        VE = sb("VE", [P, NT])
        RSTD = sb("RSTD", [P, NT])
        SM = sb("SM", [P, 64])
        DEN = sb("DEN", [P, 2, 4, NT])
        LG = sb("LG", [P, NT, 8])
        M8 = sb("M8", [P, NT, 8])
        I8 = sb("I8", [P, NT, 8], U32)
        TW = sb("TW", [P, NT, 6])
        COMB = sb("COMB", [P, NT, 9])
        ISRC = sb("ISRC", [P, ET], U32)
        IDST = sb("IDST", [P, ET], U32)
        SIDX = sb("SIDX", [P, ET], U32)
        FS = sb("FS", [P, 9, ET])
        IDS = sb("IDS", [P, 3 * AHEAD], U32)
        TS = sb("TS", [P, AHEAD, HEADS0])
        SUMS = sb("SUMS", [P, 2, HEADS0])
        HM = sb("HM", [P, 2, 4, HEADS0])
        UV = sb("UV", [128, K4, 16])
        WG = sb("WG", [128, 3, K4, 8])
        BI = sb("BI", [P, 8])
        TWOS = sb("TWOS", [8, P])
        UVT = sb("UVT", [128, 3, 4 * HEADS0])
        EB = sb("EB", [P, ET], BF16)
        HT_, XL_, PT_, KT_, V_, PR_ = 0, 2500, 5060, 8185, 10745, 13305
        AR = passing("AR", [128, PR_ + R_END])
        with nc.sbuf_tensor("AR_blocks", [128, PR_ + NT * N], F32):
            MODR = passing("MODR", [128, 2, D], F32R)
        WHI = sb("WHI", [128, 3, K4, D], F32R)
        WLO = sb("WLO", [128, 3, K4, D], F32R)
        XTL = sb("XTL", [128, K4, N], F32R)
        HTH = sb("HTH", [128, K4, N], F32R)

        def view(at, parts, *shape, dt=F32):
            n = 1
            for s in shape:
                n *= s
            words = n if dt in (F32, I32, U32) else (n + 1) // 2
            v = AR[0:parts, at:at + words]
            if dt != F32:
                v = v.bitcast(dt)[:, 0:n]
            if len(shape) == 1:
                return v
            names = "abc"[:len(shape)]
            return v.rearrange(f"p ({' '.join(names)}) -> p {' '.join(names)}",
                               **{k: s for k, s in zip(names[1:], shape[1:])})

        HT = view(HT_, 128, K4, N)
        XL = view(XL_, P, NT, D)
        HE = XL
        PT = view(PT_, P, NT, N)
        KT = view(KT_, 128, HEADS3, N)
        V = view(V_, P, NT, D)
        PRB = view(PR_, P, NT, N)
        ROWS = view(PR_, P, R_END)
        HS = [view(PT_ + 2 * ROWLEN * b, P, ROWLEN) for b in range(AHEAD)]
        HD = [view(PT_ + 2 * ROWLEN * b + ROWLEN, P, ROWLEN) for b in range(AHEAD)]
        PRD = [view(HT_ + 2 * D * b, P, 2, D) for b in range(2)]
        TAILS = XT[0:TAIL, 0, :]
        XF = XT[:, :, :].rearrange("p a b -> p (a b)").bitcast(BF16)
        PLAIN = [XF[0:P, 1250 + 626 * b:1250 + 626 * b + N] for b in range(HOTS)]
        YF = Y[:, :, :].rearrange("p a b -> p (a b)").bitcast(BF16)
        hots = [view(V_ + 313 * j, P, N, dt=BF16) for j in range(8)] + [
            YF[0:P, 626 * j:626 * j + N] for j in range(8)]
        OS = [hots[4 * b] for b in range(HOTS)]
        OD = [hots[4 * b + 1:4 * b + 4] for b in range(HOTS)]
        ZROW = view(PR_, P, 2500)
        ZB = view(PR_ + 2500, P, BANK, dt=BF16)
        KEYT = view(HT_ + 2048, ET, P)
        ER = [view(PR_ + 256 * b, P, 4, 64) for b in range(4)]
        ERR = [view(PR_ + 1024 + 256 * b, P, 4, 64) for b in range(2)]
        S1 = [view(PR_ + 3524 + 256 * b, P, 4, 128, dt=BF16) for b in range(2)]
        S2 = [view(PR_ + 4036 + 132 * b, P, 4, 66, dt=BF16) for b in range(2)]
        GF = G[:, :, :].rearrange("p a b -> p (a b)")
        HID = CNT[:, :, :].rearrange("p a b -> p (a b)")[:, 0:NT * D].rearrange(
            "p (t c) -> p t c", t=NT)
        KROW = GF[:, 0:20 * P].rearrange("p (m e) -> p m e", e=P)
        HRN = CNT[:, :, :].rearrange("p a b -> p (a b)")[:, 0:NT * ROWLEN].rearrange(
            "p (t c) -> p t c", t=NT)
        TSC = [view(PT_ + 5000 * b, P, N * HEADS0) for b in range(2)]
        SP0 = [view(HT_ + 625 * b, P, N) for b in range(4)]
        PTS = [view(PT_ + 10000 + 625 * b, P, NT, P) for b in range(2)]
        SG = [view(PT_ + 625 * b, 128, N) for b in range(2)]
        ROW = [view(PT_ + 1250 + 512 * b, P, D) for b in range(2)]
        MF = view(KT_, P, NT, 256)
        HB = view(V_, P, NT, 128)
        HBT = view(V_ + 640, 128, N)
        GE = [[view(PT_ + 1250 + 512 * (2 * b + i), P, D) for i in range(2)] for b in range(2)]
        EMB = view(PT_, 64, N)
        EMN = view(PT_ + 625, 64, N)
        EMR = view(PT_ + 1250, 64, N)
        ZC = view(PT_ + 1875, 16, N)
        COND4 = EA2
        CT8 = view(V_, 8, N)
        WTMP = view(HT_, 128, K4, D)
        AW = [MODW[:, b, :] for b in range(2)]
        SGN = [MODW[:, 2 + b, :] for b in range(2)]
        SCL = [BR[:, 1 + b, :] for b in range(2)]

        ID = CS[:, C_ID:C_ID + 128]
        SEL = CS[0:8, C_SEL:C_SEL + D]

        def wm(s, j, n=D):
            return WR[:, s, j, :].rearrange("p (c n) -> p c n", c=K4)[:, :, 0:n]


        PS = ctx.enter_context(nc.psum_tensor("PS", [128, 8 * BANK], F32))
        slots = {}
        for kind, at, size in (("T", 0, BANK), ("W", 2 * BANK, 2 * BANK), ("N", 6 * BANK, BANK)):
            slots[kind] = [Slot(PS[:, at + k * size:at + (k + 1) * size], sem(f"filled_{kind}{k}"),
                                sem(f"taken_{kind}{k}")) for k in range(2)]

        def main_of(c):
            return PS[0:P, BANK * c:BANK * c + MAIN]

        def tail_of(c):
            at = 7 * BANK + TAIL * c if c < 4 else 6 * BANK
            return PS[0:P, at:at + TAIL]

        tails = PS[0:TAIL, 5 * BANK:5 * BANK + N]


        x_in, consts_in, index_in, arow_in, small_in = map(sem, (
            "x_in", "consts_in", "index_in", "arow_in", "small_in"))
        loaded = [sem("weights_in_0"), sem("weights_in_1")]
        rows_in, edge_in = sem("rows_in"), [sem(f"edge_in_{b}") for b in range(4)]
        modw_in, br_in, mod2_in, br2_in, noise_in = map(sem, ("modw_in", "br_in", "mod2_in", "br2_in", "noise_in"))
        weights_used = sem("weights_used")
        vector_step, pool_step, scalar_step = sem("vector_step"), sem("pool_step"), sem("scalar_step")
        start_done = sem("pool_constants")
        var_ready, rstd_ready = sem("var_ready"), sem("rstd_ready")
        y_ready = sem("y_ready")
        uv_ready, hr_stored = sem("uv_ready"), sem("hr_stored")
        onehot_ready, onehot_used = sem("onehot_ready"), sem("onehot_used")
        gathered = [sem(f"gathered_{b}") for b in range(AHEAD)]
        score_ready, scattered = sem("score_ready"), sem("scattered")
        cleared, clear_row_ready = sem("cleared"), sem("clear_row_ready")
        keys_ready, sidx_ready = sem("keys_ready"), sem("sidx_ready")
        graph_filled, graph_taken = sem("graph_filled"), sem("graph_taken")
        tails_taken, tails_back = sem("tails_taken"), sem("tails_back")
        high_ready, middle_ready, low_ready = sem("high_ready"), sem("middle_ready"), sem("low_ready")
        last_ready = sem("last_ready")
        plain_ready, parts_ready = sem("plain_ready"), sem("parts_ready")
        edge_read = sem("edge_read")
        pairs_in = [sem("pair_scores_in_0"), sem("pair_scores_in_1")]
        negmax_ready, exp_ready, sums_ready = sem("negmax_ready"), sem("exp_ready"), sem("sums_ready")
        weights_summed, prob_ready = sem("weights_summed"), sem("prob_ready")
        relu_ready = sem("relu_ready")
        last_prob_ready, bias_added = sem("last_prob_ready"), sem("bias_added")
        absw_ready, kept_ready, quant_ready = sem("absw_ready"), sem("kept_ready"), sem("quant_ready")
        diff_ready, abs_ready = sem("diff_ready"), sem("abs_ready")
        score_taken = sem("score_taken")
        layer_ready = sem("layer_ready")
        attn_rows_free, mlp_rows_free = sem("attn_rows_free"), sem("mlp_rows_free")
        cond_rounded, cond_split = sem("cond_rounded"), sem("cond_split")
        mod_rounded, mod_split = sem("mod_rounded"), sem("mod_split")
        hi_ready, rounded, split_ready = sem("hi_ready"), sem("rounded"), sem("split_ready")
        normed_before = []
        landed = [0, 0]
        emb_ready, sin_ready = sem("emb_ready"), sem("sin_ready")
        out_ready, out_done = sem("out_ready"), sem("out_done")

        def store_x(eng):
            eng.drain().then_inc(out_ready, 1)

        block = ctx.enter_context(nc.Block())
        def loads(sp):
            n = Tally("sp")
            sp.dma_start(X[0:P, :, :], a["x"].rearrange("(t p) d -> p t d", p=P)).then_inc(x_in, 16)
            sp.dma_start(CS[:, :], a["consts"]).then_inc(consts_in, 16)
            batch = [0]

            def load(mats):
                k = batch[0]
                batch[0] += 1
                if k >= 2:
                    sp.wait_ge(weights_used, k - 1)
                for dst, src in mats:
                    sp.dma_start(dst, src).then_inc(loaded[k % 2], 16)
                    landed[k % 2] += 16

            def mat(s, j, name, at=None):
                src = a[name] if at is None else a[name][at]
                return WR[:, s, j, :], src

            load([mat(0, 0, "W_e"), mat(0, 1, "W_r")])
            load([mat(1, 0, "gate", 0), mat(1, 1, "up", 0), mat(1, 2, "down", 0)])
            sp.wait_ge(clear_row_ready, 1)
            for t in range(NT):
                dst = pair_scores[N * P * t:N * P * (t + 1), :].rearrange("(p q) h -> p (q h)", p=P)
                for half in range(2):
                    sp.dma_start(dst[:, 2500 * half:2500 * (half + 1)], ZROW).then_inc(cleared, 16)
            sp.wait_ge(cleared, 16 * 2 * NT)
            with sp.Fori(0, TURNS) as i:
                for b in range(4):
                    sp.wait_ge(edge_read, i * 4 + b + 1)
                    sp.dma_start(ER[b].rearrange("p a b -> p (a b)"),
                                 a["edge_attr"][:, bass.ds(i * 1024 + 256 * b, 256)]).then_inc(edge_in[b], 16)
            load([mat(0, 0, "gate", 1), mat(0, 1, "up", 1), mat(0, 2, "down", 1)])
            sp.wait_ge(scattered, 16 * ET)
            for t in range(1, NT):
                if t == 1:
                    sp.wait_ge(graph_taken, 3)
                if t >= 2:
                    sp.wait_ge(exp_ready, 1 + HEADS0 * (t - 1))
                src = pair_scores[N * P * t:N * P * (t + 1), :].rearrange("(p q) h -> p (q h)", p=P)
                sp.dma_start(TSC[t % 2], src).then_inc(pairs_in[t % 2], 16)
            load([mat(1, 0, "gate", 2), mat(1, 1, "up", 2), mat(1, 2, "down", 2)])
            sp.dma_start(ROWS, bcast(a["rows"], 0, R_END, P)).then_inc(rows_in, 16)
            load([(WR[:, 0, 0, 0:K4 * 256], a["Wm"]), (WR[:, 0, 1, 0:K4 * 128], a["W1"]),
                  (WR[:, 0, 2, 0:D], a["W2"])])
            load([mat(1, j, x) for j, x in enumerate(("e_W1", "e_W3", "e_W2"))])
            load([mat(0, j, "Wtop", j) for j in range(3)])
            load([(WR[0:64, 1, 0, 0:3 * D], a["Wbot"]), (WR[64:128, 1, 0, 0:3 * D], a["Wbot"]),
                  (WR[0:65, 1, 1, 0:3 * D], a["Wlast"])])
            load([mat(0, 0, "f_W1"), mat(0, 1, "f_W2"), (WR[0:8, 0, 2, 0:D], a["f_b2"])])
            def attn_rows(i):
                for r in range(4):
                    sp.dma_start(MODW[32 * r:32 * r + 17, 0:2, :], a["modw"][bass.ds(i, 1), :, 0:2, :]
                                 .rearrange("a p b n -> (a p) b n")).then_inc(modw_in, 16)
                sp.dma_start(BR[0:P, 0:2, :], bcast(a["brow"], i * 3 * D, 2 * D, P).rearrange(
                    "p (a b) -> p a b", a=2)).then_inc(br_in, 16)

            def mlp_rows(i):
                for r in range(4):
                    sp.dma_start(MODW[32 * r:32 * r + 17, 2:4, :], a["modw"][bass.ds(i, 1), :, 2:4, :]
                                 .rearrange("a p b n -> (a p) b n")).then_inc(mod2_in, 16)
                sp.dma_start(BR[0:P, 2, :], bcast(a["brow"], i * 3 * D + 2 * D, D, P)).then_inc(br2_in, 16)

            sp.dma_start(EMN, bcast(a["noise"], 0, N, 64)).then_inc(noise_in, 16)
            k0 = batch[0]
            with sp.Fori(0, BLOCKS) as i:
                sp.wait_ge(attn_rows_free, i + 1)
                attn_rows(i)
                sp.wait_ge(weights_used, i * 2 + k0 - 1)
                for j in range(3):
                    sp.dma_start(WR[:, 1, j, :], a["qkv"][bass.ds(i * 3 + j, 1)].rearrange(
                        "a p n -> (a p) n")).then_inc(loaded[1], 16)
                sp.wait_ge(mlp_rows_free, i + 1)
                mlp_rows(i)
                sp.wait_ge(weights_used, i * 2 + k0)
                for j in range(3):
                    sp.dma_start(WR[:, 0, j, :], a["omm"][bass.ds(i * 3 + j, 1)].rearrange(
                        "a p n -> (a p) n")).then_inc(loaded[0], 16)
            for s in range(2):
                landed[s] += 48 * BLOCKS
            k1 = k0 + 2 * BLOCKS

            def unit_weights(i, u):
                for j, x in enumerate(("x_a", "x_b", "x_c")):
                    src = a[x][bass.ds(i * 2 + u, 1)].rearrange("a p n -> (a p) n")
                    sp.dma_start(WR[:, 1 - u, j, :], src).then_inc(loaded[1 - u], 16)

            for u in range(2):
                sp.wait_ge(weights_used, k1 + u - 1)
                unit_weights(0, u)
            with sp.Fori(1, UNITS // 2) as i:
                for u in range(2):
                    sp.wait_ge(split_ready, i * 6 + 3 * u - 3)
                    unit_weights(i, u)

        @block.sync
        def _(sp):
            loads(sp)
            sp.wait_ge(out_ready, 1)
            sp.dma_start(out.rearrange("(t p) d -> p t d", p=P), X[0:P, :, :]).then_inc(out_done, 16)
            sp.wait_ge(out_done, 16)

        @block.tensor
        def _(pe):
            n = Tally("pe")
            psum = Slots(slots, n)
            mm = nc.tensor.matmul

            def fill(kind):
                s, _, before = psum.next(kind)
                if before is not None:
                    pe.wait_ge(s.taken, before)
                return s

            def weights(s, mats):
                pe.wait_ge(loaded[s], n.add(loaded[s], 16 * mats))

            def weights_done():
                pe.drain().then_inc(weights_used, 1)

            def wide(s, parts, terms, lhs, rhs):
                for c0, c1 in ((0, MAIN), (MAIN, N)):
                    for k in range(terms):
                        last = mm(s.ap[0:parts, c0:c1], lhs(k), rhs(k)[:, c0:c1],
                                  start=(k == 0), stop=(k == terms - 1))
                last.then_inc(s.filled, 1)

            def narrow(s, cols, pairs):
                for k, (lhs, rhs) in enumerate(pairs):
                    last = mm(s.ap[0:P, 0:cols], lhs, rhs, start=(k == 0), stop=(k == len(pairs) - 1))
                last.then_inc(s.filled, 1)

            def tile(t):
                return slice(P * t, P * (t + 1))

            def transpose_y():
                for t in range(NT):
                    s = fill("T")
                    pe.wait_ge(y_ready, n.add(y_ready))
                    for c in range(K4):
                        last = nc.tensor.transpose(s.ap[:, P * c:P * (c + 1)],
                                                   Y[0:P, t, 128 * c:128 * (c + 1)], ID[0:P, 0:P])
                    last.then_inc(s.filled, 1)
                all_taken("T")

            def all_taken(kinds):
                for kind in kinds:
                    for s in slots[kind]:
                        pe.wait_ge(s.taken, n.now(s.filled))

            def project_wide(w, m):
                s = fill("W")
                wide(s, 128, K4, lambda k: w[:, k, 128 * m:128 * (m + 1)], lambda k: XT[:, k, :])
                return s, n.now(s.filled)

            def logits(xs, w):
                s = fill("N")
                for t in range(NT):
                    terms = [(x, k) for x in xs for k in range(K4)]
                    for j, (x, k) in enumerate(terms):
                        last = mm(s.ap[0:P, 8 * t:8 * t + 8], x[:, k, tile(t)], w[:, k, :],
                                  start=(j == 0), stop=(j == len(terms) - 1))
                last.then_inc(s.filled, 1)

            def project_narrow(w, t, cols=D, extra=()):
                s = fill("N")
                narrow(s, cols, list(extra) + [(XT[:, k, tile(t)], w[:, k, 0:cols]) for k in range(K4)])


            pe.wait_ge(consts_in, 16)
            pe.wait_ge(start_done, 6)
            transpose_y()
            weights(0, 2)
            we, wr = wm(0, 0), wm(0, 1)
            for t in range(NT):
                project_narrow(wr, t)
            for t in range(NT):
                project_narrow(we, t)
            pe.wait_ge(uv_ready, 1)
            s = fill("N")
            for t in range(NT):
                for k in range(K4):
                    last = mm(s.ap[0:P, 16 * t:16 * t + 16], XT[:, k, tile(t)], UV[:, k, :],
                              start=(k == 0), stop=(k == K4 - 1))
            last.then_inc(s.filled, 1)
            weights_done()
            s = fill("N")
            pe.wait_ge(layer_ready, n.add(layer_ready))
            nc.tensor.transpose(s.ap[0:1, 0:P], SM[:, 0:1], ID[0:P, 0:P]).then_inc(s.filled, 1)
            s = fill("N")
            pe.wait_ge(layer_ready, n.add(layer_ready))
            mm(s.ap[0:P, 0:1], ONES[0:1, 0:P], SM[0:1, 1:2], start=True, stop=True).then_inc(s.filled, 1)

            s = fill("T")
            pe.wait_ge(keys_ready, 1)
            nc.tensor.transpose(s.ap[0:ET, 0:P], FS[:, 2, :], ID[0:P, 0:P]).then_inc(s.filled, 1)
            all_taken("T")
            for q in range(ET // 4):
                s = fill("N")
                for k in range(4):
                    m = 4 * q + k
                    last = mm(s.ap[0:P, P * k:P * (k + 1)], ID[0:ET, m:m + 1].broadcast_to([ET, P]),
                              KEYT[:, :], start=True, stop=True)
                last.then_inc(s.filled, 1)


            banks = [(BANK * c, MAIN) for c in range(5)] + [(5 * BANK, MAIN), (6 * BANK, TAIL)]

            def zero(banks, signal):
                for k, (at, size) in enumerate(banks):
                    last = mm(PS[0:128, at:at + size], ZB[:, 0:128], ZB[:, 0:size], start=True,
                              stop=False, skip_group_check=True)
                    if signal and k >= len(banks) - HOTS:
                        last.then_inc(onehot_used, 1)

            def close(banks):
                for at, size in banks:
                    last = mm(PS[0:128, at:at + size], ZB[:, 0:128], ZB[:, 0:size], start=False,
                              stop=True, skip_group_check=True)
                last.then_inc(graph_filled, 1)

            def turn_tails(k):
                pe.wait_ge(tails_taken, k)
                for c in range(NT):
                    last = nc.tensor.transpose(tail_of(c), TAILS[:, tile(c)], ID[0:TAIL, 0:TAIL])
                last.then_inc(tails_back, 1)

            def pair_pass(name, parts, ready):
                with pe.Fori(0, TURNS) as i, n.loop(i, TURNS, loops, name):
                    for k in range(STEP):
                        pe.wait_ge(ready, n.add(ready))
                        for c in range(NT):
                            for r in range(parts):
                                mm(main_of(c), OS[k % HOTS][:, tile(c)], OD[k % HOTS][r][:, 0:MAIN],
                                   start=False, stop=False, skip_group_check=True)
                        for r in range(parts):
                            for c0, c1 in ((0, MAIN), (MAIN, N)):
                                last = mm(tails[:, c0:c1], OD[k % HOTS][r][:, MAIN:N],
                                          OS[k % HOTS][:, c0:c1], start=False, stop=False,
                                          skip_group_check=True)
                        last.then_inc(onehot_used, 1)

            all_taken("TN")
            pe.wait_ge(clear_row_ready, 1)
            zero(banks, True)
            pair_pass("count", 1, onehot_ready)
            close(banks)
            turn_tails(1)
            pe.wait_ge(graph_taken, 1)
            zero(banks, False)
            pair_pass("weight", 3, parts_ready)
            close(banks)
            turn_tails(2)
            pe.wait_ge(graph_taken, 2)
            ea = [(2 * BANK, MAIN), (3 * BANK, TAIL), (4 * BANK, MAIN), (5 * BANK, TAIL)]
            zero(ea, False)
            with pe.Fori(0, TURNS) as i, n.loop(i, TURNS, loops, "edge"):
                for k in range(STEP):
                    if k % 4 == 0:
                        pe.wait_ge(low_ready, n.add(low_ready))
                    pe.wait_ge(onehot_ready, n.add(onehot_ready))
                    b = k // 4 % 2
                    for part, rows, at in ((S1[b][:, k % 4, :], 128, 2), (S2[b][:, k % 4, 0:65], 65, 4)):
                        mm(PS[0:rows, at * BANK:at * BANK + MAIN], part, OD[k % HOTS][0][:, 0:MAIN],
                           start=False, stop=False, skip_group_check=True)
                        last = mm(PS[0:rows, (at + 1) * BANK:(at + 1) * BANK + TAIL], part,
                                  OD[k % HOTS][0][:, MAIN:N], start=False, stop=False, skip_group_check=True)
                    last.then_inc(onehot_used, 1)
            close(ea)
            pe.wait_ge(graph_taken, 3)

            def quantized(u):
                for k, (j, c, width) in enumerate(groups_of(u)):
                    g = fill("T")
                    pe.wait_ge(absw_ready, n.add(absw_ready))
                    mm(g.ap[:, 0:width], ONES[:, :], AW[k % 2][:, 0:width], start=True, stop=True)\
                        .then_inc(g.filled, 1)
                    yield

            def transposed(k):
                s = fill("W")
                pe.wait_ge(weights_summed, n.add(weights_summed))
                for c in range(NT):
                    last = nc.tensor.transpose(s.ap[0:P, 128 * c:128 * c + P], SP0[k % 4][:, tile(c)],
                                               ID[0:P, 0:P])
                last.then_inc(s.filled, 1)
                return s, n.now(s.filled)

            ahead = quantized(0)
            head = transposed(0)
            for k in range(NT * HEADS0):
                h, now = k % HEADS0, head
                if k + 1 < NT * HEADS0:
                    head = transposed(k + 1)
                if h == 0:
                    o = fill("N")
                pe.wait_ge(now[0].taken, now[1])
                for c in range(NT):
                    last = mm(o.ap[0:P, DH0 * h:DH0 * (h + 1)], PTS[k % 2][:, c, :],
                              HE[:, c, DH0 * h:DH0 * (h + 1)], start=(c == 0), stop=(c == NT - 1))
                if h == HEADS0 - 1:
                    last.then_inc(o.filled, 1)
                if k % 3 == 2:
                    next(ahead, None)
            for _ in ahead:
                pass
            psum.align()

            def ffn_unit(s, chunks=K4, scaled=False, between=lambda: None):
                wa, wb, wc = wm(s, 0), wm(s, 1), wm(s, 2)
                hidden = []
                for m in range(chunks):
                    project_wide(wa, m)
                    between()
                    hidden.append(project_wide(wb, m))
                    between()
                    between()
                if scaled:
                    for t in range(NT):
                        s = fill("T")
                        if t == 0:
                            pe.wait_ge(layer_ready, n.add(layer_ready))
                        nc.tensor.transpose(s.ap[0:8, 0:P], COMB[:, t, 0:8], ID[0:P, 0:P])\
                            .then_inc(s.filled, 1)
                    all_taken("T")
                    for m in range(chunks):
                        s = fill("W")
                        wide(s, 128, 1, lambda k: SEL[:, 128 * m:128 * (m + 1)], lambda k: CT8)
                        hidden[m] = (s, n.now(s.filled))
                for t in range(NT):
                    o = fill("N")
                    for m in range(chunks):
                        if t == 0:
                            pe.wait_ge(hidden[m][0].taken, hidden[m][1])
                        last = mm(o.ap[0:P, :], HT[:, m, tile(t)], wc[:, m, :],
                                  start=(m == 0), stop=(m == chunks - 1))
                    last.then_inc(o.filled, 1)

            transpose_y()
            for u in range(3):
                weights((u + 1) % 2, 3)
                pe.wait_ge(quant_ready, n.add(quant_ready, len(groups_of(u))))
                ahead = quantized(u + 1) if u < 2 else iter(())
                ffn_unit((u + 1) % 2, WIDTHS[u] // 128, between=lambda: next(ahead, None))
                weights_done()

            transpose_y()
            weights(0, 3)
            w_m = WR[:, 0, 0, 0:K4 * 256].rearrange("p (c n) -> p c n", c=K4)
            w_1 = WR[:, 0, 1, 0:K4 * 128].rearrange("p (c n) -> p c n", c=K4)
            w_2 = WR[:, 0, 2, 0:D]
            for t in range(NT):
                project_narrow(w_m, t, 256)
            pe.wait_ge(layer_ready, n.add(layer_ready))
            for c in range(NT):
                s = fill("W")
                for t in range(NT):
                    last = nc.tensor.transpose(s.ap[0:P, 128 * t:128 * t + P], G[:, t, tile(c)], ID[0:P, 0:P])
                last.then_inc(s.filled, 1)
            all_taken("WN")
            for f in range(4):
                s = fill("W")
                by = PT if f < 2 else G
                wide(s, 128, NT, lambda k: MF[:, k, 128 * (f % 2):128 * (f % 2 + 1)], lambda k: by[:, k, :])
            all_taken("W")
            for t in range(NT):
                s = fill("N")
                narrow(s, 128, [(HT[:, f, tile(t)], w_1[:, f, :]) for f in range(4)])
            for t in range(NT):
                s = fill("T")
                pe.wait_ge(layer_ready, n.add(layer_ready))
                nc.tensor.transpose(s.ap[:, 0:P], HB[:, t, :], ID[0:P, 0:P]).then_inc(s.filled, 1)
            all_taken("T")
            for t in range(NT):
                s = fill("N")
                narrow(s, D, [(HBT[:, tile(t)], w_2)])
            weights_done()

            transpose_y()
            pe.wait_ge(small_in, 16 * SMALLS)
            logits([XT], WG[:, 0])
            weights(1, 3)
            ffn_unit(1, scaled=True)
            weights_done()

            weights(0, 3)
            weights(1, 3)
            for l in range(3):
                pe.wait_ge(layer_ready, n.add(layer_ready, NT))
                for f in range(K4):
                    s = fill("W")
                    wide(s, 128, NT, lambda k: XL[:, k, 128 * f:128 * (f + 1)], lambda k: CNT[:, k, :])
                all_taken("W")
                for t in range(NT):
                    s = fill("N")
                    narrow(s, D, [(EA1[:, tile(t)], WR[:, 1, 0, D * l:D * (l + 1)]),
                                  (EA2[0:65, tile(t)], WR[0:65, 1, 1, D * l:D * (l + 1)])]
                           + [(HT[:, f, tile(t)], wm(0, l)[:, f, :]) for f in range(K4)])
            weights_done()
            weights_done()

            transpose_y()
            logits([XT], WG[:, 1])
            weights(0, 3)
            for t in range(NT):
                project_narrow(wm(0, 0), t)
            for t in range(NT):
                s = fill("T")
                pe.wait_ge(y_ready, n.add(y_ready))
                for c in range(K4):
                    last = nc.tensor.transpose(s.ap[:, P * c:P * (c + 1)],
                                               Y[0:P, t, 128 * c:128 * (c + 1)], ID[0:P, 0:P])
                last.then_inc(s.filled, 1)
            all_taken("T")
            for t in range(NT):
                s = fill("N")
                narrow(s, D, [(TWOS[:, :], WR[0:8, 0, 2, 0:D])]
                       + [(HT[:, k, tile(t)], wm(0, 1)[:, k, :]) for k in range(K4)])
            weights_done()

            s = fill("W")
            pe.wait_ge(sin_ready, 1)
            wide(s, 16, 1, lambda k: FW[0:64, 0:16], lambda k: EMR)
            pe.wait_ge(s.taken, n.now(s.filled))
            s = fill("W")
            wide(s, 128, 1, lambda k: FW[0:16, 16:144], lambda k: ZC)
            pe.wait_ge(cond_split, 1)
            psum.align()

            def modulation(t):
                s = fill("W")
                for q in range(2):
                    last = mm(s.ap[0:P, D * q:D * (q + 1)], CONDR[:, tile(t)], MODR[:, q, :],
                              start=True, stop=True)
                last.then_inc(s.filled, 1)

            n.add(mod_split)
            normed_before.append(n.count[y_ready.name])
            with pe.Fori(0, BLOCKS) as i, n.loop(i, BLOCKS, loops, "block"):
                pe.wait_ge(mod_split, n.add(mod_split))
                for t in range(NT):
                    modulation(t)
                transpose_y()
                weights(1, 3)
                for h in range(HEADS3):
                    project_wide(wm(1, 0), h)
                    project_wide(wm(1, 1), h)
                all_taken("W")

                def scores(h, ts):
                    for t in ts:
                        s = fill("W")
                        wide(s, P, 1, lambda k: HT[:, h, tile(t)], lambda k: KT[:, h, :])

                scores(0, range(NT))
                for t in range(NT):
                    project_narrow(wm(1, 2), t)
                weights_done()
                all_taken("N")
                for h in range(HEADS3):
                    probs = G if h % 2 == 0 else PRB
                    if h + 1 < HEADS3:
                        scores(h + 1, range(NT))
                    ready = prob_ready if h < HEADS3 - 1 else last_prob_ready
                    pe.wait_ge(ready, n.add(ready, NT))
                    moved = []
                    for c in range(NT):
                        s = fill("W")
                        for t in range(NT):
                            last = nc.tensor.transpose(s.ap[0:P, 128 * t:128 * t + P],
                                                       probs[:, t, tile(c)], ID[0:P, 0:P])
                        last.then_inc(s.filled, 1)
                        moved.append((s, n.now(s.filled)))
                    s = fill("W")

                    def weights_of(k):
                        pe.wait_ge(moved[k][0].taken, moved[k][1])
                        return V[:, k, 128 * h:128 * (h + 1)]

                    wide(s, 128, NT, weights_of, lambda k: PT[:, k, :])
                all_taken("W")
                weights(0, 3)
                pe.wait_ge(mod_split, n.add(mod_split))
                for t in range(NT + 1):
                    if t < NT:
                        project_narrow(wm(0, 0), t)
                    if t:
                        modulation(t - 1)
                transpose_y()
                for m in range(K4):
                    project_wide(wm(0, 1), m)
                all_taken("W")
                for t in range(NT):
                    s = fill("N")
                    narrow(s, D, [(HT[:, k, tile(t)], wm(0, 2)[:, k, :]) for k in range(K4)])
                weights_done()
                psum.align()

            transpose_y()
            logits([XTH[:, :, :].bitcast(F32), XTL[:, :, :].bitcast(F32)], WG[:, 2])
            psum.align()

            def product(t, high, low, j):
                s = fill("N")
                narrow(s, D, [(x[:, k, tile(t)], w[:, j, k, :]) for k in range(K4)
                              for x, w in ((high, WHI), (low, WHI), (high, WLO))])
                return s, n.now(s.filled)

            def unit():
                pe.wait_ge(split_ready, n.add(split_ready))
                for t in range(NT):
                    product(t, XTH, XTL, 0)
                pe.wait_ge(split_ready, n.add(split_ready))
                hidden = [product(t, XTH, XTL, 1) for t in range(NT)]
                moved = []

                def transposed(t):
                    s = fill("T")
                    pe.wait_ge(hidden[t][0].taken, hidden[t][1])
                    for c in range(K4):
                        last = nc.tensor.transpose(s.ap[:, P * c:P * (c + 1)],
                                                   HID[:, t, 128 * c:128 * (c + 1)], ID[0:P, 0:P])
                    last.then_inc(s.filled, 1)
                    moved.append((s, n.now(s.filled)))

                for t in range(NT - 1):
                    transposed(t)
                pe.wait_ge(split_ready, n.add(split_ready))
                for t in range(NT):
                    pe.wait_ge(moved[t][0].taken, moved[t][1])
                    product(t, HTH, HTL, 2)
                    if t == 0:
                        transposed(NT - 1)

            with pe.Fori(0, UNITS // 2 - 1) as i, n.loop(i, UNITS // 2 - 1, loops, "expert"):
                for u in range(2):
                    unit()
            for u in range(2):
                unit()

        @block.scalar
        def _(act):
            n = Tally("act")
            psum = Slots(slots, n)
            fn = nc.scalar.activation

            def take(kind):
                s, k, _ = psum.next(kind)
                act.wait_ge(s.filled, k)
                return s

            def tile(t):
                return slice(P * t, P * (t + 1))

            act.dma_start(ISRC[:, :], a["src_p"].bitcast(U32)).then_inc(index_in, 16)
            act.dma_start(IDST[:, :], a["dst_p"].bitcast(U32)).then_inc(index_in, 16)
            act.dma_start(FS[:, 7, :], a["edge_weight"]).then_inc(index_in, 16)
            act.dma_start(MODW[:, :, :], bcast(a["arow"], 0, 4 * D, 128).rearrange(
                "p (a b) -> p a b", a=4)).then_inc(arow_in, 16)
            act.dma_start(BR[:, 0, :], bcast(a["arow"], 4 * D, D, 128)).then_inc(arow_in, 16)
            for j in range(3):
                act.dma_start(WG[:, j], a[f"gate_{j}"].rearrange("p (c n) -> p c n", c=K4))\
                   .then_inc(small_in, 16)
            act.dma_start(BI[:, :], bcast(a["biases"], 0, 8, P)).then_inc(small_in, 16)
            act.dma_start(PC[:, :], a["columns"]).then_inc(small_in, 16)
            act.dma_start(FW[:, 0:16], a["f_w1"]).then_inc(small_in, 16)
            act.dma_start(FW[0:16, 16:145], a["f_w2"]).then_inc(small_in, 16)
            act.dma_start(FB2[:, :], a["f_b2x4"]).then_inc(small_in, 16)

            def transpose_y():
                for t in range(NT):
                    s = take("T")
                    fn(XT[:, :, tile(t)], s.ap[:, 0:4 * P].rearrange("p (c n) -> p c n", c=K4), ACT.Copy)\
                        .then_inc(s.taken, 1)


            transpose_y()
            for t in range(NT):
                s = take("N")
                fn(HRN[:, t, 0:D], s.ap[0:P, :], ACT.Copy).then_inc(s.taken, 1)
            for t in range(NT):
                s = take("N")
                fn(HE[:, t, :], s.ap[0:P, :], ACT.Copy).then_inc(s.taken, 1)
            s = take("N")
            fn(HRN[:, :, D:ROWLEN], s.ap[0:P, 0:16 * NT].rearrange("p (t h) -> p t h", t=NT), ACT.Copy)\
                .then_inc(s.taken, 1)
            for s in slots["N"]:
                act.wait_ge(s.taken, n.now(s.filled))
            act.dma_start(hr_rows.rearrange("(t p) c -> p t c", p=P), HRN).then_inc(hr_stored, 16)
            psum.skip(N=1)
            s, k, _ = psum.next("N")
            act.wait_ge(s.taken, k)
            fn(FS[:, 8, :], FS[:, 7, :], ACT.Exp, bias=SM[:, 3:4]).then_inc(exp_ready, 1)
            n.add(exp_ready)

            s = take("T")
            fn(KEYT[:, :], s.ap[0:ET, 0:P], ACT.Copy).then_inc(s.taken, 1)
            psum.skip(N=ET // 4)


            def magnitudes_of_tile(m):
                act.wait_ge(diff_ready, n.add(diff_ready))
                fn(PRD[m % 2][:, 0, :], PRD[m % 2][:, 0, :], ACT.Abs).then_inc(abs_ready, 1)

            def take_pairs(k, dst):
                act.wait_ge(graph_filled, k)
                fn(TAILS, tails, ACT.Copy).then_inc(tails_taken, 1)
                fn(dst[:, :, 0:MAIN], PS[0:P, 0:5 * BANK].rearrange("p (c n) -> p c n", c=NT), ACT.Copy)
                act.wait_ge(tails_back, k)
                fn(dst[:, 0:4, MAIN:N], PS[0:P, 7 * BANK:7 * BANK + 4 * TAIL].rearrange(
                    "p (c n) -> p c n", c=4), ACT.Copy)
                fn(dst[:, 4, MAIN:N], tail_of(4), ACT.Copy).then_inc(graph_taken, 1)

            with act.Fori(0, TURNS) as i, n.loop(i, TURNS, loops, "count"):
                for m in range(GATHERS_A):
                    magnitudes_of_tile(m)
            take_pairs(1, CNT)
            with act.Fori(0, TURNS) as i, n.loop(i, TURNS, loops, "weight"):
                done = 0
                for k in range(STEP):
                    act.wait_ge(plain_ready, n.add(plain_ready))
                    for r in range(3):
                        last = fn(OD[k % HOTS][r], PLAIN[k % HOTS], ACT.Copy,
                                  scale=FS[:, 4 + r, bass.ds(i * STEP + k, 1)])
                    last.then_inc(parts_ready, 1)
                    while done * STEP < (k + 1) * GATHERS_B and done < GATHERS_B:
                        magnitudes_of_tile(done)
                        done += 1
            take_pairs(2, G)
            n.add(onehot_used, 2 * ET)
            n.add(edge_read, 4)
            with act.Fori(0, TURNS) as i, n.loop(i, TURNS, loops, "edge"):
                for q in range(4):
                    b = q % 2
                    act.wait_ge(edge_in[q], n.add(edge_in[q], 16))
                    act.wait_ge(onehot_used, n.now(onehot_used))
                    n.add(onehot_used, 4)
                    fn(S1[b][:, :, 0:64], ER[q], ACT.Copy).then_inc(high_ready, 1)
                    act.wait_ge(edge_read, n.add(edge_read))
                    fn(S1[b][:, :, 64:128], ERR[b], ACT.Copy).then_inc(middle_ready, 1)
                    act.wait_ge(last_ready, n.add(last_ready))
                    fn(S2[b][:, :, 0:64], ERR[b], ACT.Copy).then_inc(low_ready, 1)
            act.wait_ge(scattered, 16 * ET)
            act.dma_start(TSC[0], pair_scores[0:N * P, :].rearrange("(p q) h -> p (q h)", p=P))\
               .then_inc(pairs_in[0], 16)
            act.wait_ge(graph_filled, 3)
            fn(EA1[:, :], PS[:, 2 * BANK:2 * BANK + N], ACT.Copy)
            fn(EA2[0:65, :], PS[0:65, 4 * BANK:4 * BANK + N], ACT.Copy).then_inc(graph_taken, 1)

            done = [0]

            def quantized(u, late=False):
                def magnitudes(k):
                    j, c, width = groups[k]
                    if done[0] + k >= 2:
                        act.wait_ge(quant_ready, done[0] + k - 1)
                    w = wm((u + 1) % 2, j)[:, c, 0:width]
                    fn(AW[k % 2][:, 0:width], w, ACT.Abs).then_inc(absw_ready, 1)
                    fn(SGN[k % 2][:, 0:width], w, ACT.Sign).then_inc(scalar_step, 1)

                groups = groups_of(u)
                act.wait_ge(loaded[(u + 1) % 2], n.now(loaded[(u + 1) % 2]) + 48)
                magnitudes(0)
                for k, (j, c, width) in enumerate(groups):
                    if late:
                        yield
                    elif k + 1 < len(groups):
                        magnitudes(k + 1)
                    s = take("T")
                    fn(SCL[k % 2][:, 0:width], s.ap[:, 0:width], ACT.Copy, bias=1e-5, scale=1.0 / 128)\
                        .then_inc(s.taken, 1)
                    if late and k + 1 < len(groups):
                        magnitudes(k + 1)
                    if k == len(groups) - 1:
                        done[0] += len(groups)
                    if not late:
                        yield

            n.add(loaded[0], 32)

            def exp_scores(k):
                t, h = divmod(k, HEADS0)
                if h == 0:
                    act.wait_ge(negmax_ready, n.add(negmax_ready))
                pairs = TSC[t % 2].rearrange("p (d h) -> p d h", h=HEADS0)
                fn(SP0[k % 4], pairs[:, :, h], ACT.Exp, bias=HM[:, t % 2, 1, h:h + 1])\
                    .then_inc(exp_ready, 1)
                n.add(exp_ready)

            for k in range(3):
                exp_scores(k)
            ahead = quantized(0, late=True)
            for k in range(NT * HEADS0):
                if k + 3 < NT * HEADS0:
                    exp_scores(k + 3)
                s = take("W")
                fn(PTS[k % 2], s.ap[0:P, 0:640].rearrange("p (c n) -> p c n", c=NT)[:, :, 0:P], ACT.Copy)\
                    .then_inc(s.taken, 1)
                if k == 2 or (k % 3 == 0 and k):
                    next(ahead, None)
            for _ in ahead:
                pass
            psum.skip(N=NT)
            for s in slots["N"]:
                act.wait_ge(s.filled, n.now(s.filled))
            psum.align()

            def ffn_unit(chunks=K4, scaled=False, between=lambda: None):
                for m in range(chunks):
                    s = take("W")
                    fn(SG[m % 2], s.ap[:, 0:N], ACT.Silu).then_inc(s.taken, 1)
                    between()
                    psum.skip(W=1)
                    between()
                    between()
                    if m == 0 and scaled:
                        router_exp(TW[:, :, 0])
                if scaled:
                    for t in range(NT):
                        s = take("T")
                        fn(CT8[:, tile(t)], s.ap[0:8, 0:P], ACT.Copy).then_inc(s.taken, 1)
                    psum.skip(W=chunks)
                psum.skip(N=NT)

            transpose_y()
            for u in range(3):
                n.add(loaded[(u + 1) % 2], 48)
                ahead = quantized(u + 1) if u < 2 else iter(())
                ffn_unit(WIDTHS[u] // 128, between=lambda: next(ahead, None))

            transpose_y()
            psum.skip(N=NT)
            for c in range(NT):
                s = take("W")
                fn(PT[:, c, :].rearrange("p (c n) -> p c n", c=NT),
                   s.ap[0:P, 0:640].rearrange("p (c n) -> p c n", c=NT)[:, :, 0:P], ACT.Copy)\
                    .then_inc(s.taken, 1)
            for f in range(4):
                s = take("W")
                fn(HT[:, f, :], s.ap[:, 0:N], ACT.Copy).then_inc(s.taken, 1)
            psum.skip(N=NT)
            for t in range(NT):
                s = take("T")
                fn(HBT[:, tile(t)], s.ap[:, 0:P], ACT.Copy).then_inc(s.taken, 1)
            for t in range(NT):
                s, k, _ = psum.next("N")
                act.wait_ge(s.taken, k)
                fn(ROW[t % 2], ROW[t % 2], ACT.Relu, scale=TW[:, t, 2:3]).then_inc(relu_ready, 1)

            def router_exp(cols, scale=1.0):
                act.wait_ge(negmax_ready, n.add(negmax_ready))
                fn(cols, cols, ACT.Exp, scale=scale).then_inc(exp_ready, 1)

            transpose_y()
            psum.skip(N=1)
            ffn_unit(scaled=True)

            for l in range(3):
                for f in range(K4):
                    s = take("W")
                    fn(HT[:, f, :], s.ap[:, 0:N], ACT.Copy).then_inc(s.taken, 1)
                psum.skip(N=NT)

            transpose_y()
            psum.skip(N=1)
            router_exp(TW[:, :, 0])
            for t in range(NT):
                s, k, _ = psum.next("N")
                for i in range(2):
                    if i == 0:
                        act.wait_ge(negmax_ready, n.add(negmax_ready))
                    else:
                        act.wait_ge(s.taken, k)
                    fn(GE[t % 2][i], GE[t % 2][i], ACT.Gelu).then_inc(exp_ready, 1)
            for t in range(NT):
                s = take("T")
                fn(HT[:, :, tile(t)], s.ap[:, 0:4 * P].rearrange("p (c n) -> p c n", c=K4), ACT.Copy)\
                    .then_inc(s.taken, 1)
            psum.skip(N=NT)

            act.wait_ge(emb_ready, 1)
            fn(EMR, EMR, ACT.Sin).then_inc(sin_ready, 1)
            s = take("W")
            act.wait_ge(small_in, 16 * SMALLS)
            fn(ZC, s.ap[0:16, 0:N], ACT.Silu, bias=FW[0:16, 144:145]).then_inc(s.taken, 1)
            s = take("W")
            act.wait_ge(emb_ready, 2)
            fn(COND4[:, :], s.ap[:, 0:N], ACT.Identity, bias=FB2[:, 0:1]).then_inc(s.taken, 1)
            act.wait_ge(s.taken, n.now(s.filled))
            fn(CONDR[:, :], COND4[:, :], ACT.Copy).then_inc(cond_rounded, 1)
            psum.align()

            def round_weights(j, rows_in_):
                act.wait_ge(rows_in_, n.add(rows_in_, 64))
                fn(MODR[:, :, :], MODW[:, j:j + 2, :], ACT.Copy).then_inc(mod_rounded, 1)

            with act.Fori(0, BLOCKS) as i, n.loop(i, BLOCKS, loops, "block"):
                round_weights(0, modw_in)
                psum.skip(W=NT)
                transpose_y()
                round_weights(2, mod2_in)
                for h in range(HEADS3):
                    psum.skip(W=1)
                    s = take("W")
                    fn(KT[:, h, :], s.ap[:, 0:N], ACT.Identity,
                       bias=PC[:, bass.ds(i * 12 + 4 + h, 1)]).then_inc(s.taken, 1)
                psum.skip(N=NT)

                def exp_head(h):
                    probs = G if h % 2 == 0 else PRB
                    for t in range(NT):
                        psum.skip(W=1)
                        act.wait_ge(negmax_ready, n.add(negmax_ready))
                        fn(probs[:, t, :], probs[:, t, :], ACT.Exp, bias=DEN[:, h % 2, 1, t:t + 1])\
                            .then_inc(exp_ready, 1)

                exp_head(0)
                for h in range(HEADS3):
                    probs = G if h % 2 == 0 else PRB
                    if h < HEADS3 - 1:
                        act.wait_ge(sums_ready, n.add(sums_ready))
                        for t in range(NT):
                            fn(probs[:, t, :], probs[:, t, :], ACT.Copy, scale=DEN[:, h % 2, 3, t:t + 1])\
                                .then_inc(prob_ready, 1)
                    if h + 1 < HEADS3:
                        exp_head(h + 1)
                    for c in range(NT):
                        s = take("W")
                        fn(PT[:, c, :].rearrange("p (c n) -> p c n", c=NT),
                           s.ap[0:P, 0:640].rearrange("p (c n) -> p c n", c=NT)[:, :, 0:P], ACT.Copy)\
                            .then_inc(s.taken, 1)
                    s = take("W")
                    fn(XT[:, h, :], s.ap[:, 0:N], ACT.Copy).then_inc(s.taken, 1)
                psum.skip(N=NT, W=NT)
                transpose_y()
                for m in range(K4):
                    s = take("W")
                    fn(HT[:, m, :], s.ap[:, 0:N], ACT.Relu,
                       bias=PC[:, bass.ds(i * 12 + 8 + m, 1)]).then_inc(s.taken, 1)
                psum.skip(N=NT)
                psum.align()

            def rounded_transpose(dst):
                for t in range(NT):
                    s = take("T")
                    fn(dst[:, :, tile(t)], s.ap[:, 0:4 * P].rearrange("p (c n) -> p c n", c=K4), ACT.Copy)\
                        .then_inc(hi_ready, 1)

            def round_matrix(s, j):
                if j == 0:
                    act.wait_ge(loaded[s], n.add(loaded[s], 48))
                fn(WHI[:, j].rearrange("p c n -> p (c n)"), WR[:, s, j, :], ACT.Copy).then_inc(rounded, 1)

            for s in range(2):
                n.count[loaded[s].name] = landed[s]
            rounded_transpose(XTH)
            psum.skip(N=1)
            round_matrix(1, 0)
            round_matrix(1, 1)
            router_exp(TW[:, :, 0:2], scale=-1.0)
            psum.align()

            def unit(s, ahead=True):
                for slot in slots["N"]:
                    act.wait_ge(slot.filled, n.now(slot.filled))
                round_matrix(s, 2)
                for t in range(NT):
                    slot = take("N")
                    fn(HID[:, t, :], slot.ap[0:P, :], ACT.Silu).then_inc(slot.taken, 1)
                if ahead:
                    round_matrix(1 - s, 0)
                psum.skip(N=NT)
                rounded_transpose(HTH)
                if ahead:
                    round_matrix(1 - s, 1)
                psum.skip(N=NT)

            with act.Fori(0, UNITS // 2 - 1) as i, n.loop(i, UNITS // 2 - 1, loops, "expert"):
                for u in range(2):
                    unit(1 - u)
            unit(1)
            unit(0, ahead=False)

        @block.gpsimd
        def _(pool):
            n = Tally("pool")
            g = nc.gpsimd
            g.memset(ONES[:, :], 1.0).then_inc(start_done, 1)
            g.memset(TWOS[:, :], 2.0).then_inc(start_done, 1)
            g.memset(HALF[:, :], -0.5).then_inc(start_done, 1)
            g.memset(COMB[:, :, :], 1.0).then_inc(start_done, 1)
            g.memset(EA2[:, :], 0.0).then_inc(start_done, 1)
            g.iota(IOTA[:, :], pattern=[[1, N]], base=0, channel_multiplier=0).then_inc(start_done, 1)
            g.memset(ZB, 0.0).then_inc(pool_step, 1)
            g.memset(TS[:, :, :], 0.0).then_inc(score_taken, 1)
            n.add(score_taken)
            pool.wait_ge(pool_step, n.add(pool_step))
            g.memset(ZROW, NEG).then_inc(clear_row_ready, 1)

            def inverse_roots(tiles=range(NT)):
                for t in tiles:
                    pool.wait_ge(var_ready, n.add(var_ready))
                    g.tensor_tensor(RSTD[:, t:t + 1], VE[:, t:t + 1], HALF[:, :], ALU.pow)\
                        .then_inc(rstd_ready, 1)

            inverse_roots()
            pool.wait_ge(index_in, 48)
            pool.wait_ge(hr_stored, 16)

            def gather(m, b):
                g.tensor_copy(IDS[:, 2 * b:2 * b + 1], ISRC[:, bass.ds(m, 1)]).then_inc(pool_step, 1)
                g.tensor_copy(IDS[:, 2 * b + 1:2 * b + 2], IDST[:, bass.ds(m, 1)]).then_inc(pool_step, 1)
                pool.wait_ge(pool_step, n.add(pool_step, 2))
                g.tensor_tensor(SM[0:1, 10:11], HALF[0:1, :], HALF[0:1, :], ALU.add)
                for k, dst in enumerate((HS[b], HD[b])):
                    g.indirect_dma_start(
                        out=dst, out_offset=None, in_=hr_rows,
                        in_offset=bass.IndirectOffsetOnAxis(ap=IDS[:, 2 * b + k:2 * b + k + 1], axis=0))\
                     .then_inc(gathered[b], 16)

            def scatter(m, b, first=False):
                pool.wait_ge(score_ready, n.add(score_ready))
                if not first:
                    pool.wait_ge(scattered, n.now(scattered))
                n.add(scattered, 16)
                g.tensor_copy(IDS[:, 2 * AHEAD + b:2 * AHEAD + b + 1], SIDX[:, bass.ds(m, 1)]).then_inc(score_taken, 1)
                pool.wait_ge(score_taken, n.add(score_taken))
                g.tensor_tensor(SM[0:1, 10:11], HALF[0:1, :], HALF[0:1, :], ALU.add)
                g.indirect_dma_start(
                    out=pair_scores, out_offset=bass.IndirectOffsetOnAxis(ap=IDS[:, 2 * AHEAD + b:2 * AHEAD + b + 1], axis=0),
                    in_=TS[:, b, :], in_offset=None).then_inc(scattered, 16)

            for b in range(AHEAD):
                gather(b, b)
            pool.wait_ge(cleared, 16 * 2 * NT)
            pool.wait_ge(sidx_ready, 1)
            for b in range(AHEAD):
                scatter(b, b, first=(b == 0))
                gather(AHEAD + b, b)
            with pool.Fori(1, ET // AHEAD - 1) as i, n.loop(i - 1, ET // AHEAD - 2, loops, "gather"):
                for b in range(AHEAD):
                    scatter(i * AHEAD + b, b)
                    gather(i * AHEAD + b + AHEAD, b)
            for b in range(AHEAD):
                scatter(ET - AHEAD + b, b)
            def signed(u):
                for k, (j, c, width) in enumerate(groups_of(u)):
                    w = wm((u + 1) % 2, j)[:, c, 0:width]
                    pool.wait_ge(kept_ready, n.add(kept_ready))
                    g.tensor_tensor(w, SCL[k % 2][:, 0:width], SGN[k % 2][:, 0:width], ALU.mult)\
                     .then_inc(quant_ready, 1)
                    yield

            ahead = signed(0)
            for k in range(NT * HEADS0):
                t, h = divmod(k, HEADS0)
                if h == 2 and t:
                    inverse_roots([t - 1])
                if k % 3 == 2 and k >= 5:
                    next(ahead, None)
            for _ in ahead:
                pass
            inverse_roots([NT - 1])
            for u in (1, 2):
                for _ in signed(u):
                    pass
            inverse_roots()
            inverse_roots()
            inverse_roots()
            inverse_roots()
            for l in range(3):
                inverse_roots()
            inverse_roots()
            inverse_roots()
            inverse_roots()
            n.add(y_ready, normed_before[0])

            def add_bias(rows_in_, r):
                pool.wait_ge(y_ready, n.add(y_ready, NT))
                pool.wait_ge(rows_in_, n.add(rows_in_, 16))
                for t in range(NT):
                    g.tensor_tensor(XL[:, t, :], XL[:, t, :], BR[0:P, r, :], ALU.add)\
                     .then_inc(bias_added, 1)

            with pool.Fori(0, BLOCKS) as i, n.loop(i, BLOCKS, loops, "block"):
                add_bias(br_in, 1)
                inverse_roots()
                add_bias(br2_in, 2)
                inverse_roots()
            inverse_roots()

        @block.vector
        def _(dve):
            n = Tally("dve")
            psum = Slots(slots, n)
            v = nc.vector

            def take(kind):
                s, k, _ = psum.next(kind)
                dve.wait_ge(s.filled, k)
                return s

            def step(ins):
                ins.then_inc(vector_step, 1)
                dve.wait_ge(vector_step, n.add(vector_step))

            def signal(ins, sem):
                ins.then_inc(sem, 1)
                dve.wait_ge(sem, n.add(sem))

            def carry():
                if n.turn is not None:
                    v.tensor_copy(SM[0:1, 5:6], ONES[0:1, 0:1])

            def tile(t):
                return slice(P * t, P * (t + 1))

            def stats(t, src):
                step(v.bn_stats(ST[:, t, :], src))
                carry()
                step(v.bn_aggr(MV[:, t, :], ST[:, t, :]))
                v.tensor_scalar(VE[:, t:t + 1], MV[:, t, 1:2], 1e-5, None, ALU.add).then_inc(var_ready, 1)

            def norm(t, dst, src):
                dve.wait_ge(rstd_ready, n.add(rstd_ready))
                return v.tensor_scalar(dst, src, MV[:, t, 0:1], RSTD[:, t:t + 1], ALU.subtract, ALU.mult)

            def norm_y(t):
                norm(t, Y[0:P, t, :], X[0:P, t, :]).then_inc(y_ready, 1)
                n.add(y_ready)

            def followed(first, second):
                for t in range(NT + 1):
                    if t < NT:
                        first(t)
                    if t:
                        second(t - 1)

            def add_to_stream(t, s, scalar=None, dst=X):
                if scalar is None:
                    v.tensor_tensor(dst[0:P, t, :], s.ap[0:P, :], dst[0:P, t, :], ALU.add)\
                     .then_inc(s.taken, 1)
                else:
                    v.scalar_tensor_tensor(dst[0:P, t, :], s.ap[0:P, :], scalar, dst[0:P, t, :],
                                           ALU.mult, ALU.add).then_inc(s.taken, 1)
                dve.wait_ge(s.taken, n.now(s.filled))

            v.memset(S2[0][:, :, 64:65], 1.0)
            v.memset(S2[1][:, :, 64:65], 1.0).then_inc(edge_read, 4)
            dve.wait_ge(edge_read, n.add(edge_read, 4))


            dve.wait_ge(x_in, 16)
            followed(lambda t: stats(t, X[0:P, t, :]), norm_y)
            psum.skip(T=NT, N=NT)
            dve.wait_ge(arow_in, 32)
            dve.wait_ge(loaded[0], 32)
            for k, (w, r) in enumerate(((0, MODW[:, 0, :]), (1, BR[:, 0, :]), (0, MODW[:, 1, :]))):
                step(v.tensor_tensor(WTMP, wm(0, w), r.unsqueeze(1).broadcast_to([128, K4, D]),
                                     ALU.mult))
                step(v.tensor_reduce(UVT[:, k, :], WTMP.rearrange("p c (h d) -> p (c h) d", d=DH0),
                                     AX.X, ALU.add))
            part = [UVT[:, k, :].rearrange("p (c h) -> p c h", c=K4) for k in range(3)]
            step(v.tensor_tensor(UV[:, :, 0:8], part[0], part[1], ALU.subtract))
            v.tensor_tensor(UV[:, :, 8:16], part[2], part[1], ALU.add).then_inc(uv_ready, 1)
            dve.wait_ge(uv_ready, 1)
            psum.skip(N=NT + 1)
            dve.wait_ge(index_in, 48)
            step(v.tensor_copy(FS[:, 0, :], ISRC[:, :]))
            step(v.tensor_copy(FS[:, 1, :], IDST[:, :]))
            v.scalar_tensor_tensor(FS[:, 2, :], FS[:, 0, :], float(N), FS[:, 1, :], ALU.mult, ALU.add)\
             .then_inc(keys_ready, 1)
            dve.wait_ge(keys_ready, 1)
            v.reduce_max(SM[:, 0:1], FS[:, 7, :], AX.X).then_inc(layer_ready, 1)
            s = take("N")
            v.reduce_max(SM[0:1, 2:3], s.ap[0:1, 0:P], AX.X).then_inc(s.taken, 1)
            dve.wait_ge(s.taken, n.now(s.filled))
            v.tensor_scalar(SM[0:1, 1:2], SM[0:1, 2:3], 0.0, None, ALU.max).then_inc(layer_ready, 1)
            s = take("N")
            v.tensor_scalar(SM[:, 3:4], s.ap[0:P, 0:1], -1.0, None, ALU.mult).then_inc(s.taken, 1)
            dve.wait_ge(exp_ready, n.add(exp_ready))
            for r in range(3):
                step(v.tensor_copy(EB[:, :], FS[:, 8, :]))
                step(v.tensor_copy(FS[:, 4 + r, :], EB[:, :]))
                if r < 2:
                    step(v.tensor_tensor(FS[:, 8, :], FS[:, 8, :], FS[:, 4 + r, :], ALU.subtract))

            dve.wait_ge(consts_in, 16)
            psum.skip(T=1)
            for q in range(4):
                for m in range(20):
                    if m % 4 == 0:
                        s = take("N")
                    last = v.scalar_tensor_tensor(
                        KROW[:, m, :], s.ap[0:P, P * (m % 4):P * (m % 4 + 1)],
                        FS[:, 2, 20 * q + m:20 * q + m + 1], CS[0:P, C_TRI:C_TRI + P],
                        ALU.is_equal, ALU.mult)
                    if m % 4 == 3:
                        last.then_inc(s.taken, 1)
                dve.wait_ge(s.taken, n.now(s.filled))
                step(v.tensor_reduce(FS[:, 3, 20 * q:20 * (q + 1)], KROW, AX.X, ALU.max))
            step(v.tensor_scalar(FS[:, 8, :], FS[:, 2, :], -1.0, CS[0:P, C_DUMP:C_DUMP + 1],
                                 ALU.mult, ALU.add))
            step(v.tensor_tensor(FS[:, 8, :], FS[:, 8, :], FS[:, 3, :], ALU.mult))
            step(v.tensor_tensor(FS[:, 8, :], FS[:, 8, :], FS[:, 2, :], ALU.add))
            v.tensor_copy(SIDX[:, :], FS[:, 8, :]).then_inc(sidx_ready, 1)


            def onehot(dst, m, row):
                return v.tensor_scalar(dst, IOTA[:, :], FS[:, row, bass.ds(m, 1)], None, ALU.is_equal)

            def differences(m):
                b, z = m % AHEAD, PRD[m % 2]
                dve.wait_ge(gathered[b], n.add(gathered[b], 32))
                v.tensor_tensor(z[:, 1, :], HD[b][:, 0:D], HS[b][:, 0:D], ALU.mult)
                v.tensor_tensor(z[:, 0, :], HD[b][:, 0:D], HS[b][:, 0:D], ALU.subtract)\
                 .then_inc(diff_ready, 1)

            def edge_scores(m):
                b, z = m % AHEAD, PRD[m % 2]
                dve.wait_ge(abs_ready, n.add(abs_ready))
                step(v.tensor_tensor(z, z, MODW[0:P, 2:4, :], ALU.mult))
                step(v.tensor_reduce(SUMS[:, :, :], z.rearrange("p s (h d) -> p (s h) d", d=DH0).rearrange(
                    "p (s h) d -> p s h d", s=2), AX.X, ALU.add))
                x, y = SUMS[:, 0, :], SUMS[:, 1, :]
                step(v.tensor_tensor(x, x, HS[b][:, D:D + HEADS0], ALU.add))
                step(v.tensor_tensor(y, y, HD[b][:, D + HEADS0:ROWLEN], ALU.add))
                step(v.tensor_tensor(x, x, y, ALU.add))
                dve.wait_ge(score_taken, n.add(score_taken))
                v.scalar_tensor_tensor(TS[:, b, :], x, 0.2, x, ALU.mult, ALU.max)\
                 .then_inc(score_ready, 1)

            dve.wait_ge(start_done, 6)
            for name, scores in (("count", GATHERS_A), ("weight", GATHERS_B)):
                with dve.Fori(0, TURNS) as i, n.loop(i, TURNS, loops, name):
                    done = 0
                    for k in range(STEP):
                        dve.wait_ge(onehot_used, n.add(onehot_used))
                        onehot(OS[k % HOTS], i * STEP + k, 0)
                        if name == "weight":
                            onehot(PLAIN[k % HOTS], i * STEP + k, 1).then_inc(plain_ready, 1)
                        else:
                            onehot(OD[k % HOTS][0], i * STEP + k, 1).then_inc(onehot_ready, 1)
                        while done * STEP < (k + 1) * scores and done < scores:
                            differences(done)
                            if done:
                                edge_scores(done - 1)
                            done += 1
                    edge_scores(done - 1)
                if name == "count":
                    dve.wait_ge(graph_taken, 1)
                    step(v.tensor_scalar(MASK[:, :, :], CNT[:, :, :], 0.5, NEG, ALU.is_lt, ALU.mult))
            with dve.Fori(0, TURNS) as i, n.loop(i, TURNS, loops, "edge"):
                for q in range(4):
                    b = q % 2
                    for k in range(4):
                        if k == 0:
                            dve.wait_ge(high_ready, n.add(high_ready))
                            v.tensor_tensor(ERR[b], ER[q], S1[b][:, :, 0:64], ALU.subtract)\
                             .then_inc(edge_read, 1)
                            n.add(edge_read)
                        if k == 2:
                            dve.wait_ge(middle_ready, n.add(middle_ready))
                            v.tensor_tensor(ERR[b], ERR[b], S1[b][:, :, 64:128], ALU.subtract)\
                             .then_inc(last_ready, 1)
                        dve.wait_ge(onehot_used, n.add(onehot_used))
                        onehot(OD[k % HOTS][0], i * STEP + 4 * q + k, 1).then_inc(onehot_ready, 1)

            def quantized(u):
                for k, (j, c, width) in enumerate(groups_of(u)):
                    s = psum.next("T")
                    dve.wait_ge(s[0].taken, s[1])
                    w, z = AW[k % 2][:, 0:width], SCL[k % 2][:, 0:width]
                    step(v.scalar_tensor_tensor(w, w, 2.0, z, ALU.mult, ALU.is_gt))
                    v.tensor_tensor(z, z, w, ALU.mult).then_inc(kept_ready, 1)
                    yield

            def maxima_of(t, half):
                if half == 0:
                    dve.wait_ge(pairs_in[t % 2], 16 * (t // 2 + 1))
                hs = slice(4 * half, 4 * half + 4)
                step(v.tensor_reduce(HM[:, t % 2, 0, hs],
                                     TSC[t % 2].rearrange("p (d h) -> p h d", h=HEADS0)[:, hs, :],
                                     AX.X, ALU.max))
                if half == 0:
                    return
                v.tensor_scalar(HM[:, t % 2, 1, :], HM[:, t % 2, 0, :], -1.0, None, ALU.mult)\
                 .then_inc(negmax_ready, 1)

            def add_heads(t):
                den = HM[:, t % 2, 3, :]
                dve.wait_ge(weights_summed, HEADS0 * (t + 1))
                step(v.tensor_scalar(den, HM[:, t % 2, 2, :], 1e-16, None, ALU.add))
                step(v.reciprocal(den, den))
                s, y = take("N"), Y[0:P, t, :]
                v.tensor_tensor(y.rearrange("p (h d) -> p h d", d=DH0),
                                s.ap[0:P, :].rearrange("p (h d) -> p h d", d=DH0),
                                den.unsqueeze(2).broadcast_to([P, HEADS0, DH0]), ALU.mult)\
                 .then_inc(s.taken, 1)
                dve.wait_ge(s.taken, n.now(s.filled))
                step(v.tensor_tensor(X[0:P, t, :], X[0:P, t, :], y, ALU.add))
                stats(t, X[0:P, t, :])
                if t:
                    norm_y(t - 1)

            maxima_of(0, 0)
            maxima_of(0, 1)
            psum.skip(W=NT * HEADS0)
            ahead = quantized(0)
            for k in range(NT * HEADS0):
                t, h = divmod(k, HEADS0)
                z = SP0[k % 4]
                dve.wait_ge(exp_ready, n.add(exp_ready))
                v.tensor_tensor_reduce(out=z, in0=z, in1=CNT[:, t, :], scale=1.0, scalar=0.0,
                                       op0=ALU.mult, op1=ALU.add, accum_out=HM[:, t % 2, 2, h:h + 1])\
                 .then_inc(weights_summed, 1)
                if h in (3, 4) and t + 1 < NT:
                    maxima_of(t + 1, h - 3)
                if h == 2 and t:
                    add_heads(t - 1)
                if k % 3 == 2 and k >= 5:
                    next(ahead, None)
            for _ in ahead:
                pass
            add_heads(NT - 1)
            norm_y(NT - 1)
            psum.align()

            def ffn_unit(chunks=K4, scaled=None, scalar=None, after=None, between=lambda: None):
                for m in range(chunks):
                    s, k, _ = psum.next("W")
                    between()
                    b = take("W")
                    dve.wait_ge(s.taken, k)
                    v.tensor_tensor(HT[:, m, :], SG[m % 2], b.ap[:, 0:N], ALU.mult).then_inc(b.taken, 1)
                    if m == 0 and scaled:
                        scaled()
                    between()
                    between()
                if scaled:
                    dve.wait_ge(b.taken, n.now(b.filled))
                    psum.skip(T=NT)
                    for m in range(chunks):
                        c = take("W")
                        v.tensor_tensor(HT[:, m, :], HT[:, m, :], c.ap[:, 0:N], ALU.mult).then_inc(c.taken, 1)

                def added(t):
                    add_to_stream(t, take("N"), None if scalar is None else scalar(t))
                    if after is not None:
                        stats(t, X[0:P, t, :])

                followed(added, after or (lambda t: None))

            psum.skip(T=NT)
            for u in range(3):
                ahead = quantized(u + 1) if u < 2 else iter(())
                ffn_unit(WIDTHS[u] // 128, after=(norm_y if u == 2 else None), between=lambda: next(ahead, None))

            psum.skip(T=NT)
            step(v.tensor_reduce(TW[:, :, 0], G[:, :, :], AX.X, ALU.add))
            step(v.tensor_scalar(TW[:, :, 1], TW[:, :, 0], 1e-6, None, ALU.add))
            step(v.reciprocal(TW[:, :, 1], TW[:, :, 1]))
            step(v.tensor_scalar(TW[:, :, 2], TW[:, :, 0], 0.0, None, ALU.is_gt))
            for t in range(NT):
                last = v.tensor_scalar(G[:, t, :], G[:, t, :], TW[:, t, 1:2], None, ALU.mult)
            last.then_inc(layer_ready, 1)
            n.add(layer_ready)
            dve.wait_ge(rows_in, 16)
            for t in range(NT):
                s = take("N")
                v.tensor_tensor(MF[:, t, :], s.ap[0:P, 0:256], ROWS[:, R_BM:R_BM + 256], ALU.add)\
                 .then_inc(s.taken, 1)
            psum.skip(W=NT + 4)

            def hidden(t):
                s = take("N")
                v.tensor_tensor(HB[:, t, :], s.ap[0:P, 0:128], ROWS[:, R_B1:R_B1 + 128], ALU.add)\
                 .then_inc(s.taken, 1)
                dve.wait_ge(s.taken, n.now(s.filled))
                stats(t, HB[:, t, :])

            def hidden_normed(t):
                step(norm(t, HB[:, t, :], HB[:, t, :]))
                step(v.tensor_tensor(HB[:, t, :], HB[:, t, :], ROWS[:, R_G1:R_G1 + 128], ALU.mult))
                step(v.tensor_tensor(HB[:, t, :], HB[:, t, :], ROWS[:, R_BE1:R_BE1 + 128], ALU.add))
                v.tensor_scalar(HB[:, t, :], HB[:, t, :], 0.0, None, ALU.max).then_inc(layer_ready, 1)

            followed(hidden, hidden_normed)
            psum.skip(T=NT)

            def added(t):
                s, z = take("N"), ROW[t % 2]
                v.tensor_tensor(z, s.ap[0:P, :], ROWS[:, R_B2:R_B2 + D], ALU.add).then_inc(s.taken, 1)
                dve.wait_ge(relu_ready, n.add(relu_ready))
                step(v.tensor_tensor(X[0:P, t, :], X[0:P, t, :], z, ALU.add))
                stats(t, X[0:P, t, :])

            followed(added, norm_y)

            def best_two(values, t):
                step(v.max(M8[:, t, :], values))
                step(v.max_index(I8[:, t, :], M8[:, t, :], values))

            def shares(first):
                step(v.tensor_copy(TW[:, :, 3:5], I8[:, :, 0:2]))
                numbers = CS[0:P, C_I8:C_I8 + 8].unsqueeze(1).broadcast_to([P, NT, 8])
                for r, z in enumerate((M8, LG)):
                    step(v.tensor_tensor(z[:, :, :], numbers, TW[:, :, 3 + r:4 + r].broadcast_to([P, NT, 8]),
                                         ALU.is_equal))
                    share = TW[:, :, first + r:first + r + 1].broadcast_to([P, NT, 8])
                    step(v.tensor_tensor(z[:, :, :], z[:, :, :], share, ALU.mult))
                return v.tensor_tensor(COMB[:, :, 0:8], M8[:, :, :], LG[:, :, :], ALU.add)

            def logits():
                s = take("N")
                v.tensor_copy(LG[:, :, :], s.ap[0:P, 0:8 * NT].rearrange("p (t e) -> p t e", t=NT))\
                 .then_inc(s.taken, 1)
                dve.wait_ge(s.taken, n.now(s.filled))

            def softmax_of_two():
                v.tensor_tensor(TW[:, :, 0], M8[:, :, 1], M8[:, :, 0], ALU.subtract).then_inc(negmax_ready, 1)
                dve.wait_ge(exp_ready, n.add(exp_ready))
                step(v.tensor_scalar(TW[:, :, 1], TW[:, :, 0], 1.0, None, ALU.add))
                step(v.reciprocal(TW[:, :, 1], TW[:, :, 1]))
                step(v.tensor_tensor(TW[:, :, 2], TW[:, :, 0], TW[:, :, 1], ALU.mult))

            psum.skip(T=NT)
            logits()

            def routed():
                for t in range(NT):
                    best_two(LG[:, t, :], t)
                softmax_of_two()
                shares(1).then_inc(layer_ready, 1)
                n.add(layer_ready)

            def normed(t):
                norm(t, XL[:, t, :], X[0:P, t, :]).then_inc(layer_ready, 1)
                n.add(layer_ready)

            ffn_unit(scaled=routed, after=normed)

            def summed(t):
                add_to_stream(t, take("N"), dst=XL)
                stats(t, XL[:, t, :])

            def relu_normed(t, l):
                z = XL[:, t, :]
                step(norm(t, z, z))
                step(v.tensor_tensor(z, z, ROWS[:, R_G2 + D * l:R_G2 + D * (l + 1)], ALU.mult))
                step(v.tensor_tensor(z, z, ROWS[:, R_BE2 + D * l:R_BE2 + D * (l + 1)], ALU.add))
                if l < 2:
                    v.tensor_scalar(z, z, 0.0, None, ALU.max).then_inc(layer_ready, 1)
                    n.add(layer_ready)
                else:
                    step(v.tensor_scalar(z, z, 0.0, None, ALU.max))
                    add = v.tensor_tensor(X[0:P, t, :], X[0:P, t, :], z, ALU.add)
                    if t == 0:
                        signal(add, attn_rows_free)
                    elif t == 1:
                        signal(add, mlp_rows_free)
                    else:
                        step(add)

            v.memset(MODW[:, :, :], 0.0).then_inc(mod_split, 1)
            dve.wait_ge(mod_split, 1)
            for l in range(3):
                psum.skip(W=K4)
                followed(summed, lambda t: relu_normed(t, l))
            followed(lambda t: stats(t, X[0:P, t, :]), norm_y)

            psum.skip(T=NT)
            logits()
            for t in range(NT):
                step(v.max(M8[:, t, :], LG[:, t, :]))
            softmax_of_two()

            def hidden_inputs(t):
                s = take("N")
                for i in range(2):
                    last = v.scalar_tensor_tensor(GE[t % 2][i], s.ap[0:P, :], TW[:, t, 1 + i:2 + i],
                                                  ROWS[:, R_FB1:R_FB1 + D], ALU.mult, ALU.add)
                    if i == 0:
                        last.then_inc(negmax_ready, 1)
                last.then_inc(s.taken, 1)

            for t in range(NT + 1):
                if t < NT:
                    if t >= 2:
                        dve.wait_ge(y_ready, n.now(y_ready))
                    hidden_inputs(t)
                if t:
                    dve.wait_ge(exp_ready, n.add(exp_ready, 2))
                    n.add(y_ready)
                    v.tensor_tensor(Y[0:P, t - 1, :], GE[(t - 1) % 2][0], GE[(t - 1) % 2][1], ALU.add)\
                     .then_inc(y_ready, 1)
            dve.wait_ge(noise_in, 16)
            col = lambda c: CS[0:64, c:c + 1]
            step(v.tensor_scalar(EMN, EMN, col(C_FREQ), None, ALU.mult))
            step(v.tensor_scalar(EMB, EMN, 1.0 / (2.0 * np.pi), col(C_FRAC), ALU.mult, ALU.add))
            step(v.tensor_scalar(EMB, EMB, MAGIC, -MAGIC, ALU.add, ALU.add))
            for c in TWO_PI:
                step(v.scalar_tensor_tensor(EMN, EMB, -c, EMN, ALU.mult, ALU.add))
            step(v.tensor_scalar(EMN, EMN, col(C_SHIFT), 3.1415925, ALU.add, ALU.min))
            v.tensor_scalar(EMR, EMN, -3.1415925, None, ALU.max).then_inc(emb_ready, 2)
            psum.skip(T=NT)

            def joined(t):
                add_to_stream(t, take("N"))
                stats(t, X[0:P, t, :])

            def stream_normed(t):
                step(norm(t, XL[:, t, :], X[0:P, t, :]))

            followed(joined, stream_normed)
            for t in range(NT):
                stats(t, XL[:, t, :])

            psum.skip(W=2)
            psum.align()
            dve.wait_ge(cond_rounded, 1)
            for r in (32, 96):
                last = v.tensor_tensor(CONDR[r:r + 32, :], COND4[r:r + 32, :],
                                       CONDR[r:r + 32, :].bitcast(F32), ALU.subtract)
            last.then_inc(cond_split, 1)

            def split_weights(j):
                dve.wait_ge(mod_rounded, n.add(mod_rounded))
                v.tensor_tensor(MODR[64:128, :, :], MODW[64:128, j:j + 2, :],
                                MODR[64:128, :, :].bitcast(F32), ALU.subtract).then_inc(mod_split, 1)

            def modulated_norm(t):
                y = Y[0:P, t, :]
                step(norm(t, y, XL[:, t, :]))
                s = take("W")
                step(v.scalar_tensor_tensor(y, s.ap[0:P, 0:D], 1.0, y, ALU.add, ALU.mult))
                v.tensor_tensor(y, y, s.ap[0:P, D:2 * D], ALU.add).then_inc(s.taken, 1)
                dve.wait_ge(s.taken, n.now(s.filled))
                v.tensor_copy(SM[:, 4:5], SM[:, 3:4]).then_inc(y_ready, 1)
                n.add(y_ready)

            with dve.Fori(0, BLOCKS) as i, n.loop(i, BLOCKS, loops, "block"):
                split_weights(0)
                for t in range(NT):
                    modulated_norm(t)
                psum.skip(T=NT)
                split_weights(2)
                for h in range(HEADS3):
                    s = take("W")
                    v.tensor_scalar(HT[:, h, :], s.ap[:, 0:N], PC[:, bass.ds(i * 12 + h, 1)],
                                    128.0 ** -0.5, ALU.add, ALU.mult).then_inc(s.taken, 1)
                    psum.skip(W=1)
                dve.wait_ge(br_in, n.add(br_in, 16))

                def maxima(h):
                    probs = G if h % 2 == 0 else PRB
                    for t in range(NT):
                        s = take("W")
                        carry()
                        v.tensor_tensor_reduce(out=probs[:, t, :], in0=s.ap[0:P, 0:N], in1=MASK[:, t, :],
                                               scale=1.0, scalar=-3.0e38, op0=ALU.add, op1=ALU.max,
                                               accum_out=DEN[:, h % 2, 0, t:t + 1]).then_inc(s.taken, 1)
                        dve.wait_ge(s.taken, n.now(s.filled))
                        v.tensor_scalar(DEN[:, h % 2, 1, t:t + 1], DEN[:, h % 2, 0, t:t + 1], -1.0, None,
                                        ALU.mult).then_inc(negmax_ready, 1)

                maxima(0)
                for h in range(HEADS3):
                    probs = G if h % 2 == 0 else PRB
                    for t in range(NT):
                        if h == 0:
                            s = take("N")
                            v.tensor_tensor(V[:, t, :], s.ap[0:P, :], BR[0:P, 0, :], ALU.add)\
                             .then_inc(s.taken, 1)
                        dve.wait_ge(exp_ready, n.add(exp_ready))
                        step(v.tensor_tensor_reduce(
                            out=probs[:, t, :], in0=probs[:, t, :], in1=CNT[:, t, :], scale=1.0,
                            scalar=0.0, op0=ALU.mult, op1=ALU.add, accum_out=DEN[:, h % 2, 2, t:t + 1]))
                    step(v.tensor_scalar(DEN[:, h % 2, 3, :], DEN[:, h % 2, 2, :], 1e-30, None, ALU.max))
                    if h < HEADS3 - 1:
                        v.reciprocal(DEN[:, h % 2, 3, :], DEN[:, h % 2, 3, :]).then_inc(sums_ready, 1)
                    else:
                        step(v.reciprocal(DEN[:, h % 2, 3, :], DEN[:, h % 2, 3, :]))
                        for t in range(NT):
                            v.tensor_scalar(probs[:, t, :], probs[:, t, :], DEN[:, h % 2, 3, t:t + 1],
                                            None, ALU.mult).then_inc(last_prob_ready, 1)
                    if h + 1 < HEADS3:
                        maxima(h + 1)
                    psum.skip(W=NT + 1)
                def attention_added(t):
                    dve.wait_ge(bias_added, n.add(bias_added))
                    add_to_stream(t, take("N"), dst=XL)
                    if t == NT - 1:
                        signal(v.tensor_copy(SM[:, 4:5], SM[:, 3:4]), attn_rows_free)
                    stats(t, XL[:, t, :])

                followed(attention_added, modulated_norm)
                psum.skip(T=NT)
                psum.skip(W=K4)
                for t in range(NT):
                    dve.wait_ge(bias_added, n.add(bias_added))
                    add_to_stream(t, take("N"), dst=XL)
                    if t == NT - 1:
                        signal(v.tensor_copy(SM[:, 4:5], SM[:, 3:4]), mlp_rows_free)
                    stats(t, XL[:, t, :])
                psum.align()
            dve.wait_ge(rstd_ready, n.add(rstd_ready, NT))

            def joined(t):
                step(v.tensor_tensor(X[0:P, t, :], X[0:P, t, :], XL[:, t, :], ALU.add))
                stats(t, X[0:P, t, :])

            followed(joined, norm_y)

            def rest_of_transpose(dst, high):
                for t in range(NT):
                    s = take("T")
                    dve.wait_ge(hi_ready, n.add(hi_ready))
                    v.tensor_tensor(dst[:, :, tile(t)], s.ap[:, 0:4 * P].rearrange("p (c n) -> p c n", c=K4),
                                    high[:, :, tile(t)].bitcast(F32), ALU.subtract).then_inc(s.taken, 1)

            def split_matrix(s, j):
                dve.wait_ge(rounded, n.add(rounded))
                v.tensor_tensor(WLO[:, j].rearrange("p c n -> p (c n)"), WR[:, s, j, :],
                                WHI[:, j].rearrange("p c n -> p (c n)").bitcast(F32), ALU.subtract)\
                 .then_inc(split_ready, 1)

            rest_of_transpose(XTL, XTH)
            split_matrix(1, 0)
            split_matrix(1, 1)
            logits()
            dve.wait_ge(small_in, 16 * SMALLS)
            for t in range(NT):
                step(v.max(M8[:, t, :], LG[:, t, :]))
            step(v.tensor_copy(TW[:, :, 0:2], M8[:, :, 0:2]))
            v.tensor_copy(SM[:, 4:5], SM[:, 3:4]).then_inc(negmax_ready, 1)
            step(v.tensor_tensor(LG[:, :, :], LG[:, :, :], BI[:, :].unsqueeze(1).broadcast_to([P, NT, 8]),
                                 ALU.add))
            for t in range(NT):
                best_two(LG[:, t, :], t)
            dve.wait_ge(exp_ready, n.add(exp_ready))
            step(v.tensor_scalar(TW[:, :, 0:2], TW[:, :, 0:2], 1.0, None, ALU.add))
            step(v.reciprocal(TW[:, :, 0:2], TW[:, :, 0:2]))
            step(v.tensor_tensor(TW[:, :, 2], TW[:, :, 0], TW[:, :, 1], ALU.add))
            step(v.reciprocal(TW[:, :, 2], TW[:, :, 2]))
            step(v.tensor_tensor(TW[:, :, 0:2], TW[:, :, 0:2], TW[:, :, 2:3].broadcast_to([P, NT, 2]),
                                 ALU.mult))
            step(shares(0))
            psum.align()

            def unit(s, share, ahead=True):
                split_matrix(s, 2)
                gates = [psum.next("N") for t in range(NT)]
                for t in range(NT):
                    slot = take("N")
                    dve.wait_ge(gates[t][0].taken, gates[t][1])
                    v.tensor_tensor(HID[:, t, :], HID[:, t, :], slot.ap[0:P, :], ALU.mult)\
                     .then_inc(slot.taken, 1)
                    if t == 0 and ahead:
                        split_matrix(1 - s, 0)
                rest_of_transpose(HTL, HTH)
                for t in range(NT):
                    add_to_stream(t, take("N"), COMB[:, t, share])
                    if t == 1 and ahead:
                        split_matrix(1 - s, 1)

            with dve.Fori(0, UNITS // 2 - 1) as i, n.loop(i, UNITS // 2 - 1, loops, "expert"):
                for u in range(2):
                    unit(1 - u, bass.ds(i, 1))
            unit(1, slice(8, 9))
            unit(0, slice(8, 9), ahead=False)
            store_x(dve)
    return nc



def mat(w):
    return np.ascontiguousarray(w.reshape(K4, 128, -1).transpose(1, 0, 2)).reshape(128, -1)


def padded(w, rows, cols):
    out = np.zeros((rows, cols), w.dtype)
    out[:w.shape[0], :w.shape[1]] = w
    return out


def constants():
    c = np.zeros((128, C_END), np.float32)
    c[:, C_ID:C_ID + 128] = np.eye(128)
    c[:P, C_TRI:C_TRI + P] = np.tril(np.ones((P, P)), -1)
    c[:, C_I8:C_I8 + 8] = np.arange(8)
    freqs = np.arange(1, FREQS + 1, dtype=np.float32) * np.float32(2.0 * np.pi / 16)
    c[:2 * FREQS, C_FREQ] = np.concatenate([freqs, freqs])
    c[FREQS:2 * FREQS, C_SHIFT] = np.pi / 2
    c[FREQS:2 * FREQS, C_FRAC] = 0.25
    c[:, C_DUMP] = N * N + np.arange(128)
    for e in range(8):
        c[e, C_SEL + 64 * e:C_SEL + 64 * (e + 1)] = 1.0
    return c


def laid_out(i):
    i = {k: np.asarray(x) for k, x in i.items()}
    heads = lambda w: w.transpose(1, 0, 2).reshape(D, -1)
    col = lambda b: b.reshape(K4, 128).T
    a5 = i["L0_gnn_a"].reshape(HEADS0, 5, DH0)
    a = {
        "x": i["x"], "consts": constants(),
        "src_p": i["src"].reshape(P, ET), "dst_p": i["dst"].reshape(P, ET),
        "edge_weight": i["edge_weight"].reshape(P, ET),
        "edge_attr": i["edge_attr_64"].reshape(P, ET * 64),
        "noise": i["node_vec1"].reshape(-1),
        "W_e": mat(heads(i["L0_gnn_W_e"])), "W_r": mat(heads(i["L0_gnn_W_r"])),
        "arow": a5[:, [0, 1, 3, 4, 2]].transpose(1, 0, 2).reshape(-1),
        "Wm": mat(i["L1_gnn_Wm"]), "W1": mat(i["L1_gnn_W1"]), "W2": i["L1_gnn_W2"],
        "e_W1": mat(heads(i["L1_ffn_W1"])), "e_W3": mat(heads(i["L1_ffn_W3"])),
        "e_W2": mat(i["L1_ffn_W2"].reshape(D, D)),
        "Wtop": np.stack([mat(w[:D]) for w in i["L2_gnn_Ws"]]),
        "Wbot": i["L2_gnn_Ws"][:, D:].transpose(1, 0, 2).reshape(64, -1),
        "f_W1": mat(heads(i["L2_ffn_W1"])), "f_W2": mat(i["L2_ffn_W2"].reshape(D, D)),
        "f_b2": i["L2_ffn_b2"],
        "gate_0": mat(i["L1_ffn_gate_w"]), "gate_1": mat(i["L2_ffn_Wg"]),
        "gate_2": mat(i["L3_ffn_gate_w"].T), "biases": i["L3_ffn_biases"],
        "f_w1": i["L3_gnn_f_w1"],
    }
    a["Wlast"] = np.concatenate([a["Wbot"], i["L2_gnn_bs"].reshape(1, -1)])
    a["rows"] = np.concatenate([i[f"L1_gnn_{k}"] for k in ("bm", "b1", "gamma", "beta", "b2")]
                               + [i["L2_gnn_gammas"].reshape(-1), i["L2_gnn_betas"].reshape(-1),
                                  i["L2_ffn_b1"].reshape(-1)])
    four = lambda w: np.concatenate([padded(w, len(w), 32)] * 4, 1)
    a["f_w2"] = np.concatenate([four(i["L3_gnn_f_w2"]), i["L3_gnn_f_b1"][:, None]], 1)
    a["f_b2x4"] = four(np.append(i["L3_gnn_f_b2"], np.float32(1.0))[None]).T
    halves = lambda w: [w[:, D * u:D * (u + 1)] for u in range(3)]
    for name, w in (("gate", i["L0_ffn_w_gate"].T), ("up", i["L0_ffn_w_up"].T)):
        a[name] = np.stack([mat(padded(h, D, D)) for h in halves(w)])
    a["down"] = np.stack([mat(padded(h.T, D, D)) for h in halves(i["L0_ffn_w_down"])])
    g = lambda k: i[f"L3_gnn_{k}"]
    a["modw"] = np.stack([np.stack([np.concatenate([g(f"{k}_w")[b], g(f"{k}_b")[b][None]])
                                    for k in ("s1", "b1", "s2", "b2")], 1) for b in range(BLOCKS)])
    a["brow"] = np.stack([g(k) for k in ("bv", "bo", "m_b2")], 1).reshape(-1)
    a["columns"] = np.concatenate([col(g(k)[b]) for b in range(BLOCKS) for k in ("bq", "bk", "m_b1")], 1)
    a["qkv"] = np.stack([mat(g(k)[b]) for b in range(BLOCKS) for k in ("wq", "wk", "wv")])
    a["omm"] = np.stack([mat(g(k)[b]) for b in range(BLOCKS) for k in ("wo", "m_w1", "m_w2")])
    f = lambda k: i[f"L3_ffn_{k}"]
    for name, routed, shared in (("x_a", "w1", "sw1"), ("x_b", "w3", "sw3")):
        a[name] = np.stack([mat(w[:, D * u:D * (u + 1)]) for w in (*f(routed), f(shared)) for u in range(2)])
    a["x_c"] = np.stack([mat(w[D * u:D * (u + 1)]) for w in (*f("w2"), f("sw2")) for u in range(2)])
    return {k: np.ascontiguousarray(x) for k, x in a.items()}


def build(nc, arrays):
    aps = {k: nc.dram_tensor(f"in_{k}", x.shape, mybir.dt.from_np(x.dtype), kind="ExternalInput").ap()
           for k, x in arrays.items()}
    out = nc.dram_tensor("out_0", (N, D), F32, kind="ExternalOutput").ap()
    program(nc, aps, out, LOOPS)


def kernel(**inputs):
    import concourse.bacc as _bacc
    from concourse.bass_utils import run_bass_kernel_spmd as _run

    arrays = laid_out(inputs)
    nc = _bacc.Bacc("TRN2", target_bir_lowering=False, num_devices=1, dynamic_dma_scratch_size=8192)
    build(nc, arrays)
    r = _run(nc, [{f"in_{k}": x for k, x in arrays.items()}], core_ids=[0])
    return r.results[0]["out_0"]
```
